# Optimizing a Trainium2 kernel written in Bass

```python
import numpy as np
import jax
import jax.numpy as jnp

def _softmax(x, axis=-1):
    return jax.nn.softmax(x, axis=axis)

def _gelu(x):
    return jax.nn.gelu(x, approximate=True)

def _silu(x):
    return jax.nn.silu(x)

def _sigmoid(x):
    return jax.nn.sigmoid(x)

def _layernorm(x, axis=-1, eps=1e-05):
    m = jnp.mean(x, axis=axis, keepdims=True)
    v = jnp.var(x, axis=axis, keepdims=True)
    return (x - m) / jnp.sqrt(v + eps)

def _scatter_add(tgt, idx, src, axis=0):
    return tgt.at[idx].add(src)

def _segment_sum(src, seg, n):
    return jax.ops.segment_sum(src, seg, n)
kernel_name = 'mk_hybrid_d2_jaxref_r8_81f2cd'

def setup_inputs(seed: int=0):
    np.random.seed(seed)
    _w = jnp.asarray

    def _L0_attn_a_setup():
        import math
        import jax, jax.numpy as jnp
        import numpy as np
        N_HEAD = 16

        def _reference_tuple_inner(x, W_dq, W_uq, W_dkv, W_uk, W_uv, W_o):
            B, T, C = x.shape
            nh = N_HEAD
            hs = C // nh
            kvl = W_dkv.shape[0]
            k_eff = (W_dq.T @ W_uq.T @ W_uk).reshape(nh, hs, kvl)
            v_eff = (W_uv.T @ W_o.T).reshape(kvl, nh, hs).transpose(1, 0, 2)
            c_kv = x @ W_dkv.T
            q = (x @ W_dq.T @ W_uq.T).reshape(B, T, nh, hs).transpose(0, 2, 1, 3)
            q_lat = jnp.einsum('bhtd,hdl->bhtl', q, k_eff)
            attn = jnp.einsum('bhtl,bsl->bhts', q_lat, c_kv) / math.sqrt(hs)
            causal_mask = jnp.triu(jnp.ones((T, T), bool), k=1)
            attn = jnp.where(causal_mask[None, None], -jnp.inf, attn)
            attn = jax.nn.softmax(attn, axis=-1)
            ctx = jnp.einsum('bhts,bsl->bhtl', attn, c_kv)
            y = jnp.einsum('bhtl,hld->bhtd', ctx, v_eff).transpose(0, 2, 1, 3).reshape(B, T, C)
            return (y, c_kv)
        key = jax.random.key(seed)
        ks = jax.random.split(key, 7)
        B, T, C = (4, 256, 128)
        QL, KVL = (32, 32)
        s = 0.02
        return {'x': jax.random.normal(ks[0], (B, T, C), jnp.float32), 'W_dq': jax.random.normal(ks[1], (QL, C), jnp.float32) * s, 'W_uq': jax.random.normal(ks[2], (C, QL), jnp.float32) * s, 'W_dkv': jax.random.normal(ks[3], (KVL, C), jnp.float32) * s, 'W_uk': jax.random.normal(ks[4], (C, KVL), jnp.float32) * s, 'W_uv': jax.random.normal(ks[5], (C, KVL), jnp.float32) * s, 'W_o': jax.random.normal(ks[6], (C, C), jnp.float32) * s}
    _L0_attn_a_in = _L0_attn_a_setup()

    def _L0_attn_b_setup():
        import jax, jax.numpy as jnp
        import numpy as np
        EPS = 1e-08

        def elu_feature_map(x):
            return jax.nn.elu(x) + 1.0
        key = jax.random.key(seed)
        ks = jax.random.split(key, 5)
        B, S, D = (2, 512, 128)
        scale = 1.0 / np.sqrt(D).astype(np.float32)
        x = jax.random.normal(ks[0], (B, S, D), dtype=jnp.float32)
        Wq = jax.random.normal(ks[1], (D, D), dtype=jnp.float32) * scale
        Wk = jax.random.normal(ks[2], (D, D), dtype=jnp.float32) * scale
        Wv = jax.random.normal(ks[3], (D, D), dtype=jnp.float32) * scale
        Wo = jax.random.normal(ks[4], (D, D), dtype=jnp.float32) * scale
        return {'x': x, 'Wq': Wq, 'Wk': Wk, 'Wv': Wv, 'Wo': Wo}
    _L0_attn_b_in = _L0_attn_b_setup()

    def _L0_ffn_setup():
        import jax, jax.numpy as jnp
        import numpy as np
        D = 128
        H = 128
        E = 8
        K = 2
        I = 2 * 128
        ROUTE_SCALE = 1.0
        key = jax.random.key(seed)
        ks = jax.random.split(key, 12)
        s = lambda *sh: 1.0 / np.sqrt(sh[-1])
        return {'x': jax.random.normal(ks[0], (1, 256, D), jnp.float32), 'gate_w': jax.random.normal(ks[1], (E, D), jnp.float32) * s(E, D), 'w1': jax.random.normal(ks[2], (E, H, D), jnp.float32) * s(H, D), 'b1': jax.random.normal(ks[3], (E, H), jnp.float32) * 0.01, 'w2': jax.random.normal(ks[4], (E, D, H), jnp.float32) * s(D, H), 'b2': jax.random.normal(ks[5], (E, D), jnp.float32) * 0.01, 'w3': jax.random.normal(ks[6], (E, H, D), jnp.float32) * s(H, D), 'b3': jax.random.normal(ks[7], (E, H), jnp.float32) * 0.01, 'sw1': jax.random.normal(ks[8], (I, D), jnp.float32) * s(I, D), 'sw2': jax.random.normal(ks[9], (I, D), jnp.float32) * s(I, D), 'sw3': jax.random.normal(ks[10], (D, I), jnp.float32) * s(D, I)}
    _L0_ffn_in = _L0_ffn_setup()

    def _L1_attn_a_setup():
        import jax, jax.numpy as jnp
        import numpy as np
        DIM = 128
        NUM_HEADS = 16
        HEAD_DIM = 64
        EPS = 1e-06

        def _feature_map(x, proj):
            return jax.nn.elu(x @ proj) + 1.0
        key = jax.random.key(seed)
        ks = jax.random.split(key, 6)
        x = jax.random.normal(ks[0], (4, 256, DIM), dtype=jnp.float32)
        Wq = jax.random.normal(ks[1], (DIM, NUM_HEADS * HEAD_DIM), dtype=jnp.float32) / np.sqrt(DIM)
        Wk = jax.random.normal(ks[2], (DIM, NUM_HEADS * HEAD_DIM), dtype=jnp.float32) / np.sqrt(DIM)
        Wv = jax.random.normal(ks[3], (DIM, NUM_HEADS * HEAD_DIM), dtype=jnp.float32) / np.sqrt(DIM)
        Wo = jax.random.normal(ks[4], (NUM_HEADS * HEAD_DIM, DIM), dtype=jnp.float32) / np.sqrt(NUM_HEADS * HEAD_DIM)
        proj = jax.random.normal(ks[5], (HEAD_DIM, HEAD_DIM), dtype=jnp.float32) / np.sqrt(HEAD_DIM)
        return {'x': x, 'Wq': Wq, 'Wk': Wk, 'Wv': Wv, 'Wo': Wo, 'proj': proj}
    _L1_attn_a_in = _L1_attn_a_setup()

    def _L1_attn_b_setup():
        import jax, jax.numpy as jnp
        import numpy as np
        CHUNK = 32
        FLOOR = 0.01
        EPS_MIX = 1e-05
        EPS_NORM = 1e-05

        def l2norm(x):
            return x / jnp.sqrt(jnp.sum(x * x, -1, keepdims=True) + 1e-12)

        def dw_causal_conv(x, w):
            K = w.shape[-1]
            L = x.shape[1]
            xp = jnp.pad(x, ((0, 0), (K - 1, 0), (0, 0)))
            y = jnp.zeros_like(x)
            for t in range(K):
                y = y + xp[:, t:t + L, :] * w[:, t]
            return y

        def delta_rule_chunkwise(q, k, v, beta):
            b, h, L, dk = q.shape
            dv = v.shape[-1]
            c = CHUNK
            n = L // c
            q = l2norm(q)
            k = l2norm(k)
            v = v * beta[..., None]
            kb = k * beta[..., None]
            rs = lambda x: x.reshape(b, h, n, c, -1)
            qc, kc, vc, kbc = (rs(q), rs(k), rs(v), rs(kb))
            T = -jnp.einsum('bhnid,bhnjd->bhnij', kbc, kc)
            tri_strict = jnp.tril(jnp.ones((c, c), bool), -1)
            T = jnp.where(tri_strict, T, 0.0)
            for i in range(1, c):
                T = T.at[..., i, :i].add(jnp.einsum('bhnj,bhnji->bhni', T[..., i, :], T[..., :, :i]))
            T = T + jnp.eye(c, dtype=T.dtype)
            u = jnp.einsum('bhnij,bhnjd->bhnid', T, vc)
            w = jnp.einsum('bhnij,bhnjd->bhnid', T, kbc)
            mask_incl = jnp.tril(jnp.ones((c, c), bool), 0)

            def step(S, inp):
                qi, ki, ui, wi = inp
                attn = jnp.einsum('bhid,bhjd->bhij', qi, ki)
                attn = jnp.where(mask_incl, attn, 0.0)
                u_i = ui - jnp.einsum('bhik,bhkd->bhid', wi, S)
                o_i = jnp.einsum('bhik,bhkd->bhid', qi, S) + jnp.einsum('bhij,bhjd->bhid', attn, u_i)
                S = S + jnp.einsum('bhci,bhcd->bhid', ki, u_i)
                return (S, o_i)
            S0 = jnp.zeros((b, h, dk, dv), q.dtype)
            xs = tuple((jnp.moveaxis(a, 2, 0) for a in (qc, kc, u, w)))
            S, o = jax.lax.scan(step, S0, xs)
            o = jnp.moveaxis(o, 0, 2).reshape(b, h, L, dv)
            return (o, S)
        key = jax.random.key(seed)
        B, L, D, H = (4, 512, 128, 4)
        dh = D // H
        ks = jax.random.split(key, 20)
        s = 1.0 / np.sqrt(D)
        inp = {'hidden_states': jax.random.normal(ks[0], (B, L, D), jnp.float32), 'Wq': jax.random.normal(ks[1], (D, D), jnp.float32) * s, 'Wk': jax.random.normal(ks[2], (D, D), jnp.float32) * s, 'Wv': jax.random.normal(ks[3], (D, D), jnp.float32) * s, 'Wb': jax.random.normal(ks[4], (D, H), jnp.float32) * s, 'conv_q_w': jax.random.normal(ks[5], (D, 4), jnp.float32) * 0.5, 'conv_k_w': jax.random.normal(ks[6], (D, 4), jnp.float32) * 0.5, 'conv_v_w': jax.random.normal(ks[7], (D, 4), jnp.float32) * 0.5, 'local_w': (jax.random.normal(ks[8], (H * dh, 7), jnp.float32) / np.sqrt(7.0)).at[:, -1].add(1.0), 'mid_w': (jax.random.normal(ks[9], (H * dh, 25), jnp.float32) / np.sqrt(25.0)).at[:, -1].add(1.0), 'r_w1': jax.random.normal(ks[10], (D + 14 * H, 2 * (D + 14 * H)), jnp.float32) / np.sqrt(D + 14 * H), 'r_b1': jnp.zeros((2 * (D + 14 * H),), jnp.float32), 'r_w2': jax.random.normal(ks[11], (2 * (D + 14 * H), H * 4), jnp.float32) / np.sqrt(2.0 * (D + 14 * H)), 'r_b2': jnp.zeros((H, 4), jnp.float32).at[:, 2:].set(0.7).reshape(-1), 'mix_w': jnp.ones((H, dh), jnp.float32), 'onorm_w': jnp.ones((dh,), jnp.float32), 'Wo': jax.random.normal(ks[12], (D, D), jnp.float32) * s}
        return inp
    _L1_attn_b_in = _L1_attn_b_setup()

    def _L1_ffn_setup():
        import jax, jax.numpy as jnp
        import numpy as np
        N, T, D = (4, 512, 128)
        NUM_EXPERTS = 8
        EXPERT_CAP = 2.0
        MLP_RATIO = 4
        HIDDEN = MLP_RATIO * D
        key = jax.random.key(seed)
        k1, k2, k3, k4 = jax.random.split(key, 4)
        x = jax.random.normal(k1, (N, T, D), dtype=jnp.float32)
        gate_w = jax.random.truncated_normal(k2, -2.0, 2.0, (D, NUM_EXPERTS), dtype=jnp.float32) * 0.02
        w1 = jax.random.normal(k3, (NUM_EXPERTS, D, HIDDEN), dtype=jnp.float32) * 0.02
        w2 = jax.random.normal(k4, (NUM_EXPERTS, HIDDEN, D), dtype=jnp.float32) * 0.02
        return {'x': x, 'gate_w': gate_w, 'w1': w1, 'w2': w2}
    _L1_ffn_in = _L1_ffn_setup()
    _d = {'L0_attn_a_x': _L0_attn_a_in['x'], 'L0_attn_a_W_dq': _L0_attn_a_in['W_dq'], 'L0_attn_a_W_uq': _L0_attn_a_in['W_uq'], 'L0_attn_a_W_dkv': _L0_attn_a_in['W_dkv'], 'L0_attn_a_W_uk': _L0_attn_a_in['W_uk'], 'L0_attn_a_W_uv': _L0_attn_a_in['W_uv'], 'L0_attn_a_W_o': _L0_attn_a_in['W_o'], 'L0_attn_b_Wq': _L0_attn_b_in['Wq'], 'L0_attn_b_Wk': _L0_attn_b_in['Wk'], 'L0_attn_b_Wv': _L0_attn_b_in['Wv'], 'L0_attn_b_Wo': _L0_attn_b_in['Wo'], 'L0_ffn_gate_w': _L0_ffn_in['gate_w'], 'L0_ffn_w1': _L0_ffn_in['w1'], 'L0_ffn_b1': _L0_ffn_in['b1'], 'L0_ffn_w2': _L0_ffn_in['w2'], 'L0_ffn_b2': _L0_ffn_in['b2'], 'L0_ffn_w3': _L0_ffn_in['w3'], 'L0_ffn_b3': _L0_ffn_in['b3'], 'L0_ffn_sw1': _L0_ffn_in['sw1'], 'L0_ffn_sw2': _L0_ffn_in['sw2'], 'L0_ffn_sw3': _L0_ffn_in['sw3'], 'L1_attn_a_Wq': _L1_attn_a_in['Wq'], 'L1_attn_a_Wk': _L1_attn_a_in['Wk'], 'L1_attn_a_Wv': _L1_attn_a_in['Wv'], 'L1_attn_a_Wo': _L1_attn_a_in['Wo'], 'L1_attn_a_proj': _L1_attn_a_in['proj'], 'L1_attn_b_Wq': _L1_attn_b_in['Wq'], 'L1_attn_b_Wk': _L1_attn_b_in['Wk'], 'L1_attn_b_Wv': _L1_attn_b_in['Wv'], 'L1_attn_b_Wb': _L1_attn_b_in['Wb'], 'L1_attn_b_conv_q_w': _L1_attn_b_in['conv_q_w'], 'L1_attn_b_conv_k_w': _L1_attn_b_in['conv_k_w'], 'L1_attn_b_conv_v_w': _L1_attn_b_in['conv_v_w'], 'L1_attn_b_local_w': _L1_attn_b_in['local_w'], 'L1_attn_b_mid_w': _L1_attn_b_in['mid_w'], 'L1_attn_b_r_w1': _L1_attn_b_in['r_w1'], 'L1_attn_b_r_b1': _L1_attn_b_in['r_b1'], 'L1_attn_b_r_w2': _L1_attn_b_in['r_w2'], 'L1_attn_b_r_b2': _L1_attn_b_in['r_b2'], 'L1_attn_b_mix_w': _L1_attn_b_in['mix_w'], 'L1_attn_b_onorm_w': _L1_attn_b_in['onorm_w'], 'L1_attn_b_Wo': _L1_attn_b_in['Wo'], 'L1_ffn_gate_w': _L1_ffn_in['gate_w'], 'L1_ffn_w1': _L1_ffn_in['w1'], 'L1_ffn_w2': _L1_ffn_in['w2']}
    _x0 = _d['L0_attn_a_x']
    _d['L0_attn_a_x'] = jax.random.normal(jax.random.fold_in(jax.random.key(seed), 1), (32, 256, 128), dtype=_x0.dtype)
    del _x0
    return _d

def reference(L0_attn_a_x, L0_attn_a_W_dq, L0_attn_a_W_uq, L0_attn_a_W_dkv, L0_attn_a_W_uk, L0_attn_a_W_uv, L0_attn_a_W_o, L0_attn_b_Wq, L0_attn_b_Wk, L0_attn_b_Wv, L0_attn_b_Wo, L0_ffn_gate_w, L0_ffn_w1, L0_ffn_b1, L0_ffn_w2, L0_ffn_b2, L0_ffn_w3, L0_ffn_b3, L0_ffn_sw1, L0_ffn_sw2, L0_ffn_sw3, L1_attn_a_Wq, L1_attn_a_Wk, L1_attn_a_Wv, L1_attn_a_Wo, L1_attn_a_proj, L1_attn_b_Wq, L1_attn_b_Wk, L1_attn_b_Wv, L1_attn_b_Wb, L1_attn_b_conv_q_w, L1_attn_b_conv_k_w, L1_attn_b_conv_v_w, L1_attn_b_local_w, L1_attn_b_mid_w, L1_attn_b_r_w1, L1_attn_b_r_b1, L1_attn_b_r_w2, L1_attn_b_r_b2, L1_attn_b_mix_w, L1_attn_b_onorm_w, L1_attn_b_Wo, L1_ffn_gate_w, L1_ffn_w1, L1_ffn_w2):

    def _L0_attn_a_ref(x, W_dq, W_uq, W_dkv, W_uk, W_uv, W_o):
        import math
        import jax, jax.numpy as jnp
        import numpy as np
        N_HEAD = 16

        def _reference_tuple_inner(x, W_dq, W_uq, W_dkv, W_uk, W_uv, W_o):
            B, T, C = x.shape
            nh = N_HEAD
            hs = C // nh
            kvl = W_dkv.shape[0]
            k_eff = (W_dq.T @ W_uq.T @ W_uk).reshape(nh, hs, kvl)
            v_eff = (W_uv.T @ W_o.T).reshape(kvl, nh, hs).transpose(1, 0, 2)
            c_kv = x @ W_dkv.T
            q = (x @ W_dq.T @ W_uq.T).reshape(B, T, nh, hs).transpose(0, 2, 1, 3)
            q_lat = jnp.einsum('bhtd,hdl->bhtl', q, k_eff)
            attn = jnp.einsum('bhtl,bsl->bhts', q_lat, c_kv) / math.sqrt(hs)
            causal_mask = jnp.triu(jnp.ones((T, T), bool), k=1)
            attn = jnp.where(causal_mask[None, None], -jnp.inf, attn)
            attn = jax.nn.softmax(attn, axis=-1)
            ctx = jnp.einsum('bhts,bsl->bhtl', attn, c_kv)
            y = jnp.einsum('bhtl,hld->bhtd', ctx, v_eff).transpose(0, 2, 1, 3).reshape(B, T, C)
            return (y, c_kv)
        return _reference_tuple_inner(x, W_dq, W_uq, W_dkv, W_uk, W_uv, W_o)[0]

    def _L0_attn_b_ref(x, Wq, Wk, Wv, Wo):
        import jax, jax.numpy as jnp
        import numpy as np
        EPS = 1e-08

        def elu_feature_map(x):
            return jax.nn.elu(x) + 1.0
        B, S, D = x.shape
        H = 16
        Dh = D // H

        def proj(W):
            return (x @ W.T).reshape(B, S, H, Dh)
        q = elu_feature_map(proj(Wq))
        k = elu_feature_map(proj(Wk))
        v = proj(Wv)
        q_t = jnp.moveaxis(q, 1, 0)
        k_t = jnp.moveaxis(k, 1, 0)
        v_t = jnp.moveaxis(v, 1, 0)

        def step(carry, qkv):
            kv_sum, k_sum = carry
            q_i, k_i, v_i = qkv
            kv_sum = kv_sum + jnp.einsum('bhd,bhe->bhde', k_i, v_i)
            k_sum = k_sum + k_i
            num = jnp.einsum('bhd,bhde->bhe', q_i, kv_sum)
            den = jnp.sum(q_i * k_sum, axis=-1, keepdims=True)
            out_i = num / (den + EPS)
            return ((kv_sum, k_sum), out_i)
        kv0 = jnp.zeros((B, H, Dh, Dh), dtype=x.dtype)
        ks0 = jnp.zeros((B, H, Dh), dtype=x.dtype)
        _, out = jax.lax.scan(step, (kv0, ks0), (q_t, k_t, v_t))
        out = jnp.moveaxis(out, 0, 1).reshape(B, S, D)
        return out @ Wo.T

    def _L0_ffn_ref(x, gate_w, w1, b1, w2, b2, w3, b3, sw1, sw2, sw3):
        import jax, jax.numpy as jnp
        import numpy as np
        D = 128
        H = 128
        E = 8
        K = 2
        I = 2 * 128
        ROUTE_SCALE = 1.0
        B, S, _ = x.shape
        xt = x.reshape(-1, D)
        logits = xt @ gate_w.T
        scores = jax.nn.softmax(logits.astype(jnp.float32), axis=-1)
        top_vals, idx = jax.lax.top_k(scores, K)
        weights = jnp.take_along_axis(scores, idx, axis=1).astype(x.dtype) * ROUTE_SCALE
        xs = xt[:, None, :] * weights[:, :, None]
        y = jnp.zeros_like(xt)
        for e in range(E):
            mask = (idx == e).astype(x.dtype)
            h = jax.nn.silu(jnp.einsum('tkd,hd->tkh', xs, w1[e]) + b1[e])
            x2 = jnp.einsum('tkh,dh->tkd', h, w2[e]) + b2[e]
            x3 = jnp.einsum('tkd,hd->tkh', xs, w3[e]) + b3[e]
            y = y + jnp.sum(x2 * x3 * mask[:, :, None], axis=1)
        z = jax.nn.silu(xt @ sw1.T) * (xt @ sw2.T) @ sw3.T
        return (y + z).reshape(B, S, D)

    def _L1_attn_a_ref(x, Wq, Wk, Wv, Wo, proj):
        import jax, jax.numpy as jnp
        import numpy as np
        DIM = 128
        NUM_HEADS = 16
        HEAD_DIM = 64
        EPS = 1e-06

        def _feature_map(x, proj):
            return jax.nn.elu(x @ proj) + 1.0
        B, S, _ = x.shape
        H, D = (NUM_HEADS, HEAD_DIM)
        q = (x @ Wq).reshape(B, S, H, D)
        k = (x @ Wk).reshape(B, S, H, D)
        v = (x @ Wv).reshape(B, S, H, D)
        q = _feature_map(q, proj)
        k = _feature_map(k, proj)
        q_t = jnp.moveaxis(q, 1, 0)
        k_t = jnp.moveaxis(k, 1, 0)
        v_t = jnp.moveaxis(v, 1, 0)

        def step(carry, qkv):
            kv, ksum = carry
            qt, kt, vt = qkv
            kv = kv + kt[..., :, None] * vt[..., None, :]
            ksum = ksum + kt
            num = jnp.einsum('bhd,bhde->bhe', qt, kv)
            den = jnp.einsum('bhd,bhd->bh', qt, ksum) + EPS
            return ((kv, ksum), num / den[..., None])
        kv0 = jnp.zeros((B, H, D, D), dtype=x.dtype)
        ks0 = jnp.zeros((B, H, D), dtype=x.dtype)
        _, out = jax.lax.scan(step, (kv0, ks0), (q_t, k_t, v_t))
        out = jnp.moveaxis(out, 0, 1).reshape(B, S, H * D)
        return out @ Wo

    def _L1_attn_b_ref(hidden_states, Wq, Wk, Wv, Wb, conv_q_w, conv_k_w, conv_v_w, local_w, mid_w, r_w1, r_b1, r_w2, r_b2, mix_w, onorm_w, Wo):
        import jax, jax.numpy as jnp
        import numpy as np
        CHUNK = 32
        FLOOR = 0.01
        EPS_MIX = 1e-05
        EPS_NORM = 1e-05

        def l2norm(x):
            return x / jnp.sqrt(jnp.sum(x * x, -1, keepdims=True) + 1e-12)

        def dw_causal_conv(x, w):
            K = w.shape[-1]
            L = x.shape[1]
            xp = jnp.pad(x, ((0, 0), (K - 1, 0), (0, 0)))
            y = jnp.zeros_like(x)
            for t in range(K):
                y = y + xp[:, t:t + L, :] * w[:, t]
            return y

        def delta_rule_chunkwise(q, k, v, beta):
            b, h, L, dk = q.shape
            dv = v.shape[-1]
            c = CHUNK
            n = L // c
            q = l2norm(q)
            k = l2norm(k)
            v = v * beta[..., None]
            kb = k * beta[..., None]
            rs = lambda x: x.reshape(b, h, n, c, -1)
            qc, kc, vc, kbc = (rs(q), rs(k), rs(v), rs(kb))
            T = -jnp.einsum('bhnid,bhnjd->bhnij', kbc, kc)
            tri_strict = jnp.tril(jnp.ones((c, c), bool), -1)
            T = jnp.where(tri_strict, T, 0.0)
            for i in range(1, c):
                T = T.at[..., i, :i].add(jnp.einsum('bhnj,bhnji->bhni', T[..., i, :], T[..., :, :i]))
            T = T + jnp.eye(c, dtype=T.dtype)
            u = jnp.einsum('bhnij,bhnjd->bhnid', T, vc)
            w = jnp.einsum('bhnij,bhnjd->bhnid', T, kbc)
            mask_incl = jnp.tril(jnp.ones((c, c), bool), 0)

            def step(S, inp):
                qi, ki, ui, wi = inp
                attn = jnp.einsum('bhid,bhjd->bhij', qi, ki)
                attn = jnp.where(mask_incl, attn, 0.0)
                u_i = ui - jnp.einsum('bhik,bhkd->bhid', wi, S)
                o_i = jnp.einsum('bhik,bhkd->bhid', qi, S) + jnp.einsum('bhij,bhjd->bhid', attn, u_i)
                S = S + jnp.einsum('bhci,bhcd->bhid', ki, u_i)
                return (S, o_i)
            S0 = jnp.zeros((b, h, dk, dv), q.dtype)
            xs = tuple((jnp.moveaxis(a, 2, 0) for a in (qc, kc, u, w)))
            S, o = jax.lax.scan(step, S0, xs)
            o = jnp.moveaxis(o, 0, 2).reshape(b, h, L, dv)
            return (o, S)
        B, L, D = hidden_states.shape
        H = mix_w.shape[0]
        dh = mix_w.shape[1]
        q = jax.nn.silu(dw_causal_conv(hidden_states @ Wq, conv_q_w))
        k = jax.nn.silu(dw_causal_conv(hidden_states @ Wk, conv_k_w))
        v = jax.nn.silu(dw_causal_conv(hidden_states @ Wv, conv_v_w))
        q4 = q.reshape(B, L, H, dh)
        k4 = k.reshape(B, L, H, dh)
        v4 = v.reshape(B, L, H, dh)
        beta = jax.nn.sigmoid(hidden_states @ Wb)
        delta_out, _ = delta_rule_chunkwise(jnp.transpose(q4, (0, 2, 1, 3)), jnp.transpose(k4, (0, 2, 1, 3)), jnp.transpose(v4, (0, 2, 1, 3)), jnp.transpose(beta, (0, 2, 1)))
        delta_out = jnp.transpose(delta_out, (0, 2, 1, 3))
        v_direct = v4
        vflat = v4.reshape(B, L, H * dh)
        local_out = dw_causal_conv(vflat, local_w).reshape(B, L, H, dh)
        mid_out = dw_causal_conv(vflat, mid_w).reshape(B, L, H, dh)
        outs = [local_out, mid_out, delta_out, v_direct]
        feats = []
        for o_ in outs:
            feats.append(o_.mean(-1))
            feats.append(jnp.var(o_, -1, ddof=1))
        for i in range(4):
            for j in range(i + 1, 4):
                feats.append((outs[i] * outs[j]).mean(-1))
        router_feat = jnp.concatenate([hidden_states] + feats, axis=-1)
        h1 = jax.nn.silu(router_feat @ r_w1 + r_b1)
        logits = (h1 @ r_w2 + r_b2).reshape(B, L, H, 4)
        p = jax.nn.softmax(logits, -1)
        p = p * (1.0 - 4.0 * FLOOR) + FLOOR
        mixed = sum((p[..., i:i + 1] * outs[i] for i in range(4)))
        rms = jnp.sqrt(jnp.mean(mixed * mixed, -1, keepdims=True) + EPS_MIX)
        mixed = mixed / rms * mix_w
        rms2 = jnp.sqrt(jnp.mean(mixed * mixed, -1, keepdims=True) + EPS_NORM)
        o_n = mixed / rms2 * onorm_w
        return o_n.reshape(B, L, H * dh) @ Wo

    def _L1_ffn_ref(x, gate_w, w1, w2):
        import jax, jax.numpy as jnp
        import numpy as np
        N, T, D = (4, 512, 128)
        NUM_EXPERTS = 8
        EXPERT_CAP = 2.0
        MLP_RATIO = 4
        HIDDEN = MLP_RATIO * D
        x = x.astype(jnp.float32)
        n, t, d = x.shape
        k = int(EXPERT_CAP * t / NUM_EXPERTS)
        scores = jnp.einsum('ntd,de->nte', x, gate_w)
        probs = jax.nn.softmax(scores, axis=-1)
        probs = jnp.transpose(probs, (0, 2, 1))
        g, m = jax.lax.top_k(probs, k)
        xin = jax.vmap(lambda xb, mb: xb[mb])(x, m)
        h = jax.nn.gelu(jnp.einsum('nekd,edf->nekf', xin, w1))
        h = jnp.einsum('nekf,efd->nekd', h, w2)
        weighted = g[..., None] * h
        flat_idx = (m + jnp.arange(n, dtype=m.dtype)[:, None, None] * t).reshape(-1)
        out = jnp.zeros((n * t, d), dtype=jnp.float32).at[flat_idx].add(weighted.reshape(-1, d))
        out = out.reshape(n, t, d)
        return out.astype(jnp.bfloat16)
    x = L0_attn_a_x
    x = x + _L0_attn_a_ref(_layernorm(x, axis=-1), L0_attn_a_W_dq, L0_attn_a_W_uq, L0_attn_a_W_dkv, L0_attn_a_W_uk, L0_attn_a_W_uv, L0_attn_a_W_o)
    x = x + _L0_ffn_ref(_layernorm(x, axis=-1), L0_ffn_gate_w, L0_ffn_w1, L0_ffn_b1, L0_ffn_w2, L0_ffn_b2, L0_ffn_w3, L0_ffn_b3, L0_ffn_sw1, L0_ffn_sw2, L0_ffn_sw3)
    x = x + _L0_attn_b_ref(_layernorm(x, axis=-1), L0_attn_b_Wq, L0_attn_b_Wk, L0_attn_b_Wv, L0_attn_b_Wo)
    x = x + _L0_ffn_ref(_layernorm(x, axis=-1), L0_ffn_gate_w, L0_ffn_w1, L0_ffn_b1, L0_ffn_w2, L0_ffn_b2, L0_ffn_w3, L0_ffn_b3, L0_ffn_sw1, L0_ffn_sw2, L0_ffn_sw3)
    x = x + _L1_attn_a_ref(_layernorm(x, axis=-1), L1_attn_a_Wq, L1_attn_a_Wk, L1_attn_a_Wv, L1_attn_a_Wo, L1_attn_a_proj)
    x = x + _L1_ffn_ref(_layernorm(x, axis=-1), L1_ffn_gate_w, L1_ffn_w1, L1_ffn_w2)
    x = x + _L1_attn_b_ref(_layernorm(x, axis=-1), L1_attn_b_Wq, L1_attn_b_Wk, L1_attn_b_Wv, L1_attn_b_Wb, L1_attn_b_conv_q_w, L1_attn_b_conv_k_w, L1_attn_b_conv_v_w, L1_attn_b_local_w, L1_attn_b_mid_w, L1_attn_b_r_w1, L1_attn_b_r_b1, L1_attn_b_r_w2, L1_attn_b_r_b2, L1_attn_b_mix_w, L1_attn_b_onorm_w, L1_attn_b_Wo)
    x = x + _L1_ffn_ref(_layernorm(x, axis=-1), L1_ffn_gate_w, L1_ffn_w1, L1_ffn_w2)
    return x

_drawn_inputs = setup_inputs


def setup_inputs(seed=0):
    import zlib

    import numpy as np

    out = dict(_drawn_inputs(seed))
    spreads = {'L1_attn_b_r_b1': (0.0, 0.461),
     'L1_attn_b_mix_w': (1.0, 0.2),
     'L1_attn_b_onorm_w': (1.0, 0.2)}
    factors = {'L0_attn_a_W_dq': 8.0,
     'L0_attn_a_W_uq': 8.0,
     'L0_attn_a_W_dkv': 8.0,
     'L0_attn_a_W_uk': 8.0,
     'L0_attn_a_W_uv': 8.0,
     'L0_attn_a_W_o': 8.0,
     'L0_ffn_b1': 8.0,
     'L0_ffn_b2': 8.0,
     'L0_ffn_b3': 8.0,
     'L1_attn_a_Wq': 6.533,
     'L1_attn_a_Wk': 4.376,
     'L1_attn_a_proj': 4.861,
     'L1_ffn_gate_w': 5.033,
     'L1_ffn_w1': 4.449,
     'L1_ffn_w2': 4.36,
     'L0_attn_b_Wq': 3.222}
    for name, (base, spread) in spreads.items():
        noise = np.random.default_rng([zlib.crc32(name.encode()), seed]).standard_normal(out[name].shape)
        drawn = base * np.exp(spread * noise) if base else spread * noise
        out[name] = jnp.asarray(drawn.astype(out[name].dtype))
    for name, factor in factors.items():
        out[name] = (out[name] * factor).astype(out[name].dtype)
    return out
```

```python
from contextlib import ExitStack

import numpy as np
import concourse.bass as bass
from concourse import mybir

F32 = mybir.dt.float32
BF16 = mybir.dt.bfloat16
ALU = mybir.AluOpType
ACT = mybir.ActivationFunctionType
AX = mybir.AxisListType

P = 128
D = 128
T = 256
LN_EPS = 1e-5
NEG = -1e30


class Counter:

    def __init__(self, sem, per, credit):
        self.sem, self.per, self.credit = sem, per, per if credit else 0

    def now(self, i, n=None):
        return i * self.per + (self.per if n is None else n) + self.credit

    def last(self, i, n=None):
        assert self.credit
        return i * self.per + (self.per if n is None else n)


class Stage:

    def __init__(self, nc, name):
        self.nc, self.name, self.ctx = nc, name, ExitStack()
        self.counters = []

    def __enter__(self):
        self.ctx.__enter__()
        return self

    def sb(self, name, shape, dt=F32):
        return self.ctx.enter_context(self.nc.sbuf_tensor(f"{self.name}_{name}", shape, dt))

    def ps(self, name, cols, dt=F32):
        return self.ctx.enter_context(self.nc.psum_tensor(f"{self.name}_{name}", [P, cols], dt))

    def semaphore(self, name, per, credit=False):
        s = Counter(self.ctx.enter_context(self.nc.semaphore(f"{self.name}_{name}")), per, credit)
        self.counters.append(s)
        return s

    def chain(self):
        return self.semaphore("vector_chain", 1)

    def give_credits(self, eng):
        for s in self.counters:
            if s.credit:
                eng.sem_inc(s.sem, s.credit)

    def __exit__(self, *a):
        if a[0] is None:
            sems = [s.sem for s in self.counters]
            for s in sems:
                self.nc.gpsimd.sem_clear(s)
            self.nc.all_engine_barrier()
        return self.ctx.__exit__(*a)


class Chain:

    def __init__(self, eng, counter):
        self.eng, self.sem, self.n = eng, counter.sem, 0

    def restart(self):
        self.eng.sem_clear(self.sem)
        self.n = 0

    def mark(self, ins):
        self.n += 1
        ins.then_inc(self.sem, 1)
        return self.n

    def need(self, n):
        self.eng.wait_ge(self.sem, n)

    def link(self, ins):
        self.need(self.mark(ins))


def const_table():
    p = np.arange(P)[:, None]
    f = np.arange(P)[None, :]
    parts = {
        "ident": (p == f),
        "neg_after": np.where(f > p, NEG, 0.0),
        "upto_f": (p <= f),
        "head_rows": ((p // 8) % 4 == np.arange(4)[None, :]),
        "before": (f < p),
        "same_head": (p // 32 == f // 32),
        **{f"mT{s}": ((p // (2 * s) == f // (2 * s)) & (f // s % 2 == 1) & (p // s % 2 == 0)) for s in (1, 2, 4, 8, 16)},
        "m1": ((p // 2 == f // 2) & (p % 2 == 1) & (f % 2 == 0)),
        "mT_off": (p // 32 < f // 32),
        "ones128": np.ones((1, P)) + 0 * p,
        "own_head": (p // 8 == np.arange(16)[None, :]),
        "iota": np.tile(np.arange(64)[None, :] + 1, (P, 1)),
        "earlier8": np.tile((np.arange(8)[None, :] < np.arange(8)[:, None]).reshape(1, 64), (P, 1)),
        "ones32": np.ones((1, 32)) + 0 * p,
        "pick8": (np.arange(P)[:, None, None] == np.arange(8)[None, :, None]) * np.ones((1, 1, P)),
    }
    out, at, n = [], {}, 0
    for k, v in parts.items():
        v = np.asarray(v, np.float32).reshape(P, -1)
        at[k] = (n, n + v.shape[1])
        n += v.shape[1]
        out.append(v)
    return np.concatenate(out, 1), at


CONSTS, CONST_AT = const_table()


class Shared:

    def c(self, name):
        a, b = CONST_AT[name]
        return self.consts[:, a:b]


def residual(sh, vec, c, i, y, done):
    x = sh.x[:, bass.ds(2 * i, 2), :]
    n = c.mark(vec.tensor_tensor(x, x, y, ALU.add))
    c.need(n)
    for k in range(2):
        ins = vec.bn_stats(sh.stats[:, bass.ds(2 * i + k, 1), :], sh.x[:, bass.ds(2 * i + k, 1), :])
    if done is not None:
        ins.then_inc(done.sem, 1)


def front_vector(sh, st, vec, ch, i, xhat):
    for k in range(2):
        ins = vec.tensor_scalar(xhat[:, k, :], sh.x[:, bass.ds(2 * i + k, 1), :],
                                sh.mean[:, bass.ds(2 * i + k, 1)], sh.rstd[:, bass.ds(2 * i + k, 1)],
                                ALU.subtract, ALU.mult)
    return ins


def finish_stats(sh, name):
    nc = sh.nc
    with Stage(nc, name) as st:
        ch = st.chain()
        var_ready, std_ready = st.semaphore("var_ready", 1), st.semaphore("std_ready", 1)
        dm, var = st.sb("dm", [P, sh.tiles]), st.sb("var", [P, sh.tiles])
        with nc.Block() as block:
            s = sh.stats

            @block.vector
            def _(vec):
                c = Chain(vec, ch)
                vec.tensor_tensor(sh.mean[:], s[:, :, 1], s[:, :, 4], ALU.add)
                vec.tensor_tensor(var[:], s[:, :, 2], s[:, :, 5], ALU.add)
                c.link(vec.tensor_tensor(dm[:], s[:, :, 1], s[:, :, 4], ALU.subtract))
                c.link(vec.tensor_tensor(dm[:], dm[:], dm[:], ALU.mult))
                c.link(vec.tensor_scalar(dm[:], dm[:], 0.25, LN_EPS, ALU.mult, ALU.add))
                vec.scalar_tensor_tensor(var[:], var[:], 1.0 / D, dm[:], ALU.mult, ALU.add).then_inc(var_ready.sem, 1)
                c.link(vec.tensor_scalar(sh.mean[:], sh.mean[:], 0.5, None, ALU.mult))
                vec.wait_ge(std_ready.sem, 1)
                vec.reciprocal(sh.rstd[:], var[:])

            @block.scalar
            def _(act):
                act.wait_ge(var_ready.sem, 1)
                act.activation(var[:], var[:], ACT.Sqrt).then_inc(std_ready.sem, 1)


def latent_attention(sh, w):
    nc, NH, HS, L = sh.nc, 16, 8, 32
    SCALE = float(HS) ** -0.5
    NS = sh.seqs
    with Stage(nc, "latent") as st:
        wq, wqT, keffT, veff = (st.sb("wq", [P, P]), st.sb("wqT", [P, P]), st.sb("keffT", [L, P]), st.sb("veff", [L, P]))
        wk, wv = st.sb("wk", [P, P]), st.sb("wv", [P, P])
        identb, negb = st.sb("identb", [P, P], BF16), st.sb("negb", [P, 2 * P], BF16)
        xhat, xT = st.sb("xhat", [P, 2, P]), st.sb("xT", [P, T])
        q_h, k_f = st.sb("q_h", [P, 4, T]), st.sb("k_f", [P, T])
        v1 = st.sb("v1", [P, 2, NH, HS + 1])
        probs = st.sb("probs", [P, 2, 1024])
        probsT = st.sb("probsT", [P, 2, 1024])
        mx, rs = st.sb("mx", [P, 6, 8]), st.sb("rs", [P, 2, NH])
        y = st.sb("y", [P, 2, NH, HS])
        S = st.ps("scores", 2048)
        PT = st.ps("probsT_ps", 1024)
        FR = st.ps("front_ps", 512)
        QK = st.ps("qk_ps", 512)

        ch = st.chain()
        prep = st.semaphore("prep", 1)
        prep_sb = st.semaphore("prep_sb", 1)
        xhat_ready = st.semaphore("xhat_ready", 1)
        xT_ps, xT_sb = st.semaphore("xT_ps", 1, True), st.semaphore("xT_sb", 1)
        proj = st.semaphore("proj", 2, True)
        q_ready, kv_ready = st.semaphore("q_ready", 1, True), st.semaphore("kv_ready", 2, True)
        scored = st.semaphore("scored", 6, True)
        shifted = st.semaphore("shifted", 6, True)
        expd = st.semaphore("expd", 6, True)
        turned = st.semaphore("turned", 6, True)
        turned_sb = st.semaphore("turned_sb", 6, True)
        summed = st.semaphore("summed", 6, True)
        out_read = st.semaphore("out_read", 1, True)

        def unit(u):
            g, jp = u // 2, u % 2
            if g == 0:
                return 0, [(j, r, [(0, j * 512 + r * 128)]) for j in (2 * jp, 2 * jp + 1) for r in range(4)]
            return 1, [(j, 2 * (g - 1) + r, [(0, j * 512 + r * 256), (1, j * 512 + r * 256 + 128)])
                       for j in (2 * jp, 2 * jp + 1) for r in range(2)]

        with nc.Block() as block:

            @block.gpsimd
            def _(pool):
                st.give_credits(pool)

            @block.tensor
            def _(pe):
                def mm(out, lhsT, rhs):
                    return pe.matmul(out, lhsT, rhs, start=True, stop=True)

                mm(FR[:, 0:128], w["A_wdq"], w["A_wuqT"])
                mm(FR[:, 128:256], w["A_wuqT"], w["A_wdq"])
                mm(FR[0:L, 256:384], w["A_wuv"], w["A_woT"]).then_inc(prep.sem, 1)
                pe.wait_ge(prep_sb.sem, 1)
                mm(QK[0:L, 0:128], w["A_wuk"], wqT[:])
                mm(QK[:, 128:256], w["A_wdkv"], veff[:]).then_inc(prep.sem, 1)
                pe.wait_ge(prep_sb.sem, 2)
                mm(QK[:, 256:384], w["A_wdkv"], keffT[:]).then_inc(prep.sem, 1)
                pe.wait_ge(prep_sb.sem, 3)

                with pe.Fori(0, NS) as i:
                    pe.wait_ge(xhat_ready.sem, xhat_ready.now(i))
                    pe.wait_ge(kv_ready.sem, kv_ready.last(i))
                    for k in range(2):
                        ins = pe.transpose(FR[:, 128 * k:128 * k + 128], xhat[:, k, :], sh.c("ident"))
                    ins.then_inc(xT_ps.sem, 1)
                    pe.wait_ge(xT_sb.sem, xT_sb.now(i))
                    pe.wait_ge(out_read.sem, out_read.last(i))
                    mm(QK[:, 0:T], wq[:], xT[:]).then_inc(proj.sem, 1)
                    mm(FR[:, 0:T], wk[:], xT[:])
                    for k in range(2):
                        ins = mm(FR[:, T + 128 * k:T + 128 * k + 128], xT[:, 128 * k:128 * k + 128], wv[:])
                    ins.then_inc(proj.sem, 1)

                    def scores(u):
                        tq, heads = unit(u)
                        if u < 2:
                            pe.wait_ge(shifted.sem, shifted.last(i, u + 5))
                        else:
                            pe.wait_ge(shifted.sem, shifted.now(i, u - 1))
                        for j, r, cols in heads:
                            c0, n = cols[0][1], 128 * len(cols)
                            pe.matmul(S[:, c0:c0 + n], q_h[32 * j:32 * j + 32, r, 128 * tq:128 * tq + 128],
                                      k_f[32 * j:32 * j + 32, 0:n], start=True, stop=False)
                            ins = pe.matmul(S[:, c0:c0 + n], identb[:], negb[:, 256 - n:256], start=False, stop=True)
                        ins.then_inc(scored.sem, 1)

                    def turn(u):
                        pe.wait_ge(expd.sem, expd.now(i, u + 1))
                        if u:
                            pe.wait_ge(turned_sb.sem, turned_sb.now(i, u))
                        else:
                            pe.wait_ge(turned_sb.sem, turned_sb.last(i))
                        for b in range(8):
                            ins = pe.transpose(PT[:, 128 * b:128 * b + 128], probs[:, u % 2, 128 * b:128 * b + 128], sh.c("ident"))
                        ins.then_inc(turned.sem, 1)

                    def values(u):
                        pe.wait_ge(turned_sb.sem, turned_sb.now(i, u + 1))
                        tq, heads = unit(u)
                        b = 0
                        for j, r, cols in heads:
                            h = 4 * j + r
                            o = QK[:, 144 * tq + 9 * h:144 * tq + 9 * h + 9]
                            for n, (tk, _) in enumerate(cols):
                                ins = pe.matmul(o, probsT[:, u % 2, 128 * b:128 * b + 128], v1[:, tk, h, :],
                                                start=(n == 0), stop=(n == len(cols) - 1))
                                b += 1
                        ins.then_inc(summed.sem, 1)

                    pe.wait_ge(q_ready.sem, q_ready.now(i))
                    pe.wait_ge(kv_ready.sem, kv_ready.now(i))
                    scores(0)
                    scores(1)
                    for u in range(6):
                        turn(u)
                        if u + 2 < 6:
                            scores(u + 2)
                        if u:
                            values(u - 1)
                    values(5)

            @block.scalar
            def _(act):
                act.wait_ge(prep.sem, 1)
                act.copy(wq[:], FR[:, 0:128])
                act.copy(wqT[:], FR[:, 128:256])
                act.copy(veff[:], FR[0:L, 256:384]).then_inc(prep_sb.sem, 1)
                act.wait_ge(prep.sem, 2)
                act.copy(keffT[:], QK[0:L, 0:128])
                act.copy(wv[:], QK[:, 128:256]).then_inc(prep_sb.sem, 1)
                act.wait_ge(prep.sem, 3)
                act.copy(identb[:], sh.c("ident"))
                act.copy(wk[:], QK[:, 256:384])
                act.mul(negb[:, 0:P], sh.c("neg_after"), 0.0)
                act.copy(negb[:, P:2 * P], sh.c("neg_after"))
                act.copy(v1[:, :, :, HS], sh.c("ones32").rearrange("p (a b) -> p a b", a=2)).then_inc(prep_sb.sem, 1)
                with act.Fori(0, NS) as i:
                    act.wait_ge(xT_ps.sem, xT_ps.now(i))
                    act.wait_ge(proj.sem, proj.last(i))
                    act.copy(xT[:], FR[:, 0:T]).then_inc(xT_sb.sem, 1)
                    act.wait_ge(proj.sem, proj.now(i, 2))
                    act.wait_ge(scored.sem, scored.last(i))
                    act.copy(k_f[:], FR[:, 0:T]).then_inc(kv_ready.sem, 1)
                    act.wait_ge(summed.sem, summed.last(i))
                    act.copy(v1[:, :, :, 0:HS], FR[:, T:2 * T].rearrange("p (a h d) -> p a h d", a=2, h=NH)).then_inc(kv_ready.sem, 1)

                    def expo(u):
                        act.wait_ge(shifted.sem, shifted.now(i, u + 1))
                        act.activation(probs[:, u % 2, :], probs[:, u % 2, :], ACT.Exp, scale=SCALE).then_inc(expd.sem, 1)

                    def evac(u):
                        act.wait_ge(turned.sem, turned.now(i, u + 1))
                        if u >= 2:
                            act.wait_ge(summed.sem, summed.now(i, u - 1))
                        act.copy(probsT[:, u % 2, :], PT[:]).then_inc(turned_sb.sem, 1)

                    expo(0)
                    for u in range(6):
                        if u + 1 < 6:
                            expo(u + 1)
                        evac(u)

            @block.vector
            def _(vec):
                c = Chain(vec, ch)
                with vec.Fori(0, NS) as i:
                    c.restart()
                    vec.wait_ge(out_read.sem, out_read.last(i))
                    vec.wait_ge(xT_ps.sem, xT_ps.last(i))
                    front_vector(sh, st, vec, c, i, xhat).then_inc(xhat_ready.sem, 1)
                    vec.wait_ge(proj.sem, proj.now(i, 1))
                    vec.wait_ge(scored.sem, scored.last(i))
                    for r in range(4):
                        ins = vec.tensor_scalar(q_h[:, r, :], QK[:, 0:T], sh.c("head_rows")[:, r:r + 1], None, ALU.mult)
                    ins.then_inc(q_ready.sem, 1)
                    for u in range(6):
                        tq, heads = unit(u)
                        n = len(heads)
                        s = S[:, 1024 * (u % 2):1024 * (u % 2) + 1024].rearrange("p (h s) -> p h s", h=n)
                        vec.wait_ge(scored.sem, scored.now(i, u + 1))
                        c.link(vec.tensor_reduce(mx[:, u, 0:n], s, AX.X, ALU.max))
                        if u >= 2:
                            vec.wait_ge(turned.sem, turned.now(i, u - 1))
                        else:
                            vec.wait_ge(turned.sem, turned.last(i, u + 5))
                        vec.tensor_tensor(probs[:, u % 2, :].rearrange("p (h s) -> p h s", h=n), s,
                                          mx[:, u, 0:n].unsqueeze(2).broadcast_to([P, n, 1024 // n]),
                                          ALU.subtract).then_inc(shifted.sem, 1)
                    vec.wait_ge(summed.sem, summed.now(i, 6))
                    o = QK[:, 0:288].rearrange("p (a h d) -> p a h d", a=2, h=NH)
                    c.link(vec.reciprocal(rs[:], o[:, :, :, HS]))
                    for k in range(2):
                        m = c.mark(vec.tensor_tensor(y[:, k], o[:, k, :, 0:HS], rs[:, k].unsqueeze(2).broadcast_to([P, NH, HS]), ALU.mult))
                    c.need(m)
                    residual(sh, vec, c, i, y[:].rearrange("p a h d -> p a (h d)"), out_read)


def gate(sh, name, gate_w, logits, xT_all):
    nc, turns = sh.nc, sh.seqs // 2
    with Stage(nc, name) as st:
        xhat, xT = st.sb("xhat", [P, 4, P]), st.sb("xT", [P, 4 * P])
        XT, LG = st.ps("xT_ps", 512), st.ps("logits_ps", 32)
        xhat_ready = st.semaphore("xhat_ready", 1)
        turned, xT_sb = st.semaphore("turned", 1, True), st.semaphore("xT_sb", 1, True)
        scored, scored_sb = st.semaphore("scored", 1, True), st.semaphore("scored_sb", 1, True)
        kept = st.semaphore("kept", 1, True)
        with nc.Block() as block:

            @block.gpsimd
            def _(pool):
                st.give_credits(pool)
                with pool.Fori(0, turns) as i:
                    pool.wait_ge(xT_sb.sem, xT_sb.now(i))
                    if xT_all is not None:
                        pool.tensor_copy(xT_all[:, bass.ds(i * 512, 512)], xT[:]).then_inc(kept.sem, 1)
                    else:
                        pool.sem_inc(kept.sem, 1)

            @block.vector
            def _(vec):
                with vec.Fori(0, turns) as i:
                    vec.wait_ge(turned.sem, turned.last(i))
                    for k in range(4):
                        t = 4 * i + k
                        ins = vec.tensor_scalar(xhat[:, k, :], sh.x[:, bass.ds(t, 1), :], sh.mean[:, bass.ds(t, 1)],
                                                sh.rstd[:, bass.ds(t, 1)], ALU.subtract, ALU.mult)
                    ins.then_inc(xhat_ready.sem, 1)
                    vec.wait_ge(scored.sem, scored.now(i))
                    vec.tensor_copy(logits[:, bass.ds(4 * i, 4), :], LG[:].rearrange("p (k e) -> p k e", k=4)).then_inc(scored_sb.sem, 1)

            @block.tensor
            def _(pe):
                with pe.Fori(0, turns) as i:
                    pe.wait_ge(xhat_ready.sem, xhat_ready.now(i))
                    pe.wait_ge(xT_sb.sem, xT_sb.last(i))
                    for k in range(4):
                        ins = pe.transpose(XT[:, 128 * k:128 * k + 128], xhat[:, k, :], sh.c("ident"))
                    ins.then_inc(turned.sem, 1)
                    pe.wait_ge(xT_sb.sem, xT_sb.now(i))
                    pe.wait_ge(scored_sb.sem, scored_sb.last(i))
                    for k in range(4):
                        ins = pe.matmul(LG[:, 8 * k:8 * k + 8], xT[:, 128 * k:128 * k + 128], gate_w, start=True, stop=True)
                    ins.then_inc(scored.sem, 1)

            @block.scalar
            def _(act):
                with act.Fori(0, turns) as i:
                    act.wait_ge(turned.sem, turned.now(i))
                    act.wait_ge(scored.sem, scored.last(i))
                    act.wait_ge(kept.sem, kept.last(i))
                    act.copy(xT[:], XT[:]).then_inc(xT_sb.sem, 1)


def softmax8(sh, name, logits, after=None):
    nc, n = sh.nc, sh.tiles
    with Stage(nc, name) as st:
        ch, shifted, expd = st.chain(), st.semaphore("shifted", 1), st.semaphore("expd", 1)
        m = st.sb("m", [P, n])
        extra = after and after(st)
        with nc.Block() as block:
            @block.vector
            def _(vec):
                c = Chain(vec, ch)
                c.link(vec.tensor_reduce(m[:], logits[:], AX.X, ALU.max))
                vec.tensor_tensor(logits[:], logits[:], m[:].unsqueeze(2).broadcast_to([P, n, 8]),
                                  ALU.subtract).then_inc(shifted.sem, 1)
                vec.wait_ge(expd.sem, 1)
                c.link(vec.tensor_reduce(m[:], logits[:], AX.X, ALU.add))
                c.link(vec.reciprocal(m[:], m[:]))
                c.link(vec.tensor_tensor(logits[:], logits[:], m[:].unsqueeze(2).broadcast_to([P, n, 8]), ALU.mult))
                if extra:
                    extra(vec, c)

            @block.scalar
            def _(act):
                act.wait_ge(shifted.sem, 1)
                act.activation(logits[:], logits[:], ACT.Exp).then_inc(expd.sem, 1)


def top2_ffn(sh, w, name):
    nc, NE, NS = sh.nc, 8, sh.seqs
    with ExitStack() as ctx:
        def keep(n, shape, dt=F32):
            return ctx.enter_context(nc.sbuf_tensor(f"{name}_{n}", shape, dt))
        g_all, xT_all = keep("g_all", [P, sh.tiles, NE]), keep("xT_all", [P, sh.tiles * P])
        picked_all = keep("picked_all", [P, sh.tiles, NE])
        gate(sh, name + "_gate", w["B_gateT"], g_all, xT_all)

        def top2(st):
            half = sh.tiles // 2
            better, equal = st.sb("better", [P, half, NE, NE]), st.sb("equal", [P, half, NE, NE])
            rank = st.sb("rank", [P, half, NE])

            def run(vec, c):
                for b in range(2):
                    g = g_all[:, b * half:(b + 1) * half, :]
                    other = g.unsqueeze(2).broadcast_to([P, half, NE, NE])
                    own = g.unsqueeze(3).broadcast_to([P, half, NE, NE])
                    vec.tensor_tensor(better[:], other, own, ALU.is_gt)
                    c.link(vec.tensor_tensor(equal[:], other, own, ALU.is_equal))
                    tie = sh.c("earlier8").rearrange("p (a b) -> p a b", a=NE).unsqueeze(1).broadcast_to([P, half, NE, NE])
                    c.link(vec.tensor_tensor(equal[:], equal[:], tie, ALU.mult))
                    c.link(vec.tensor_tensor(better[:], better[:], equal[:], ALU.add))
                    c.link(vec.tensor_reduce(rank[:], better[:], AX.X, ALU.add))
                    picked = picked_all[:, b * half:(b + 1) * half, :]
                    c.link(vec.tensor_scalar(picked, rank[:], 1.5, None, ALU.is_lt))
                    c.link(vec.tensor_tensor(g, g, picked, ALU.mult))
            return run

        softmax8(sh, name + "_top2", g_all, top2)

        with Stage(nc, name) as st:
            g, picked = st.sb("g", [P, 2, NE]), st.sb("picked", [P, 2, NE], BF16)
            identb = st.sb("identb", [P, P], BF16)
            xs, picked_f = st.sb("xs", [P, 4, T]), st.sb("picked_f", [P, 2, 512])
            h = st.sb("h", [P, 2, T])
            t1, y, ysum, hz = st.sb("t1", [P, 2, T]), st.sb("y", [P, 2, T]), st.sb("ysum", [P, T]), st.sb("hz", [P, 2, T])
            GB, MB = st.ps("g_ps", 512), st.ps("picked_ps", 512)
            H = [st.ps("h0_ps", 512), st.ps("h1_ps", 512)]
            X = [st.ps("x0_ps", 512), st.ps("x1_ps", 512)]
            Y = st.ps("y_ps", 512)
            ch = st.chain()
            ready = st.semaphore("ready", 1)
            staged = st.semaphore("staged", 1)
            spread = st.semaphore("spread", 4, True)
            picked_sb = st.semaphore("picked_sb", 4, True)
            scaled = st.semaphore("scaled", 8, True)
            up = st.semaphore("up", 10, True)
            act_done = st.semaphore("act_done", 10, True)
            down = st.semaphore("down", 8, True)
            taken = st.semaphore("taken", 10, True)
            total = st.semaphore("total", 1)
            out_ps, out_read = st.semaphore("out_ps", 1, True), st.semaphore("out_read", 1, True)

            with nc.Block() as block:

                @block.gpsimd
                def _(pool):
                    pool.tensor_copy(identb[:], sh.c("ident")).then_inc(ready.sem, 1)
                    st.give_credits(pool)
                    with pool.Fori(0, NS) as i:
                        pool.wait_ge(spread.sem, spread.last(i))
                        pool.tensor_copy(g[:], g_all[:, bass.ds(2 * i, 2), :])
                        pool.tensor_copy(picked[:], picked_all[:, bass.ds(2 * i, 2), :]).then_inc(staged.sem, 1)

                @block.tensor
                def _(pe):
                    pe.wait_ge(ready.sem, 1)
                    with pe.Fori(0, NS) as i:
                        pe.wait_ge(staged.sem, staged.now(i))
                        xT = xT_all[:, bass.ds(i * T, T)]

                        def prev(sig, m, n):
                            if m > 0:
                                pe.wait_ge(sig.sem, sig.now(i, m))
                            else:
                                pe.wait_ge(sig.sem, sig.last(i, m + n))

                        def spread_pair(p):
                            prev(scaled, 2 * p, 8)
                            prev(picked_sb, p, 4)
                            for e in (2 * p, 2 * p + 1):
                                for k in range(2):
                                    c0 = 256 * (e % 2) + 128 * k
                                    pe.transpose(GB[:, c0:c0 + 128], g[:, k, e:e + 1].broadcast_to([P, P]), sh.c("ident"))
                                    ins = pe.matmul(MB[:, c0:c0 + 128], picked[:, k, e:e + 1].broadcast_to([P, P]), identb[:],
                                                    start=True, stop=True)
                            ins.then_inc(spread.sem, 1)

                        def expand(e):
                            prev(act_done, e - 1, 10)
                            prev(taken, e - 1, 10)
                            if e < NE:
                                pe.wait_ge(scaled.sem, scaled.now(i, e + 1))
                                a, b, src = w["B_w1T"][:, 128 * e:128 * e + 128], w["B_w3T"][:, 128 * e:128 * e + 128], xs[:, e % 4, :]
                            else:
                                c0 = 128 * (e - NE)
                                a, b, src = w["B_sw1T"][:, c0:c0 + 128], w["B_sw2T"][:, c0:c0 + 128], xT
                            pe.matmul(H[e % 2][:, 0:T], a, src, start=True, stop=True)
                            pe.matmul(X[e % 2][:, 0:T], b, src, start=True, stop=True).then_inc(up.sem, 1)

                        def contract(e):
                            pe.wait_ge(act_done.sem, act_done.now(i, e + 1))
                            pe.matmul(X[e % 2][:, T:2 * T], w["B_w2T"][:, 128 * e:128 * e + 128], h[:, e % 2, :],
                                      start=True, stop=True).then_inc(down.sem, 1)

                        spread_pair(0)
                        expand(0)
                        expand(1)
                        for e in range(NE):
                            if e % 2 == 0 and e < 6:
                                spread_pair(e // 2 + 1)
                            contract(e)
                            expand(e + 2)
                        pe.wait_ge(total.sem, total.now(i))
                        pe.wait_ge(out_read.sem, out_read.last(i))
                        for k in range(2):
                            t = slice(128 * k, 128 * k + 128)
                            pe.matmul(Y[:, t], hz[:, 0, t], w["B_sw3T"][:, 0:128], start=True, stop=False)
                            pe.matmul(Y[:, t], hz[:, 1, t], w["B_sw3T"][:, 128:256], start=False, stop=False)
                            ins = pe.matmul(Y[:, t], ysum[:, t], sh.c("ident"), start=False, stop=True)
                        ins.then_inc(out_ps.sem, 1)

                @block.scalar
                def _(act):
                    with act.Fori(0, NS) as i:
                        def masks(p):
                            act.wait_ge(spread.sem, spread.now(i, p + 1))
                            if p < 2:
                                act.wait_ge(taken.sem, taken.last(i))
                            else:
                                act.wait_ge(taken.sem, taken.now(i, 2 * (p - 2) + 2))
                            act.copy(picked_f[:, p % 2, :], MB[:]).then_inc(picked_sb.sem, 1)

                        masks(0)
                        for e in range(10):
                            if e % 2 == 1 and e < 7:
                                masks((e + 1) // 2)
                            act.wait_ge(up.sem, up.now(i, e + 1))
                            if e < 2:
                                act.wait_ge(taken.sem, taken.last(i))
                            else:
                                act.wait_ge(down.sem, down.now(i, e - 1))
                            bias = w["B_b1T"][:, e:e + 1] if e < NE else 0.0
                            act.activation(h[:, e % 2, :], H[e % 2][:, 0:T], ACT.Silu, bias=bias).then_inc(act_done.sem, 1)

                @block.vector
                def _(vec):
                    c = Chain(vec, ch)
                    with vec.Fori(0, NS) as i:
                        c.restart()
                        vec.wait_ge(out_read.sem, out_read.last(i))
                        xT = xT_all[:, bass.ds(i * T, T)]

                        def scale(e):
                            vec.wait_ge(spread.sem, spread.now(i, e // 2 + 1))
                            if e < 4:
                                vec.wait_ge(up.sem, up.last(i))
                            else:
                                vec.wait_ge(up.sem, up.now(i, e - 3))
                            vec.tensor_tensor(xs[:, e % 4, :], xT, GB[:, 256 * (e % 2):256 * (e % 2) + 256], ALU.mult).then_inc(scaled.sem, 1)

                        scale(0)
                        scale(1)
                        done_y = None
                        for e in range(NE):
                            vec.wait_ge(down.sem, down.now(i, e + 1))
                            vec.wait_ge(picked_sb.sem, picked_sb.now(i, e // 2 + 1))
                            m = picked_f[:, (e // 2) % 2, 256 * (e % 2):256 * (e % 2) + 256]
                            n1 = c.mark(vec.scalar_tensor_tensor(t1[:, e % 2, :], X[e % 2][:, 0:T], w["B_b3T"][:, e:e + 1], m, ALU.add, ALU.mult))
                            if e + 2 < NE:
                                scale(e + 2)
                            c.need(n1)
                            dst = ysum[:] if e == 0 else y[:, e % 2, :]
                            vec.scalar_tensor_tensor(dst, X[e % 2][:, T:2 * T], w["B_b2T"][:, e:e + 1], t1[:, e % 2, :],
                                                     ALU.add, ALU.mult).then_inc(taken.sem, 1)
                            if e:
                                vec.wait_ge(taken.sem, taken.now(i, e + 1))
                                done_y = c.mark(vec.tensor_tensor(ysum[:], ysum[:], y[:, e % 2, :], ALU.add))
                            else:
                                vec.wait_ge(taken.sem, taken.now(i, 1))
                                done_y = 0
                            if done_y:
                                c.need(done_y)
                        for s in range(2):
                            e = NE + s
                            vec.wait_ge(act_done.sem, act_done.now(i, e + 1))
                            vec.wait_ge(out_ps.sem, out_ps.last(i))
                            vec.tensor_tensor(hz[:, s, :], h[:, e % 2, :], X[e % 2][:, 0:T], ALU.mult).then_inc(taken.sem, 1)
                        vec.wait_ge(taken.sem, taken.now(i))
                        vec.sem_inc(total.sem, 1)
                        vec.wait_ge(out_ps.sem, out_ps.now(i))
                        residual(sh, vec, c, i, Y[:, 0:T].rearrange("p (a b) -> p a b", a=2), out_read)


def top2_ffn_first(sh, w):
    top2_ffn(sh, w, "ffn_b")


def top2_ffn_second(sh, w):
    top2_ffn(sh, w, "ffn_d")


def linear_attention_small(sh, w):
    nc, NH, HS, NS = sh.nc, 16, 8, sh.seqs
    EPS = 1e-8
    with Stage(nc, "small") as st:
        xhat, xT = st.sb("xhat", [P, 2, P]), st.sb("xT", [P, T])
        e, f = st.sb("e", [P, 2 * T]), st.sb("f", [P, 2 * T])
        neg = st.sb("neg", [P, 2 * T])
        q_h, k_t = st.sb("q_h", [P, 4, T]), st.sb("k_t", [P, P])
        v1, state = st.sb("v1", [P, 2, NH, HS + 1]), st.sb("state", [P, NH, HS + 1])
        A = st.sb("A", [P, 2, 1024])
        den, y, yT = st.sb("den", [P, 2, NH]), st.sb("y", [P, 2, NH, HS]), st.sb("yT", [P, T])
        S = st.ps("scores", 2048)
        FR, QK, O, Y = (st.ps(n, 512) for n in ("front_ps", "qk_ps", "o_ps", "y_ps"))

        ch = st.chain()
        ready = st.semaphore("ready", 1)
        xhat_ready = st.semaphore("xhat_ready", 1)
        xT_ps, xT_sb = st.semaphore("xT_ps", 1, True), st.semaphore("xT_sb", 1, True)
        qk_ps, v_ps = st.semaphore("qk_ps", 1, True), st.semaphore("v_ps", 1, True)
        neg_ready = st.semaphore("neg_ready", 1)
        elu_in, f_ready = st.semaphore("elu_in", 1, True), st.semaphore("f_ready", 1)
        v_sb = st.semaphore("v_sb", 1, True)
        q_ready = st.semaphore("q_ready", 1)
        kt_ps, kt_sb = st.semaphore("kt_ps", 1), st.semaphore("kt_sb", 1)
        state_ps, state_sb = st.semaphore("state_ps", 1), st.semaphore("state_sb", 1, True)
        scored, masked, summed = st.semaphore("scored", 4, True), st.semaphore("masked", 4, True), st.semaphore("summed", 4, True)
        y_ready, yT_ps, yT_sb = st.semaphore("y_ready", 1, True), st.semaphore("yT_ps", 1, True), st.semaphore("yT_sb", 1)
        out_ps, out_read = st.semaphore("out_ps", 1, True), st.semaphore("out_read", 1, True)

        with nc.Block() as block:

            @block.gpsimd
            def _(pool):
                st.give_credits(pool)
                pool.tensor_copy(v1[:, :, :, HS], sh.c("ones32").rearrange("p (a b) -> p a b", a=2)).then_inc(ready.sem, 1)

            @block.tensor
            def _(pe):
                def mm(out, lhsT, rhs, start=True, stop=True, **k):
                    return pe.matmul(out, lhsT, rhs, start=start, stop=stop, **k)

                pe.wait_ge(ready.sem, 1)
                with pe.Fori(0, NS) as i:
                    pe.wait_ge(xhat_ready.sem, xhat_ready.now(i))
                    pe.wait_ge(v_sb.sem, v_sb.last(i))
                    for k in range(2):
                        ins = pe.transpose(FR[:, 128 * k:128 * k + 128], xhat[:, k, :], sh.c("ident"))
                    ins.then_inc(xT_ps.sem, 1)
                    pe.wait_ge(xT_sb.sem, xT_sb.now(i))
                    pe.wait_ge(state_sb.sem, state_sb.last(i))
                    mm(QK[:, 0:T], w["C_wqT"], xT[:])
                    mm(QK[:, T:2 * T], w["C_wkT"], xT[:]).then_inc(qk_ps.sem, 1)
                    for k in range(2):
                        ins = mm(FR[:, 128 * k:128 * k + 128], xT[:, 128 * k:128 * k + 128], w["C_wvT"])
                    ins.then_inc(v_ps.sem, 1)

                    def scores(u):
                        k, jp = u // 2, u % 2
                        if u < 2:
                            pe.wait_ge(masked.sem, masked.last(i, u + 3))
                        else:
                            pe.wait_ge(masked.sem, masked.now(i, u - 1))
                        t = slice(128 * k, 128 * k + 128)
                        for j in (2 * jp, 2 * jp + 1):
                            for r in range(4):
                                c0 = 512 * j + 128 * r
                                ins = mm(S[:, c0:c0 + 128], f[32 * j:32 * j + 32, T + 128 * k:T + 128 * k + 128], q_h[32 * j:32 * j + 32, r, t])
                        ins.then_inc(scored.sem, 1)

                    def values(u):
                        pe.wait_ge(masked.sem, masked.now(i, u + 1))
                        k, jp = u // 2, u % 2
                        if u == 0:
                            pe.wait_ge(v_sb.sem, v_sb.now(i))
                            pe.wait_ge(y_ready.sem, y_ready.last(i))
                        for b in range(8):
                            h = 8 * jp + b
                            ins = mm(O[:, 144 * k + 9 * h:144 * k + 9 * h + 9], A[:, u % 2, 128 * b:128 * b + 128], v1[:, k, h, :],
                                     start=(h == 0), stop=(k == 0), skip_group_check=True)
                        if u == 3:
                            pe.wait_ge(state_sb.sem, state_sb.now(i))
                            ins = mm(O[:, 144:288], f[:, 128:256], state[:].rearrange("p h d -> p (h d)"), start=False, skip_group_check=True)
                        ins.then_inc(summed.sem, 1)

                    pe.wait_ge(f_ready.sem, f_ready.now(i))
                    pe.transpose(QK[:, 0:128], f[:, T:T + 128], sh.c("ident")).then_inc(kt_ps.sem, 1)
                    pe.wait_ge(q_ready.sem, q_ready.now(i))
                    scores(0)
                    scores(1)
                    pe.wait_ge(kt_sb.sem, kt_sb.now(i))
                    pe.wait_ge(v_sb.sem, v_sb.now(i))
                    mm(QK[:, 0:144], k_t[:], v1[:, 0].rearrange("p h d -> p (h d)")).then_inc(state_ps.sem, 1)
                    values(0)
                    scores(2)
                    values(1)
                    scores(3)
                    values(2)
                    values(3)
                    pe.wait_ge(y_ready.sem, y_ready.now(i))
                    pe.wait_ge(out_read.sem, out_read.last(i))
                    for k in range(2):
                        ins = pe.transpose(Y[:, 128 * k:128 * k + 128], y[:, k].rearrange("p h d -> p (h d)"), sh.c("ident"))
                    ins.then_inc(yT_ps.sem, 1)
                    pe.wait_ge(yT_sb.sem, yT_sb.now(i))
                    for k in range(2):
                        ins = mm(Y[:, 128 * k:128 * k + 128], yT[:, 128 * k:128 * k + 128], w["C_woT"])
                    ins.then_inc(out_ps.sem, 1)

            @block.scalar
            def _(act):
                with act.Fori(0, NS) as i:
                    act.wait_ge(xT_ps.sem, xT_ps.now(i))
                    act.wait_ge(v_ps.sem, v_ps.last(i))
                    act.copy(xT[:], FR[:, 0:T]).then_inc(xT_sb.sem, 1)
                    act.wait_ge(qk_ps.sem, qk_ps.now(i))
                    act.wait_ge(y_ready.sem, y_ready.last(i))
                    act.activation(neg[:], QK[:], ACT.Relu, scale=-1.0).then_inc(neg_ready.sem, 1)
                    act.wait_ge(neg_ready.sem, neg_ready.now(i))
                    act.activation(e[:], neg[:], ACT.Exp, scale=-1.0).then_inc(elu_in.sem, 1)
                    act.wait_ge(v_ps.sem, v_ps.now(i))
                    act.wait_ge(summed.sem, summed.last(i))
                    act.copy(v1[:, :, :, 0:HS], FR[:, 0:T].rearrange("p (a h d) -> p a h d", a=2, h=NH)).then_inc(v_sb.sem, 1)
                    act.wait_ge(kt_ps.sem, kt_ps.now(i))
                    act.copy(k_t[:], QK[:, 0:128]).then_inc(kt_sb.sem, 1)
                    act.wait_ge(yT_ps.sem, yT_ps.now(i))
                    act.wait_ge(out_ps.sem, out_ps.last(i))
                    act.copy(yT[:], Y[:, 0:T]).then_inc(yT_sb.sem, 1)

            @block.vector
            def _(vec):
                c = Chain(vec, ch)
                with vec.Fori(0, NS) as i:
                    c.restart()
                    vec.wait_ge(out_read.sem, out_read.last(i))
                    vec.wait_ge(xT_ps.sem, xT_ps.last(i))
                    front_vector(sh, st, vec, c, i, xhat).then_inc(xhat_ready.sem, 1)
                    vec.wait_ge(elu_in.sem, elu_in.now(i))
                    vec.wait_ge(summed.sem, summed.last(i))
                    vec.scalar_tensor_tensor(f[:], QK[:], 0.0, e[:], ALU.max, ALU.add).then_inc(f_ready.sem, 1)
                    vec.wait_ge(f_ready.sem, f_ready.now(i))
                    for r in range(4):
                        ins = vec.tensor_scalar(q_h[:, r, :], f[:, 0:T], sh.c("head_rows")[:, r:r + 1], None, ALU.mult)
                    ins.then_inc(q_ready.sem, 1)
                    for u in range(4):
                        vec.wait_ge(scored.sem, scored.now(i, u + 1))
                        if u < 2:
                            vec.wait_ge(summed.sem, summed.last(i, u + 3))
                        else:
                            vec.wait_ge(summed.sem, summed.now(i, u - 1))
                        vec.tensor_tensor(A[:, u % 2, :].rearrange("p (b t) -> p b t", b=8),
                                          S[:, 1024 * (u % 2):1024 * (u % 2) + 1024].rearrange("p (b t) -> p b t", b=8),
                                          sh.c("upto_f").unsqueeze(1).broadcast_to([P, 8, P]), ALU.mult).then_inc(masked.sem, 1)
                        if u == 1:
                            vec.wait_ge(state_ps.sem, state_ps.now(i))
                            vec.tensor_tensor(state[:], QK[:, 0:144].rearrange("p (h d) -> p h d", h=NH),
                                              sh.c("own_head").unsqueeze(2).broadcast_to([P, NH, HS + 1]), ALU.mult).then_inc(state_sb.sem, 1)
                    vec.wait_ge(summed.sem, summed.now(i))
                    o = O[:, 0:288].rearrange("p (a h d) -> p a h d", a=2, h=NH)
                    c.link(vec.tensor_scalar(den[:], o[:, :, :, HS], EPS, None, ALU.add))
                    c.link(vec.reciprocal(den[:], den[:]))
                    vec.wait_ge(yT_ps.sem, yT_ps.last(i))
                    for k in range(2):
                        ins = vec.tensor_tensor(y[:, k], o[:, k, :, 0:HS], den[:, k].unsqueeze(2).broadcast_to([P, NH, HS]), ALU.mult)
                    ins.then_inc(y_ready.sem, 1)
                    vec.wait_ge(out_ps.sem, out_ps.now(i))
                    residual(sh, vec, c, i, Y[:, 0:T].rearrange("p (a b) -> p a b", a=2), out_read)


def linear_attention_large(sh, w):
    nc, NH, HS, NS = sh.nc, 16, 64, sh.seqs
    NU = NH // 2
    EPS = 1e-6
    V1 = HS + 1
    with Stage(nc, "large") as st:
        wqp, wkp = st.sb("wqp", [P, NH * HS]), st.sb("wkp", [P, NH * HS])
        xhat, xT = st.sb("xhat", [P, 2, P]), st.sb("xT", [P, T])
        e, neg, f = st.sb("e", [P, 2, 2 * T]), st.sb("neg", [P, 2, 2 * T]), st.sb("f", [P, 2, 2 * T])
        v1 = st.sb("v1", [P, 2, NH, V1])
        A, mask3 = st.sb("A", [P, 2, 2, 3 * P]), st.sb("mask3", [P, 3, P])
        den, y, yT = st.sb("den", [P, 2, 4]), st.sb("y", [P, 2, 2, 2, HS]), st.sb("yT", [P, 2, T])
        S = st.ps("scores", 2048)
        QK, O, YT, Y = (st.ps(n, 512) for n in ("qk_ps", "o_ps", "yT_ps", "y_ps"))

        ch = st.chain()
        ready = st.semaphore("ready", 1)
        prep, prep_sb = st.semaphore("prep", 1), st.semaphore("prep_sb", 1)
        xhat_ready = st.semaphore("xhat_ready", 1)
        xT_ps, xT_sb = st.semaphore("xT_ps", 1, True), st.semaphore("xT_sb", 1, True)
        v_ps, v_sb = st.semaphore("v_ps", 4), st.semaphore("v_sb", 4, True)
        qk_ps = st.semaphore("qk_ps", NU, True)
        neg_ready = st.semaphore("neg_ready", NU)
        elu_in, f_ready = st.semaphore("elu_in", NU), st.semaphore("f_ready", NU, True)
        scored, masked, summed = st.semaphore("scored", NU, True), st.semaphore("masked", NU, True), st.semaphore("summed", NU, True)
        y_ready, turned, turned_sb = st.semaphore("y_ready", NU, True), st.semaphore("turned", NU, True), st.semaphore("turned_sb", NU, True)
        projected = st.semaphore("projected", NU, True)
        out_read = st.semaphore("out_read", 1, True)

        with nc.Block() as block:
            def prev(eng, sig, i, m):
                if m > 0:
                    eng.wait_ge(sig.sem, sig.now(i, m))
                else:
                    eng.wait_ge(sig.sem, sig.last(i, m + sig.per))

            @block.gpsimd
            def _(pool):
                st.give_credits(pool)
                pool.memset(v1[:, :, :, HS:V1], 1.0)
                pool.memset(mask3[:, 1, :], 1.0)
                pool.tensor_copy(mask3[:, 0, :], sh.c("upto_f"))
                pool.tensor_copy(mask3[:, 2, :], sh.c("upto_f")).then_inc(ready.sem, 1)

            @block.tensor
            def _(pe):
                def mm(out, lhsT, rhs, start=True, stop=True, **k):
                    return pe.matmul(out, lhsT, rhs, start=start, stop=stop, **k)

                for n, wt in enumerate((w["E_wqT"], w["E_wkT"])):
                    for h in range(NH):
                        ins = mm(S[:, 1024 * n + HS * h:1024 * n + HS * h + HS], wt[:, P * h:P * h + P], w["E_proj"])
                ins.then_inc(prep.sem, 1)
                pe.wait_ge(prep_sb.sem, 1)
                pe.wait_ge(ready.sem, 1)
                with pe.Fori(0, NS) as i:
                    pe.wait_ge(xhat_ready.sem, xhat_ready.now(i))
                    prev(pe, turned_sb, i, 0)
                    for k in range(2):
                        ins = pe.transpose(YT[:, 128 * k:128 * k + 128], xhat[:, k, :], sh.c("ident"))
                    ins.then_inc(xT_ps.sem, 1)
                    pe.wait_ge(xT_sb.sem, xT_sb.now(i))
                    prev(pe, y_ready, i, 0)

                    def project(p):
                        prev(pe, f_ready, i, p)
                        mm(QK[:, 0:T], wqp[:, P * p:P * p + P], xT[:])
                        mm(QK[:, T:2 * T], wkp[:, P * p:P * p + P], xT[:]).then_inc(qk_ps.sem, 1)

                    def values_of(n):
                        if n >= 2:
                            pe.wait_ge(v_sb.sem, v_sb.now(i, n - 1))
                        mm((O, YT)[n % 2][:], xT[:, 128 * (n // 2):128 * (n // 2) + 128], w["E_wv"][:, 512 * (n % 2):512 * (n % 2) + 512]).then_inc(v_ps.sem, 1)

                    def scores(p):
                        pe.wait_ge(f_ready.sem, f_ready.now(i, p + 1))
                        prev(pe, masked, i, p - 1)
                        for a in range(2):
                            b, r = 1024 * (p % 2) + 512 * a, slice(64 * a, 64 * a + 64)
                            mm(S[:, b:b + 256], f[r, p % 2, T:T + 128], f[r, p % 2, 0:T])
                            ins = mm(S[:, b + 256:b + 384], f[r, p % 2, T + 128:2 * T], f[r, p % 2, 128:T])
                        ins.then_inc(scored.sem, 1)

                    def values(p):
                        pe.wait_ge(masked.sem, masked.now(i, p + 1))
                        if p == 0:
                            pe.wait_ge(v_sb.sem, v_sb.now(i))
                        prev(pe, y_ready, i, p)
                        for a in range(2):
                            h = 2 * p + a
                            mm(O[:, V1 * a:V1 * a + V1], A[:, p % 2, a, 0:128], v1[:, 0, h, :])
                            o = O[:, V1 * (2 + a):V1 * (2 + a) + V1]
                            mm(o, A[:, p % 2, a, 128:256], v1[:, 0, h, :], stop=False)
                            ins = mm(o, A[:, p % 2, a, 256:384], v1[:, 1, h, :], start=False)
                        ins.then_inc(summed.sem, 1)

                    def turn(p):
                        pe.wait_ge(y_ready.sem, y_ready.now(i, p + 1))
                        if p == 0:
                            pe.wait_ge(v_sb.sem, v_sb.now(i))
                        prev(pe, turned_sb, i, p)
                        for k in range(2):
                            ins = pe.transpose(YT[:, 128 * k:128 * k + 128], y[:, p % 2, k].rearrange("p a d -> p (a d)"), sh.c("ident"))
                        ins.then_inc(turned.sem, 1)

                    def out_of(p):
                        pe.wait_ge(turned_sb.sem, turned_sb.now(i, p + 1))
                        if p == 0:
                            pe.wait_ge(out_read.sem, out_read.last(i))
                        for k in range(2):
                            ins = mm(Y[:, 128 * k:128 * k + 128], yT[:, p % 2, 128 * k:128 * k + 128], w["E_wo"][:, P * p:P * p + P],
                                     start=(p == 0 and k == 0), stop=(p == NU - 1), skip_group_check=True)
                        ins.then_inc(projected.sem, 1)

                    project(0)
                    for n in range(4):
                        values_of(n)
                    for p in range(NU + 3):
                        if p + 1 < NU:
                            project(p + 1)
                        if p < NU:
                            scores(p)
                        if 1 <= p <= NU:
                            values(p - 1)
                        if 2 <= p <= NU + 1:
                            turn(p - 2)
                        if 3 <= p <= NU + 2:
                            out_of(p - 3)

            @block.scalar
            def _(act):
                act.wait_ge(prep.sem, 1)
                act.copy(wqp[:], S[:, 0:1024])
                act.copy(wkp[:], S[:, 1024:2048]).then_inc(prep_sb.sem, 1)
                with act.Fori(0, NS) as i:
                    act.wait_ge(xT_ps.sem, xT_ps.now(i))
                    act.wait_ge(qk_ps.sem, qk_ps.last(i))
                    act.copy(xT[:], YT[:, 0:T]).then_inc(xT_sb.sem, 1)

                    def elu_inputs(p):
                        act.wait_ge(qk_ps.sem, qk_ps.now(i, p + 1))
                        prev(act, f_ready, i, p - 1)
                        act.activation(neg[:, p % 2, :], QK[:], ACT.Relu, scale=-1.0).then_inc(neg_ready.sem, 1)
                        act.wait_ge(neg_ready.sem, neg_ready.now(i, p + 1))
                        act.activation(e[:, p % 2, :], neg[:, p % 2, :], ACT.Exp, scale=-1.0).then_inc(elu_in.sem, 1)

                    def turned_copy(p):
                        act.wait_ge(turned.sem, turned.now(i, p + 1))
                        prev(act, projected, i, p - 1)
                        act.copy(yT[:, p % 2, :], YT[:, 0:T]).then_inc(turned_sb.sem, 1)

                    elu_inputs(0)
                    act.wait_ge(summed.sem, summed.last(i))
                    for n in range(4):
                        act.wait_ge(v_ps.sem, v_ps.now(i, n + 1))
                        act.copy(v1[:, n // 2, 8 * (n % 2):8 * (n % 2) + 8, 0:HS], (O, YT)[n % 2][:].rearrange("p (h d) -> p h d", h=8)).then_inc(v_sb.sem, 1)
                    for p in range(NU + 2):
                        if p + 1 < NU:
                            elu_inputs(p + 1)
                        if p >= 2:
                            turned_copy(p - 2)

            @block.vector
            def _(vec):
                c = Chain(vec, ch)
                with vec.Fori(0, NS) as i:
                    c.restart()
                    vec.wait_ge(out_read.sem, out_read.last(i))
                    vec.wait_ge(xT_ps.sem, xT_ps.last(i))
                    front_vector(sh, st, vec, c, i, xhat).then_inc(xhat_ready.sem, 1)

                    def features(p):
                        vec.wait_ge(elu_in.sem, elu_in.now(i, p + 1))
                        prev(vec, scored, i, p - 1)
                        vec.scalar_tensor_tensor(f[:, p % 2, :], QK[:], 0.0, e[:, p % 2, :], ALU.max, ALU.add).then_inc(f_ready.sem, 1)

                    def mask(p):
                        vec.wait_ge(scored.sem, scored.now(i, p + 1))
                        prev(vec, summed, i, p - 1)
                        vec.tensor_tensor(A[:, p % 2].rearrange("p a (b t) -> p a b t", b=3),
                                          S[:, 1024 * (p % 2):1024 * (p % 2) + 1024].rearrange("p (a b t) -> p a b t", a=2, b=4)[:, :, 0:3, :],
                                          mask3[:].unsqueeze(1).broadcast_to([P, 2, 3, P]), ALU.mult).then_inc(masked.sem, 1)

                    def normalise(p):
                        vec.wait_ge(summed.sem, summed.now(i, p + 1))
                        o = O[:, 0:4 * V1].rearrange("p (b d) -> p b d", b=4)
                        c.link(vec.tensor_scalar(den[:, p % 2, :], o[:, :, HS], EPS, None, ALU.add))
                        c.link(vec.reciprocal(den[:, p % 2, :], den[:, p % 2, :]))
                        prev(vec, turned, i, p - 1)
                        vec.tensor_tensor(y[:, p % 2].rearrange("p k a d -> p (k a) d"), o[:, :, 0:HS],
                                          den[:, p % 2, :].unsqueeze(2).broadcast_to([P, 4, HS]), ALU.mult).then_inc(y_ready.sem, 1)

                    features(0)
                    for p in range(NU + 1):
                        if p + 1 < NU:
                            features(p + 1)
                        if p < NU:
                            mask(p)
                        if p >= 1:
                            normalise(p - 1)
                    vec.wait_ge(projected.sem, projected.now(i))
                    residual(sh, vec, c, i, Y[:, 0:T].rearrange("p (a b) -> p a b", a=2), out_read)


def expert_choice_ffn(sh, w, name):
    nc, NE, NS = sh.nc, 8, sh.seqs
    KEEP = 2 * T // NE
    HC = 4
    turns = NS // 2
    rows = min(16, NS) * NE
    groups = NS * NE // rows
    per_group = rows // NE
    with ExitStack() as ctx:
        p_all = ctx.enter_context(nc.sbuf_tensor(f"{name}_p_all", [P, sh.tiles, NE], F32))
        slot_all = ctx.enter_context(nc.sbuf_tensor(f"{name}_slot_all", [P, sh.tiles, NE], F32))
        gate(sh, name + "_gate", w["F_gate"], p_all, None)
        softmax8(sh, name + "_probs", p_all)

        with Stage(nc, name + "_pick") as st:
            pT = st.sb("pT", [rows, groups, T])
            best = st.sb("best", [rows, groups, KEEP])
            slots, one = st.sb("slots", [rows, groups, T]), st.sb("one", [rows, T])
            PT, ST = st.ps("pT_ps", groups * T), st.ps("slots_ps", 1024)
            pk = st.sb("pk", [P, 2, NS * NE])
            ch, split = st.chain(), st.semaphore("split", 1)
            turned, turned_sb = st.semaphore("turned", 1), st.semaphore("turned_sb", 1)
            placed, back = st.semaphore("placed", 1), st.semaphore("back", 1)

            def by_tile(a, g, k):
                v = a[:].rearrange("p (s k) e -> p s k e", k=2)
                return v[:, g * per_group:(g + 1) * per_group, k, :]

            with nc.Block() as block:
                @block.tensor
                def _(pe):
                    pe.wait_ge(split.sem, 1)
                    for g in range(groups):
                        for k in range(2):
                            c0 = g * T + 128 * k
                            ins = pe.transpose(PT[0:rows, c0:c0 + 128], pk[:, k, g * rows:(g + 1) * rows], sh.c("ident"))
                    ins.then_inc(turned.sem, 1)
                    pe.wait_ge(placed.sem, 1)
                    for g in range(groups):
                        for k in range(2):
                            c0 = (2 * g + k) * rows
                            ins = pe.transpose(ST[:, c0:c0 + rows], slots[:, g, 128 * k:128 * k + 128], sh.c("ident")[0:rows, 0:rows])
                    ins.then_inc(back.sem, 1)

                @block.scalar
                def _(act):
                    act.wait_ge(turned.sem, 1)
                    act.copy(pT[:].rearrange("p g t -> p (g t)"), PT[0:rows, :]).then_inc(turned_sb.sem, 1)

                @block.vector
                def _(vec):
                    c = Chain(vec, ch)
                    vec.memset(one[:], 1.0)
                    vec.tensor_copy(pk[:].rearrange("p k (s e) -> p s k e", e=NE), p_all[:].rearrange("p (s k) e -> p s k e", k=2)).then_inc(split.sem, 1)
                    vec.wait_ge(turned_sb.sem, 1)
                    for r in range(KEEP // 8):
                        for g in range(groups):
                            m = c.mark(vec.max(best[:, g, 8 * r:8 * r + 8], pT[:, g, :]))
                        for g in range(groups):
                            c.need(m - groups + 1 + g)
                            m2 = c.mark(vec.match_replace(pT[:, g, :], best[:, g, 8 * r:8 * r + 8], pT[:, g, :], -1.0))
                        c.need(m2)
                    c.link(vec.tensor_scalar(pT[:], pT[:], 0.0, None, ALU.is_lt))
                    for g in range(groups):
                        m = c.mark(vec.tensor_tensor_scan(slots[:, g, :], one[:], pT[:, g, :], 0.0, ALU.mult, ALU.add))
                    c.need(m)
                    vec.tensor_tensor(slots[:], slots[:], pT[:], ALU.mult).then_inc(placed.sem, 1)
                    vec.wait_ge(back.sem, 1)
                    for g in range(groups):
                        for k in range(2):
                            c0 = (2 * g + k) * rows
                            vec.tensor_copy(by_tile(slot_all, g, k), ST[:, c0:c0 + rows].rearrange("p (s e) -> p s e", e=NE))

        with Stage(nc, name) as st:
            xhat = st.sb("xhat", [P, 4, P])
            sel, selp = st.sb("sel", [P, 4, NE, KEEP]), st.sb("selp", [P, 2, NE, 2, KEEP])
            xin = st.sb("xin", [P, 2, NE, KEEP])
            selT, h = st.sb("selT", [P, 3, T]), st.sb("h", [P, 2, HC * P])
            yd = st.sb("yd", [P, 3, D])
            ob = st.sb("ob", [P, 4, D], BF16)
            G, TR = st.ps("gather_ps", 512), st.ps("selT_ps", 512)
            H = [st.ps("h0_ps", 512), st.ps("h1_ps", 512)]
            Y = [st.ps("y0_ps", 512), st.ps("y1_ps", 512)]
            O = [st.ps("o0_ps", 512), st.ps("o1_ps", 512)]
            ch = st.chain()
            sel_ready, selp_ready = st.semaphore("sel_ready", 1), st.semaphore("selp_ready", 1)
            gathered, gathered_sb = st.semaphore("gathered", 2, True), st.semaphore("gathered_sb", 2, True)
            up, gelu_done = st.semaphore("up", NE, True), st.semaphore("gelu_done", NE, True)
            down, down_sb = st.semaphore("down", NE, True), st.semaphore("down_sb", NE, True)
            turned, turned_sb = st.semaphore("turned", NE, True), st.semaphore("turned_sb", NE, True)
            scattered = st.semaphore("scattered", NE, True)
            rounded, out_read = st.semaphore("rounded", 1, True), st.semaphore("out_read", 1, True)

            def prev(eng, sig, i, m):
                if m > 0:
                    eng.wait_ge(sig.sem, sig.now(i, m))
                else:
                    eng.wait_ge(sig.sem, sig.last(i, m + sig.per))

            with nc.Block() as block:

                @block.gpsimd
                def _(pool):
                    st.give_credits(pool)

                @block.tensor
                def _(pe):
                    with pe.Fori(0, turns) as i:
                        pe.wait_ge(sel_ready.sem, sel_ready.now(i))
                        for s in range(2):
                            prev(pe, gathered_sb, i, s)
                            for k in range(2):
                                ins = pe.matmul(G[:], xhat[:, 2 * s + k, :], sel[:, 2 * s + k].rearrange("p e c -> p (e c)"),
                                                start=(k == 0), stop=(k == 1))
                            ins.then_inc(gathered.sem, 1)
                        pe.wait_ge(gathered_sb.sem, gathered_sb.now(i))
                        pe.wait_ge(selp_ready.sem, selp_ready.now(i))

                        def expand(e):
                            prev(pe, gelu_done, i, e - 1)
                            for m in range(HC):
                                w0 = (e * HC + m) * P
                                ins = pe.matmul(H[e % 2][:, P * m:P * m + P], w["F_w1"][:, w0:w0 + P], xin[:, :, e, :], start=True, stop=True)
                            ins.then_inc(up.sem, 1)

                        def turn(e):
                            prev(pe, turned_sb, i, e)
                            for k in range(2):
                                ins = pe.transpose(TR[:, P * k:P * k + P], selp[:, k, e].rearrange("p s c -> p (s c)"), sh.c("ident"))
                            ins.then_inc(turned.sem, 1)

                        def contract(e):
                            pe.wait_ge(gelu_done.sem, gelu_done.now(i, e + 1))
                            prev(pe, down_sb, i, e - 1)
                            for m in range(HC):
                                w0 = (e * HC + m) * P
                                ins = pe.matmul(Y[e % 2][:, 0:D], h[:, e % 2, P * m:P * m + P], w["F_w2"][:, w0:w0 + P], start=(m == 0), stop=(m == HC - 1))
                            ins.then_inc(down.sem, 1)

                        def scatter(e):
                            pe.wait_ge(down_sb.sem, down_sb.now(i, e + 1))
                            pe.wait_ge(turned_sb.sem, turned_sb.now(i, e + 1))
                            if e == 0:
                                pe.wait_ge(rounded.sem, rounded.last(i))
                            for k in range(2):
                                for s in range(2):
                                    r = slice(64 * s, 64 * s + 64)
                                    ins = pe.matmul(O[s][:, P * k:P * k + P], selT[r, e % 3, P * k:P * k + P], yd[r, e % 3, :],
                                                    start=(e == 0 and k == 0), stop=(e == NE - 1), skip_group_check=True)
                            ins.then_inc(scattered.sem, 1)

                        for e in range(NE + 2):
                            if e < NE:
                                expand(e)
                                turn(e)
                            if 1 <= e <= NE:
                                contract(e - 1)
                            if e >= 2:
                                scatter(e - 2)

                @block.scalar
                def _(act):
                    with act.Fori(0, turns) as i:
                        for s in range(2):
                            act.wait_ge(gathered.sem, gathered.now(i, s + 1))
                            act.wait_ge(up.sem, up.last(i))
                            act.copy(xin[:, s].rearrange("p e c -> p (e c)"), G[:]).then_inc(gathered_sb.sem, 1)
                        for e in range(NE):
                            act.wait_ge(up.sem, up.now(i, e + 1))
                            prev(act, down, i, e - 1)
                            act.activation(h[:, e % 2, :], H[e % 2][:], ACT.Gelu_apprx_tanh).then_inc(gelu_done.sem, 1)
                        act.wait_ge(scattered.sem, scattered.now(i))
                        act.wait_ge(out_read.sem, out_read.last(i))
                        act.copy(ob[:, 0:2, :].rearrange("p k d -> p (k d)"), O[0][:, 0:T])
                        act.copy(ob[:, 2:4, :].rearrange("p k d -> p (k d)"), O[1][:, 0:T]).then_inc(rounded.sem, 1)

                @block.vector
                def _(vec):
                    c = Chain(vec, ch)
                    with vec.Fori(0, turns) as i:
                        c.restart()
                        vec.wait_ge(out_read.sem, out_read.last(i))
                        vec.wait_ge(gathered.sem, gathered.last(i))
                        for k in range(4):
                            t = 4 * i + k
                            vec.tensor_scalar(xhat[:, k, :], sh.x[:, bass.ds(t, 1), :], sh.mean[:, bass.ds(t, 1)],
                                              sh.rstd[:, bass.ds(t, 1)], ALU.subtract, ALU.mult)
                        for k in range(4):
                            ins = vec.tensor_tensor(sel[:, k], sh.c("iota").unsqueeze(1).broadcast_to([P, NE, KEEP]),
                                                    slot_all[:, bass.ds(4 * i + k, 1), :].rearrange("p a e -> p (a e)").unsqueeze(2).broadcast_to([P, NE, KEEP]), ALU.is_equal)
                        ins.then_inc(sel_ready.sem, 1)
                        vec.wait_ge(sel_ready.sem, sel_ready.now(i))
                        vec.wait_ge(turned.sem, turned.last(i))
                        for k in range(4):
                            ins = vec.tensor_tensor(selp[:, k % 2, :, k // 2, :], sel[:, k],
                                                    p_all[:, bass.ds(4 * i + k, 1), :].rearrange("p a e -> p (a e)").unsqueeze(2).broadcast_to([P, NE, KEEP]), ALU.mult)
                        ins.then_inc(selp_ready.sem, 1)
                        for e in range(NE + 1):
                            if e < NE:
                                vec.wait_ge(turned.sem, turned.now(i, e + 1))
                                prev(vec, scattered, i, e - 2)
                                vec.tensor_copy(selT[:, e % 3, :], TR[:, 0:T]).then_inc(turned_sb.sem, 1)
                            if e:
                                vec.wait_ge(down.sem, down.now(i, e))
                                prev(vec, scattered, i, e - 3)
                                vec.tensor_copy(yd[:, (e - 1) % 3, :], Y[(e - 1) % 2][:, 0:D]).then_inc(down_sb.sem, 1)
                        vec.wait_ge(rounded.sem, rounded.now(i))
                        for s in range(2):
                            residual(sh, vec, c, 2 * i + s, ob[:, 2 * s:2 * s + 2, :], out_read if s else None)


def expert_choice_ffn_first(sh, w):
    expert_choice_ffn(sh, w, "ffn_f")


def expert_choice_ffn_second(sh, w):
    expert_choice_ffn(sh, w, "ffn_h")


def delta_rule_mixer(sh, w):
    nc, NH, HS, NS = sh.nc, 4, 32, sh.seqs
    TAPS, LOCAL, MID = 4, 7, 25
    NF, RH = 14 * NH, 2 * (D + 14 * NH)
    NFW = 80
    FLOOR, EPS = 0.01, 1e-5
    RC = [(0, 128), (128, 256), (256, RH)]
    LEVELS = (2, 4, 8, 16)
    with Stage(nc, "delta") as st:
        sb = st.sb
        wtap = sb("wtap", [P, 3, TAPS, P])
        diag = sb("diag", [P, MID, P])
        xhat, xT = sb("xhat", [P, 2, P]), sb("xT", [P, TAPS - 1 + T])
        qk_f, v_f = sb("qk_f", [P, 2 * T]), sb("v_f", [P, MID - 1 + T])
        beta = sb("beta", [P, 2, NH])
        loc_f, mid_f = sb("loc_f", [P, T]), sb("mid_f", [P, T])
        qk_t, sq = sb("qk_t", [P, 2, 2, P]), sb("sq", [P, 2, 2, P])
        ss, rn, half = sb("ss", [P, 16]), sb("rn", [P, 16]), sb("half", [P, 16])
        nkb, vb = sb("nkb", [P, 2, P]), sb("vb", [P, 2, P])
        qkn_T = sb("qkn_T", [P, 3, T])
        A, At = sb("A", [P, 2, 4 * P]), sb("At", [P, 2, 4 * P])
        Tm, Um, Q, Wt = sb("Tm", [P, 8 * P]), sb("Um", [P, 8 * P]), sb("Q", [P, 8 * P]), sb("Wt", [P, 8 * P])
        r, u = sb("r", [P, P]), sb("u", [P, 2, 4, P])
        S = sb("S", [P, P])
        outs, sqo = sb("outs", [P, 2, 4, P]), sb("sqo", [P, 2, 4, P])
        prod = sb("prod", [P, 2, 6, P])
        feats, mm2 = sb("feats", [P, 2, NFW]), sb("mm2", [P, 2, 16])
        featsT, h1 = sb("featsT", [NF, T]), sb("h1", [P, 3, T])
        lg, lm = sb("lg", [P, 2, NH, 4]), sb("lm", [P, 2, NH])
        mixed, sqm = sb("mixed", [P, 2, P]), sb("sqm", [P, 2, P])
        rm, rr = sb("rm", [P, 2, NH]), sb("rr", [P, 2, NH])
        oT = sb("oT", [P, T])
        B = [st.ps(f"bank{n}", 512) for n in range(8)]

        sig = st.semaphore
        ch = st.chain()
        prep, prep_sb, ready = sig("prep", 1), sig("prep_sb", 1), sig("ready", 1)
        out_read = sig("out_read", 1, True)
        xhat_ready, xT_ps, xT_sb = sig("xhat_ready", 1), sig("xT_ps", 1), sig("xT_sb", 1)
        qk_ps, v_ps, qk_sb, v_sb, beta_sb = (sig(n, 1) for n in ("qk_ps", "v_ps", "qk_sb", "v_sb", "beta_sb"))
        mid_ps, mid_sb, loc_sb = sig("mid_ps", 1), sig("mid_sb", 1), sig("loc_sb", 1)
        qk_turned, v_turned, mid_turned = sig("qk_turned", 1), sig("v_turned", 1), sig("mid_turned", 1)
        qkt_sb, v_t_sb, conv_sb = sig("qkt_sb", 1), sig("v_t_sb", 1), sig("conv_sb", 1)
        ss_ready, rn_ready = sig("ss_ready", 1), sig("rn_ready", 1)
        normed, normed_ps, normed_sb = sig("normed", 1), sig("normed_ps", 1), sig("normed_sb", 1)
        gram, gram_read = sig("gram", 2), sig("gram_read", 2)
        q_ps, q_sb, tu_ps, tu_sb = sig("q_ps", 5), sig("q_sb", 5), sig("tu_ps", 4), sig("tu_sb", 4)
        first_tu = sig("first_tu", 1)
        r_ready = sig("r_ready", 2)
        z_ps, z_sb = sig("z_ps", 8), sig("z_sb", 8)
        s_ps, s_sb, ks_ps = sig("s_ps", 1), sig("s_sb", 1), sig("ks_ps", 1)
        o_ps, o_sb = sig("o_ps", 1), sig("o_sb", 1)
        squared = sig("squared", 1)
        feats_ready, featsT_ps, featsT_sb = sig("feats_ready", 1), sig("featsT_ps", 1), sig("featsT_sb", 1)
        h1_ps, h1_sb = sig("h1_ps", 2), sig("h1_sb", 1)
        lg_ps, lg_shifted, lg_exp = sig("lg_ps", 1), sig("lg_shifted", 1), sig("lg_exp", 1)
        ms_ready, mr_ready = sig("ms_ready", 2), sig("mr_ready", 2)
        on_ready, oT_ps, oT_sb, out_ps = (sig(n, 1) for n in ("on_ready", "oT_ps", "oT_sb", "out_ps"))

        def heads(ap, n=2):
            return ap.rearrange("p k (h d) -> p (k h) d", h=NH)

        def spread(ap, n, m):
            return ap.unsqueeze(2).broadcast_to([P, n, m])

        with nc.Block() as block:

            @block.gpsimd
            def _(pool):
                st.give_credits(pool)
                pool.memset(half[:], -0.5)
                pool.memset(feats[:], 0.0)
                pool.memset(xT[:, 0:TAPS - 1], 0.0)
                pool.memset(v_f[:, 0:MID - 1], 0.0).then_inc(ready.sem, 1)
                pool.wait_ge(ready.sem, 1)
                with pool.Fori(0, NS) as i:
                    pool.wait_ge(ss_ready.sem, ss_ready.now(i))
                    pool.tensor_tensor(rn[:], ss[:], half[:], ALU.pow).then_inc(rn_ready.sem, 1)
                    for n in range(2):
                        pool.wait_ge(ms_ready.sem, ms_ready.now(i, n + 1))
                        pool.tensor_tensor(rr[:].rearrange("p k h -> p (k h)"), rm[:].rearrange("p k h -> p (k h)"), half[:, 0:8], ALU.pow).then_inc(mr_ready.sem, 1)

            @block.tensor
            def _(pe):
                def mm(out, lhsT, rhs, start=True, stop=True, **k):
                    return pe.matmul(out, lhsT, rhs, start=start, stop=stop, **k)

                ident = sh.c("ident")
                for n in range(3):
                    for tau in range(TAPS):
                        ins = pe.transpose(B[n][:, P * tau:P * tau + P], w["G_conv"][:, TAPS * n + tau:TAPS * n + tau + 1].broadcast_to([P, P]), ident)
                ins.then_inc(prep.sem, 1)
                pe.wait_ge(prep_sb.sem, 1)
                pe.wait_ge(ready.sem, 1)
                with pe.Fori(0, NS) as i:
                    pe.wait_ge(out_read.sem, out_read.last(i))
                    pe.wait_ge(xhat_ready.sem, xhat_ready.now(i))
                    for k in range(2):
                        ins = pe.transpose(B[0][:, P * k:P * k + P], xhat[:, k, :], ident)
                    ins.then_inc(xT_ps.sem, 1)
                    pe.wait_ge(xT_sb.sem, xT_sb.now(i))
                    for n, (b, c0) in ((2, (2, 0)), (0, (1, 0)), (1, (1, T))):
                        for tau in range(TAPS):
                            ins = mm(B[b][:, c0:c0 + T], wtap[:, n, tau, :], xT[:, tau:tau + T], start=(tau == 0), stop=(tau == TAPS - 1))
                        if n == 2:
                            for k in range(2):
                                t0 = TAPS - 1 + P * k
                                ins = mm(B[2][:, T + NH * k:T + NH * k + NH], xT[:, t0:t0 + P], w["G_wb"])
                            ins.then_inc(v_ps.sem, 1)
                    ins.then_inc(qk_ps.sem, 1)
                    pe.wait_ge(v_sb.sem, v_sb.now(i))
                    for tau in range(MID):
                        ins = mm(B[0][:, 0:T], diag[:, tau, :], v_f[:, tau:tau + T], start=(tau == 0), stop=(tau == MID - 1))
                    ins.then_inc(mid_ps.sem, 1)
                    pe.wait_ge(qk_sb.sem, qk_sb.now(i))
                    for n in range(4):
                        ins = pe.transpose(B[3][:, P * n:P * n + P], qk_f[:, P * n:P * n + P], ident)
                    ins.then_inc(qk_turned.sem, 1)
                    pe.wait_ge(loc_sb.sem, loc_sb.now(i))
                    for k in range(2):
                        pe.transpose(B[4][:, P * k:P * k + P], v_f[:, MID - 1 + P * k:MID - 1 + P * k + P], ident)
                        ins = pe.transpose(B[4][:, T + P * k:T + P * k + P], loc_f[:, P * k:P * k + P], ident)
                    ins.then_inc(v_turned.sem, 1)
                    pe.wait_ge(mid_sb.sem, mid_sb.now(i))
                    for k in range(2):
                        ins = pe.transpose(B[5][:, P * k:P * k + P], mid_f[:, P * k:P * k + P], ident)
                    ins.then_inc(mid_turned.sem, 1)
                    pe.wait_ge(normed.sem, normed.now(i))
                    pe.wait_ge(v_t_sb.sem, v_t_sb.now(i))
                    for n in range(2):
                        for k in range(2):
                            pe.transpose(B[3][:, T * n + P * k:T * n + P * k + P], qk_t[:, n, k, :], ident)
                    for k in range(2):
                        ins = pe.transpose(B[4][:, P * k:P * k + P], nkb[:, k, :], ident)
                    ins.then_inc(normed_ps.sem, 1)
                    pe.wait_ge(normed_sb.sem, normed_sb.now(i))
                    pe.wait_ge(conv_sb.sem, conv_sb.now(i))
                    for k in range(2):
                        if k:
                            pe.wait_ge(gram_read.sem, gram_read.now(i, 1))
                        for h in range(NH):
                            f = slice(HS * h, HS * h + HS)
                            q, kk, nk = (qkn_T[f, n, P * k:P * k + P] for n in range(3))
                            mm(B[3 + h][:, 0:P], nk, kk)
                            mm(B[3 + h][:, P:2 * P], kk, nk)
                            ins = mm(B[3 + h][:, 2 * P:3 * P], kk, q)
                        ins.then_inc(gram.sem, 1)
                    pe.wait_ge(gram_read.sem, gram_read.now(i))

                    def col(n):
                        return slice(P * n, P * n + P)

                    for lv in range(len(LEVELS) + 1):
                        if lv:
                            pe.wait_ge(tu_sb.sem, tu_sb.now(i, lv))
                        else:
                            pe.wait_ge(first_tu.sem, first_tu.now(i))
                        for n in range(8):
                            ins = mm(B[3 + n // 4][:, col(n % 4)], A[:, n // 4, col(n % 4)], Um[:, col(n)])
                        ins.then_inc(q_ps.sem, 1)
                        if lv < len(LEVELS):
                            pe.wait_ge(q_sb.sem, q_sb.now(i, lv + 1))
                            for n in range(8):
                                ins = mm(B[5 + n // 4][:, col(n % 4)], Tm[:, col(n)], Q[:, col(n)])
                            if lv < len(LEVELS) - 1:
                                for n in range(8):
                                    ins = mm(B[(7, 2)[n // 4]][:, col(n % 4)], Q[:, col(n)], Tm[:, col(n)])
                            ins.then_inc(tu_ps.sem, 1)
                    pe.wait_ge(q_sb.sem, q_sb.now(i, 5))
                    for k in range(2):
                        pe.wait_ge(r_ready.sem, r_ready.now(i, k + 1))
                        for s in range(4):
                            if s:
                                pe.wait_ge(z_sb.sem, z_sb.now(i, 4 * k + s))
                            for h in range(NH):
                                f = slice(HS * h, HS * h + HS)
                                ins = mm(B[1 + s % 2][:, f], (Wt if s else Um)[:, col(4 * k + h)], u[:, k, s - 1, f] if s else r[:, f])
                            ins.then_inc(z_ps.sem, 1)
                        pe.wait_ge(z_sb.sem, z_sb.now(i, 4 * k + 4))
                        if k == 0:
                            mm(B[1][:, 0:P], qk_t[:, 1, 0, :], u[:, 0, 3, :]).then_inc(s_ps.sem, 1)
                            pe.wait_ge(s_sb.sem, s_sb.now(i))
                            mm(B[2][:, 0:P], qkn_T[:, 2, P:2 * P], S[:]).then_inc(ks_ps.sem, 1)
                        for h in range(NH):
                            f = slice(HS * h, HS * h + HS)
                            ins = mm(B[5][:, P * k + HS * h:P * k + HS * h + HS], At[:, k, col(h)], u[:, k, 3, f], start=(h == 0), stop=(k == 0), skip_group_check=True)
                    mm(B[5][:, P:2 * P], qkn_T[:, 0, P:2 * P], S[:], start=False, skip_group_check=True).then_inc(o_ps.sem, 1)
                    pe.wait_ge(feats_ready.sem, feats_ready.now(i))
                    for k in range(2):
                        ins = pe.transpose(B[0][0:NFW, P * k:P * k + P], feats[:, k, :], ident)
                    ins.then_inc(featsT_ps.sem, 1)
                    pe.wait_ge(featsT_sb.sem, featsT_sb.now(i))
                    for n, (a, b) in enumerate(RC):
                        o = B[3 + n // 2][0:b - a, T * (n % 2):T * (n % 2) + T]
                        mm(o, w["G_rw1x"][:, a:b], xT[:, TAPS - 1:TAPS - 1 + T], stop=False)
                        ins = mm(o, w["G_rw1f"][:, a:b], featsT[:], start=False)
                        if n:
                            ins.then_inc(h1_ps.sem, 1)
                    pe.wait_ge(h1_sb.sem, h1_sb.now(i))
                    for k in range(2):
                        o = B[6][:, 16 * k:16 * k + 16]
                        for n, (a, b) in enumerate(RC):
                            mm(o, h1[0:b - a, n, P * k:P * k + P], w["G_rw2"][0:b - a, 16 * n:16 * n + 16], start=(n == 0), stop=False)
                        ins = mm(o, sh.c("ones128")[0:1, :], w["G_rb2"], start=False)
                    ins.then_inc(lg_ps.sem, 1)
                    pe.wait_ge(on_ready.sem, on_ready.now(i))
                    for k in range(2):
                        ins = pe.transpose(B[7][:, P * k:P * k + P], mixed[:, k, :], ident)
                    ins.then_inc(oT_ps.sem, 1)
                    pe.wait_ge(oT_sb.sem, oT_sb.now(i))
                    for k in range(2):
                        ins = mm(B[0][:, P * k:P * k + P], oT[:, P * k:P * k + P], w["G_wo"])
                    ins.then_inc(out_ps.sem, 1)

            @block.scalar
            def _(act):
                with act.Fori(0, NS) as i:
                    act.wait_ge(out_read.sem, out_read.last(i))
                    act.wait_ge(xT_ps.sem, xT_ps.now(i))
                    act.copy(xT[:, TAPS - 1:TAPS - 1 + T], B[0][:, 0:T]).then_inc(xT_sb.sem, 1)
                    act.wait_ge(v_ps.sem, v_ps.now(i))
                    act.activation(v_f[:, MID - 1:MID - 1 + T], B[2][:, 0:T], ACT.Silu).then_inc(v_sb.sem, 1)
                    act.wait_ge(qk_ps.sem, qk_ps.now(i))
                    act.activation(qk_f[:], B[1][:], ACT.Silu).then_inc(qk_sb.sem, 1)
                    act.activation(beta[:].rearrange("p k h -> p (k h)"), B[2][:, T:T + 2 * NH], ACT.Sigmoid).then_inc(beta_sb.sem, 1)
                    act.wait_ge(qk_turned.sem, qk_turned.now(i))
                    act.copy(qk_t[:].rearrange("p n k d -> p (n k d)"), B[3][:]).then_inc(qkt_sb.sem, 1)
                    act.wait_ge(v_turned.sem, v_turned.now(i))
                    act.copy(outs[:, :, 3, :], B[4][:, 0:T].rearrange("p (k d) -> p k d", k=2))
                    act.copy(outs[:, :, 0, :], B[4][:, T:2 * T].rearrange("p (k d) -> p k d", k=2)).then_inc(v_t_sb.sem, 1)
                    act.wait_ge(mid_ps.sem, mid_ps.now(i))
                    act.copy(mid_f[:], B[0][:, 0:T]).then_inc(mid_sb.sem, 1)
                    act.wait_ge(mid_turned.sem, mid_turned.now(i))
                    act.copy(outs[:, :, 1, :], B[5][:, 0:T].rearrange("p (k d) -> p k d", k=2)).then_inc(conv_sb.sem, 1)
                    act.wait_ge(normed_ps.sem, normed_ps.now(i))
                    act.copy(qkn_T[:, 0:2, :].rearrange("p n t -> p (n t)"), B[3][:])
                    act.copy(qkn_T[:, 2, :], B[4][:, 0:T]).then_inc(normed_sb.sem, 1)
                    act.wait_ge(o_ps.sem, o_ps.now(i))
                    act.copy(outs[:, :, 2, :], B[5][:, 0:T].rearrange("p (k d) -> p k d", k=2)).then_inc(o_sb.sem, 1)
                    act.wait_ge(o_sb.sem, o_sb.now(i))
                    act.activation(sqo[:].rearrange("p k n d -> p (k n d)"), outs[:].rearrange("p k n d -> p (k n d)"), ACT.Square).then_inc(squared.sem, 1)
                    act.wait_ge(featsT_ps.sem, featsT_ps.now(i))
                    act.copy(featsT[:], B[0][0:NF, 0:T]).then_inc(featsT_sb.sem, 1)
                    act.wait_ge(h1_ps.sem, h1_ps.now(i, 1))
                    for n, (a, b) in enumerate(RC):
                        if n == 2:
                            act.wait_ge(h1_ps.sem, h1_ps.now(i))
                        ins = act.activation(h1[0:b - a, n, :], B[3 + n // 2][0:b - a, T * (n % 2):T * (n % 2) + T], ACT.Silu, bias=w["G_rb1"][0:b - a, n:n + 1])
                    ins.then_inc(h1_sb.sem, 1)
                    act.wait_ge(lg_shifted.sem, lg_shifted.now(i))
                    act.activation(lg[:], lg[:], ACT.Exp).then_inc(lg_exp.sem, 1)
                    act.wait_ge(oT_ps.sem, oT_ps.now(i))
                    act.copy(oT[:], B[7][:, 0:T]).then_inc(oT_sb.sem, 1)

            @block.vector
            def _(vec):
                c = Chain(vec, ch)
                vec.wait_ge(prep.sem, 1)
                for n, name in enumerate(("G_wq", "G_wk", "G_wv")):
                    vec.tensor_tensor(wtap[:, n], B[n][:].rearrange("p (a c) -> p a c", a=TAPS),
                                      w[name].unsqueeze(1).broadcast_to([P, TAPS, P]), ALU.mult)
                for tau in range(MID):
                    ins = vec.tensor_scalar(diag[:, tau, :], sh.c("ident"), w["G_mid"][:, tau:tau + 1], None, ALU.mult)
                ins.then_inc(prep_sb.sem, 1)
                with vec.Fori(0, NS) as i:
                    c.restart()
                    vec.wait_ge(out_read.sem, out_read.last(i))
                    front_vector(sh, st, vec, c, i, xhat).then_inc(xhat_ready.sem, 1)
                    vec.wait_ge(v_sb.sem, v_sb.now(i))
                    s0 = MID - LOCAL
                    c.link(vec.tensor_scalar(loc_f[:], v_f[:, s0:s0 + T], w["G_local"][:, 0:1], None, ALU.mult))
                    for tau in range(1, LOCAL):
                        ins = vec.scalar_tensor_tensor(loc_f[:], v_f[:, s0 + tau:s0 + tau + T], w["G_local"][:, tau:tau + 1], loc_f[:], ALU.mult, ALU.add)
                        if tau < LOCAL - 1:
                            c.link(ins)
                    ins.then_inc(loc_sb.sem, 1)
                    vec.wait_ge(qkt_sb.sem, qkt_sb.now(i))
                    qkt = qk_t[:].rearrange("p n k (h d) -> p (n k h) d", h=NH)
                    c.link(vec.tensor_tensor(sq[:].rearrange("p n k d -> p (n k d)"), qk_t[:].rearrange("p n k d -> p (n k d)"),
                                             qk_t[:].rearrange("p n k d -> p (n k d)"), ALU.mult))
                    c.link(vec.tensor_reduce(ss[:], sq[:].rearrange("p n k (h d) -> p (n k h) d", h=NH), AX.X, ALU.add))
                    vec.tensor_scalar(ss[:], ss[:], 1e-12, None, ALU.add).then_inc(ss_ready.sem, 1)
                    vec.wait_ge(rn_ready.sem, rn_ready.now(i))
                    c.link(vec.tensor_tensor(qkt, qkt, spread(rn[:], 16, HS), ALU.mult))
                    vec.wait_ge(beta_sb.sem, beta_sb.now(i))
                    vec.scalar_tensor_tensor(heads(nkb[:]), heads(qk_t[:, 1]), -1.0, spread(beta[:].rearrange("p k h -> p (k h)"), 8, HS), ALU.mult, ALU.mult).then_inc(normed.sem, 1)
                    vec.wait_ge(v_t_sb.sem, v_t_sb.now(i))
                    for k in range(2):
                        ins = vec.tensor_tensor(vb[:, k].rearrange("p (h d) -> p h d", h=NH), outs[:, k, 3, :].rearrange("p (h d) -> p h d", h=NH), spread(beta[:, k], NH, HS), ALU.mult)
                    c.link(ins)
                    vec.tensor_copy(r[:], vb[:, 0, :]).then_inc(r_ready.sem, 1)

                    def four(ap):
                        return ap.rearrange("p (h t) -> p h t", h=NH)

                    def over(name, n=NH):
                        return sh.c(name).unsqueeze(1).broadcast_to([P, n, P])

                    for k in range(2):
                        vec.wait_ge(gram.sem, gram.now(i, k + 1))
                        Tk, Uk = Tm[:, 512 * k:512 * k + 512], Um[:, 512 * k:512 * k + 512]
                        for h in range(NH):
                            f = slice(P * h, P * h + P)
                            vec.tensor_tensor(A[:, k, f], B[3 + h][:, 0:P], sh.c("before"), ALU.mult)
                            vec.tensor_tensor(Um[:, 512 * k + P * h:512 * k + P * h + P], B[3 + h][:, P:2 * P], sh.c("mT1"), ALU.mult)
                            ins = vec.tensor_tensor(At[:, k, f], B[3 + h][:, 2 * P:3 * P], sh.c("upto_f"), ALU.mult)
                        ins.then_inc(gram_read.sem, 1)
                        if k == 0:
                            vec.wait_ge(gram_read.sem, gram_read.now(i, 1))
                        else:
                            vec.wait_ge(gram_read.sem, gram_read.now(i, 2))
                        vec.tensor_tensor(four(Uk), four(Uk), over("ident"), ALU.add)
                        c.link(vec.tensor_tensor(four(Tk), four(A[:, k, :]), over("m1"), ALU.mult))
                        m = c.mark(vec.tensor_tensor(four(Tk), four(Tk), over("ident"), ALU.add))
                    c.need(m)
                    vec.sem_inc(first_tu.sem, 1)
                    for lv, s in enumerate(LEVELS):
                        vec.wait_ge(q_ps.sem, q_ps.now(i, lv + 1))
                        for k in range(2):
                            ins = vec.tensor_tensor(four(Q[:, 512 * k:512 * k + 512]), four(B[3 + k][:]), over(f"mT{s}"), ALU.mult)
                        ins.then_inc(q_sb.sem, 1)
                        vec.wait_ge(tu_ps.sem, tu_ps.now(i, lv + 1))
                        for k in range(2):
                            f = slice(512 * k, 512 * k + 512)
                            ins = vec.tensor_tensor(Um[:, f], B[5 + k][:], Um[:, f], ALU.add)
                            if lv < len(LEVELS) - 1:
                                ins = vec.tensor_tensor(Tm[:, f], B[(7, 2)[k]][:], Tm[:, f], ALU.add)
                        ins.then_inc(tu_sb.sem, 1)
                        vec.wait_ge(tu_sb.sem, tu_sb.now(i, lv + 1))
                    vec.wait_ge(q_ps.sem, q_ps.now(i, 5))
                    for k in range(2):
                        ins = vec.tensor_tensor(four(Wt[:, 512 * k:512 * k + 512]), four(B[3 + k][:]), over("mT_off"), ALU.mult)
                    ins.then_inc(q_sb.sem, 1)
                    for k in range(2):
                        for s in range(4):
                            vec.wait_ge(z_ps.sem, z_ps.now(i, 4 * k + s + 1))
                            if s == 0:
                                ins = vec.tensor_copy(u[:, k, 0, :], B[1][:, 0:P])
                            else:
                                ins = vec.tensor_tensor(u[:, k, s, :], B[1 + s % 2][:, 0:P], u[:, k, 0, :], ALU.add)
                            ins.then_inc(z_sb.sem, 1)
                            if s == 0:
                                vec.wait_ge(z_sb.sem, z_sb.now(i, 4 * k + 1))
                        if k == 0:
                            vec.wait_ge(s_ps.sem, s_ps.now(i))
                            vec.tensor_tensor(S[:], B[1][:, 0:P], sh.c("same_head"), ALU.mult).then_inc(s_sb.sem, 1)
                            vec.wait_ge(ks_ps.sem, ks_ps.now(i))
                            vec.tensor_tensor(r[:], B[2][:, 0:P], vb[:, 1, :], ALU.add).then_inc(r_ready.sem, 1)
                    vec.wait_ge(o_sb.sem, o_sb.now(i))
                    for k in range(2):
                        c0 = 0
                        for a in range(3):
                            n = 3 - a
                            vec.tensor_tensor(prod[:, k, c0:c0 + n, :], outs[:, k, a + 1:4, :], outs[:, k, a:a + 1, :].broadcast_to([P, n, P]), ALU.mult)
                            c0 += n
                        m = c.mark(vec.tensor_reduce(feats[:, k, 0:16], outs[:, k].rearrange("p n (h d) -> p (n h) d", h=NH), AX.X, ALU.add))
                    vec.wait_ge(squared.sem, squared.now(i))
                    c.need(m)
                    for k in range(2):
                        vec.tensor_reduce(feats[:, k, 16:32], sqo[:, k].rearrange("p n (h d) -> p (n h) d", h=NH), AX.X, ALU.add)
                        vec.tensor_reduce(feats[:, k, 32:56], prod[:, k].rearrange("p n (h d) -> p (n h) d", h=NH), AX.X, ALU.add)
                        m = c.mark(vec.scalar_tensor_tensor(mm2[:, k, :], feats[:, k, 0:16], 1.0 / HS, feats[:, k, 0:16], ALU.mult, ALU.mult))
                    c.need(m)
                    vec.tensor_scalar(feats[:, :, 0:16], feats[:, :, 0:16], 1.0 / HS, None, ALU.mult)
                    vec.tensor_scalar(feats[:, :, 32:56], feats[:, :, 32:56], 1.0 / HS, None, ALU.mult)
                    c.link(vec.tensor_tensor(feats[:, :, 16:32], feats[:, :, 16:32], mm2[:], ALU.subtract))
                    vec.tensor_scalar(feats[:, :, 16:32], feats[:, :, 16:32], 1.0 / (HS - 1), None, ALU.mult).then_inc(feats_ready.sem, 1)
                    vec.wait_ge(lg_ps.sem, lg_ps.now(i))
                    lps = B[6][:, 0:32].rearrange("p (n j) -> p n j", j=4)
                    lgv = lg[:].rearrange("p k h j -> p (k h) j")
                    lmv = lm[:].rearrange("p k h -> p (k h)")
                    c.link(vec.tensor_reduce(lmv, lps, AX.X, ALU.max))
                    vec.tensor_tensor(lgv, lps, spread(lmv, 8, 4), ALU.subtract).then_inc(lg_shifted.sem, 1)
                    vec.wait_ge(lg_exp.sem, lg_exp.now(i))
                    c.link(vec.tensor_reduce(lmv, lgv, AX.X, ALU.add))
                    c.link(vec.reciprocal(lmv, lmv))
                    c.link(vec.tensor_tensor(lgv, lgv, spread(lmv, 8, 4), ALU.mult))
                    c.link(vec.tensor_scalar(lgv, lgv, 1.0 - 4.0 * FLOOR, FLOOR, ALU.mult, ALU.add))
                    for k in range(2):
                        m = c.mark(vec.tensor_tensor(sqo[:, k].rearrange("p n (h d) -> p n h d", h=NH), outs[:, k].rearrange("p n (h d) -> p n h d", h=NH),
                                                     lg[:, k].rearrange("p h j -> p j h").unsqueeze(3).broadcast_to([P, 4, NH, HS]), ALU.mult))
                    c.need(m)
                    c.link(vec.tensor_reduce(mixed[:], sqo[:].rearrange("p k n d -> p k d n"), AX.X, ALU.add))
                    rmv, rrv = rm[:].rearrange("p k h -> p (k h)"), rr[:].rearrange("p k h -> p (k h)")
                    for n, weight in enumerate(("G_mix", "G_onorm")):
                        c.link(vec.tensor_tensor(sqm[:], mixed[:], mixed[:], ALU.mult))
                        c.link(vec.tensor_reduce(rmv, heads(sqm[:]), AX.X, ALU.add))
                        vec.tensor_scalar(rmv, rmv, 1.0 / HS, EPS, ALU.mult, ALU.add).then_inc(ms_ready.sem, 1)
                        vec.wait_ge(mr_ready.sem, mr_ready.now(i, n + 1))
                        c.link(vec.tensor_tensor(heads(mixed[:]), heads(mixed[:]), spread(rrv, 8, HS), ALU.mult))
                        ins = vec.tensor_tensor(mixed[:], mixed[:], w[weight].unsqueeze(1).broadcast_to([P, 2, P]), ALU.mult)
                        if n == 0:
                            c.link(ins)
                    ins.then_inc(on_ready.sem, 1)
                    vec.wait_ge(out_ps.sem, out_ps.now(i))
                    residual(sh, vec, c, i, B[0][:, 0:T].rearrange("p (a b) -> p a b", a=2), out_read)


LAYERS = [latent_attention, top2_ffn_first, linear_attention_small, top2_ffn_second,
          linear_attention_large, expert_choice_ffn_first, delta_rule_mixer, expert_choice_ffn_second]



WEIGHTS = {
    "A_wdq": ("L0_attn_a_W_dq", lambda a: a),
    "A_wuqT": ("L0_attn_a_W_uq", lambda a: a.T),
    "A_wdkv": ("L0_attn_a_W_dkv", lambda a: a),
    "A_wuk": ("L0_attn_a_W_uk", lambda a: a),
    "A_wuv": ("L0_attn_a_W_uv", lambda a: a),
    "A_woT": ("L0_attn_a_W_o", lambda a: a.T),
    "B_gateT": ("L0_ffn_gate_w", lambda a: a.T),
    "B_w1T": ("L0_ffn_w1", lambda a: a.transpose(2, 0, 1).reshape(D, -1)),
    "B_w3T": ("L0_ffn_w3", lambda a: a.transpose(2, 0, 1).reshape(D, -1)),
    "B_w2T": ("L0_ffn_w2", lambda a: a.transpose(2, 0, 1).reshape(D, -1)),
    "B_b1T": ("L0_ffn_b1", lambda a: a.T),
    "B_b2T": ("L0_ffn_b2", lambda a: a.T),
    "B_b3T": ("L0_ffn_b3", lambda a: a.T),
    "B_sw1T": ("L0_ffn_sw1", lambda a: a.T),
    "B_sw2T": ("L0_ffn_sw2", lambda a: a.T),
    "B_sw3T": ("L0_ffn_sw3", lambda a: a.T.reshape(2, P, D).transpose(1, 0, 2).reshape(P, -1)),
    "C_wqT": ("L0_attn_b_Wq", lambda a: a.T),
    "C_wkT": ("L0_attn_b_Wk", lambda a: a.T),
    "C_wvT": ("L0_attn_b_Wv", lambda a: a.T),
    "C_woT": ("L0_attn_b_Wo", lambda a: a.T),
    "E_wqT": ("L1_attn_a_Wq", lambda a: a.T.reshape(16, 64, D).transpose(1, 0, 2).reshape(64, -1)),
    "E_wkT": ("L1_attn_a_Wk", lambda a: a.T.reshape(16, 64, D).transpose(1, 0, 2).reshape(64, -1)),
    "E_wv": ("L1_attn_a_Wv", lambda a: a),
    "E_wo": ("L1_attn_a_Wo", lambda a: a.reshape(8, P, D).transpose(1, 0, 2).reshape(P, -1)),
    "E_proj": ("L1_attn_a_proj", lambda a: a),
    "F_gate": ("L1_ffn_gate_w", lambda a: a),
    "F_w1": ("L1_ffn_w1", lambda a: a.transpose(1, 0, 2).reshape(D, -1)),
    "F_w2": ("L1_ffn_w2", lambda a: a.reshape(8, 4, P, D).transpose(2, 0, 1, 3).reshape(P, -1)),
    "G_wq": ("L1_attn_b_Wq", lambda a: a),
    "G_wk": ("L1_attn_b_Wk", lambda a: a),
    "G_wv": ("L1_attn_b_Wv", lambda a: a),
    "G_wb": ("L1_attn_b_Wb", lambda a: a),
    "G_conv": (("L1_attn_b_conv_q_w", "L1_attn_b_conv_k_w", "L1_attn_b_conv_v_w"), lambda *a: np.concatenate(a, 1)),
    "G_local": ("L1_attn_b_local_w", lambda a: a),
    "G_mid": ("L1_attn_b_mid_w", lambda a: a),
    "G_rw1x": ("L1_attn_b_r_w1", lambda a: a[:D]),
    "G_rw1f": ("L1_attn_b_r_w1", lambda a: np.concatenate(
        [a[D:D + 32].reshape(4, 2, 4, -1)[:, 0].reshape(16, -1), a[D:D + 32].reshape(4, 2, 4, -1)[:, 1].reshape(16, -1), a[D + 32:]])),
    "G_rb1": ("L1_attn_b_r_b1", lambda a: np.concatenate([a, a[:16]]).reshape(3, P).T),
    "G_rw2": ("L1_attn_b_r_w2", lambda a: np.concatenate([a, a[:16]]).reshape(3, P, 16).transpose(1, 0, 2).reshape(P, -1)),
    "G_rb2": ("L1_attn_b_r_b2", lambda a: a.reshape(1, -1)),
    "G_mix": ("L1_attn_b_mix_w", lambda a: np.tile(a.reshape(1, -1), (P, 1))),
    "G_onorm": ("L1_attn_b_onorm_w", lambda a: np.tile(a.reshape(1, -1), (P, 4))),
    "G_wo": ("L1_attn_b_Wo", lambda a: a),
}


def build(nc, x_in, const_in, weights_in, out):
    sh = Shared()
    sh.nc, sh.seqs = nc, x_in.shape[0]
    sh.tiles = x_in.shape[0] * T // P
    with ExitStack() as ctx:
        def sb(name, shape, dt=F32):
            return ctx.enter_context(nc.sbuf_tensor(name, shape, dt))

        sh.x = sb("x", [P, sh.tiles, D])
        sh.stats = sb("stats", [P, sh.tiles, 6])
        sh.mean, sh.rstd = sb("mean", [P, sh.tiles]), sb("rstd", [P, sh.tiles])
        sh.consts = sb("consts", list(const_in.shape))
        late = {k: a for k, a in weights_in.items() if k.startswith("E_")}
        weights_in = {k: a for k, a in weights_in.items() if k not in late}
        w = {k: sb(k, list(a.shape)) for k, a in weights_in.items()}

        parts = 4
        with Stage(nc, "load") as st:
            x_in_sb = [st.semaphore(f"x_part{n}", 16) for n in range(parts)]
            weights_sb = st.semaphore("weights", 16)
            xv = x_in.rearrange("s (k p) d -> p (s k) d", p=P)
            step = sh.tiles // parts
            with nc.Block() as block:
                @block.sync
                def _(sync):
                    for n in range(parts):
                        sync.dma_start(sh.x[:, n * step:(n + 1) * step, :], xv[:, n * step:(n + 1) * step, :]).then_inc(x_in_sb[n].sem, 16)

                @block.scalar
                def _(act):
                    act.dma_start(sh.consts[:], const_in).then_inc(weights_sb.sem, 16)
                    for k, a in weights_in.items():
                        act.dma_start(w[k][:], a).then_inc(weights_sb.sem, 16)
                    act.wait_ge(weights_sb.sem, 16 * (1 + len(w)))

                @block.vector
                def _(vec):
                    for n in range(parts):
                        vec.wait_ge(x_in_sb[n].sem, 16)
                        for t in range(n * step, (n + 1) * step):
                            vec.bn_stats(sh.stats[:, t, :], sh.x[:, t, :])

        w = {k: v[:] for k, v in w.items()}
        late_ctx = ExitStack()
        at = LAYERS.index(linear_attention_large) if linear_attention_large in LAYERS else -1
        for n, layer in enumerate(LAYERS):
            if n == max(at - 1, 0) and at >= 0:
                late_sb = {k: late_ctx.enter_context(nc.sbuf_tensor(k, list(a.shape), F32)) for k, a in late.items()}
                late_in = late_ctx.enter_context(nc.semaphore("late_weights"))
                with nc.Block() as block:
                    @block.sync
                    def _(sync):
                        for k, a in late.items():
                            sync.dma_start(late_sb[k][:], a).then_inc(late_in, 16)
            if n == at:
                with nc.Block() as block:
                    @block.sync
                    def _(sync):
                        sync.wait_ge(late_in, 16 * len(late))
                w.update({k: v[:] for k, v in late_sb.items()})
            finish_stats(sh, f"norm{n}")
            layer(sh, w)
            if n == at:
                late_ctx.close()

        with Stage(nc, "store") as st:
            stored = st.semaphore("stored", 16)
            with nc.Block() as block:
                @block.sync
                def _(sync):
                    sync.dma_start(out.rearrange("s (k p) d -> p (s k) d", p=P), sh.x[:]).then_inc(stored.sem, 16)
                    sync.wait_ge(stored.sem, 16)


def kernel(**inputs):
    import numpy as _np
    import concourse.bacc as _bacc
    from concourse import mybir as _mybir
    from concourse.bass_utils import run_bass_kernel_spmd as _run

    nc = _bacc.Bacc("TRN2", target_bir_lowering=False, num_devices=1)
    arrays = {"x_dram": _np.ascontiguousarray(inputs["L0_attn_a_x"]), "const_dram": CONSTS}
    for name, (source, layout) in WEIGHTS.items():
        arrays[f"{name}_dram"] = _np.ascontiguousarray(
            layout(*(_np.asarray(inputs[s]) for s in ((source,) if isinstance(source, str) else source))))
    aps = {k: nc.dram_tensor(k, a.shape, _mybir.dt.from_np(a.dtype), kind="ExternalInput").ap() for k, a in arrays.items()}
    out = nc.dram_tensor("out_dram", arrays["x_dram"].shape, F32, kind="ExternalOutput").ap()
    build(nc, aps["x_dram"], aps["const_dram"], {k: aps[f"{k}_dram"] for k in WEIGHTS}, out)
    r = _run(nc, [arrays], core_ids=[0])
    return r.results[0]["out_dram"]
```

```python
from contextlib import ExitStack

import numpy as np
import concourse.bass as bass
from concourse import mybir

F32 = mybir.dt.float32
BF16 = mybir.dt.bfloat16
ALU = mybir.AluOpType
ACT = mybir.ActivationFunctionType
AX = mybir.AxisListType

P = 128
D = 128
T = 256
PAD = 4
LN_EPS = 1e-5
NEG = -1e30


class Counter:

    def __init__(self, sem, per, credit):
        self.sem, self.per, self.credit = sem, per, per if credit else 0

    def now(self, i, n=None):
        return i * self.per + (self.per if n is None else n) + self.credit

    def last(self, i, n=None):
        assert self.credit
        return i * self.per + (self.per if n is None else n)


class Stage:

    def __init__(self, nc, name):
        self.nc, self.name, self.ctx = nc, name, ExitStack()
        self.counters = []

    def __enter__(self):
        self.ctx.__enter__()
        return self

    def sb(self, name, shape, dt=F32):
        return self.ctx.enter_context(self.nc.sbuf_tensor(f"{self.name}_{name}", shape, dt))

    def ps(self, name, cols, dt=F32):
        return self.ctx.enter_context(self.nc.psum_tensor(f"{self.name}_{name}", [P, cols], dt))

    def semaphore(self, name, per, credit=False):
        s = Counter(self.ctx.enter_context(self.nc.semaphore(f"{self.name}_{name}")), per, credit)
        self.counters.append(s)
        return s

    def chain(self):
        return self.semaphore("vector_chain", 1)

    def give_credits(self, eng):
        for s in self.counters:
            if s.credit:
                eng.sem_inc(s.sem, s.credit)

    def __exit__(self, *a):
        if a[0] is None:
            sems = [s.sem for s in self.counters]
            for s in sems:
                self.nc.gpsimd.sem_clear(s)
            self.nc.all_engine_barrier()
        return self.ctx.__exit__(*a)


class Chain:

    def __init__(self, eng, counter):
        self.eng, self.sem, self.n = eng, counter.sem, 0

    def restart(self):
        self.eng.sem_clear(self.sem)
        self.n = 0

    def mark(self, ins):
        self.n += 1
        ins.then_inc(self.sem, 1)
        return self.n

    def need(self, n):
        self.eng.wait_ge(self.sem, n)

    def link(self, ins):
        self.need(self.mark(ins))


def const_table():
    p = np.arange(P)[:, None]
    f = np.arange(P)[None, :]
    parts = {
        "ident": (p == f),
        "neg_after": np.where(f > p, NEG, 0.0),
        "upto_f": (p <= f),
        "head_rows": ((p // 8) % 4 == np.arange(4)[None, :]),
        "before": (f < p),
        "same_head": (p // 32 == f // 32),
        **{f"mT{s}": ((p // (2 * s) == f // (2 * s)) & (f // s % 2 == 1) & (p // s % 2 == 0)) for s in (1, 2, 4, 8, 16, 32, 64)},
        "ones128": np.ones((1, P)) + 0 * p,
        "own_head": (p // 8 == np.arange(16)[None, :]),
        "same_head8": (p // 8 == f // 8),
        "iota": np.tile(np.arange(64)[None, :] + 1, (P, 1)),
        "earlier8": np.tile((np.arange(8)[None, :] < np.arange(8)[:, None]).reshape(1, 64), (P, 1)),
        "ones32": np.ones((1, 32)) + 0 * p,
        "pick8": (np.arange(P)[:, None, None] == np.arange(8)[None, :, None]) * np.ones((1, 1, P)),
    }
    out, at, n = [], {}, 0
    for k, v in parts.items():
        v = np.asarray(v, np.float32).reshape(P, -1)
        at[k] = (n, n + v.shape[1])
        n += v.shape[1]
        out.append(v)
    return np.concatenate(out, 1), at


CONSTS, CONST_AT = const_table()


class Shared:

    def c(self, name):
        a, b = CONST_AT[name]
        return self.consts[:, a:b]


def residual(sh, vec, c, i, y, done):
    x = sh.x[:, bass.ds(2 * i, 2), :]
    n = c.mark(vec.tensor_tensor(x, x, y, ALU.add))
    c.need(n)
    for k in range(2):
        ins = vec.bn_stats(sh.stats[:, bass.ds(2 * i + k, 1), :], sh.x[:, bass.ds(2 * i + k, 1), :])
    if done is not None:
        ins.then_inc(done.sem, 1)


def front_vector(sh, st, vec, ch, i, xhat):
    for k in range(2):
        ins = vec.tensor_scalar(xhat[:, k, :], sh.x[:, bass.ds(2 * i + k, 1), :],
                                sh.mean[:, bass.ds(2 * i + k, 1)], sh.rstd[:, bass.ds(2 * i + k, 1)],
                                ALU.subtract, ALU.mult)
    return ins


def finish_stats(sh, name):
    nc = sh.nc
    with Stage(nc, name) as st:
        ch = st.chain()
        var_ready, std_ready = st.semaphore("var_ready", 1), st.semaphore("std_ready", 1)
        dm, var = st.sb("dm", [P, sh.tiles]), st.sb("var", [P, sh.tiles])
        with nc.Block() as block:
            s, mean, rstd = sh.stats, sh.mean[:, 0:sh.tiles], sh.rstd[:, 0:sh.tiles]

            @block.vector
            def _(vec):
                c = Chain(vec, ch)
                vec.tensor_tensor(mean, s[:, :, 1], s[:, :, 4], ALU.add)
                vec.tensor_tensor(var[:], s[:, :, 2], s[:, :, 5], ALU.add)
                c.link(vec.tensor_tensor(dm[:], s[:, :, 1], s[:, :, 4], ALU.subtract))
                c.link(vec.tensor_tensor(dm[:], dm[:], dm[:], ALU.mult))
                c.link(vec.tensor_scalar(dm[:], dm[:], 0.25, LN_EPS, ALU.mult, ALU.add))
                vec.scalar_tensor_tensor(var[:], var[:], 1.0 / D, dm[:], ALU.mult, ALU.add).then_inc(var_ready.sem, 1)
                c.link(vec.tensor_scalar(mean, mean, 0.5, None, ALU.mult))
                vec.wait_ge(std_ready.sem, 1)
                vec.reciprocal(rstd, var[:])

            @block.scalar
            def _(act):
                act.wait_ge(var_ready.sem, 1)
                act.activation(var[:], var[:], ACT.Sqrt).then_inc(std_ready.sem, 1)


def latent_attention(sh, w):
    nc, NH, HS, L = sh.nc, 16, 8, 32
    SCALE = float(HS) ** -0.5
    NS = sh.seqs
    with Stage(nc, "latent") as st:
        wq, wqT, keffT, veff = (st.sb("wq", [P, P]), st.sb("wqT", [P, P]), st.sb("keffT", [L, P]), st.sb("veff", [L, P]))
        wk, wv = st.sb("wk", [P, P]), st.sb("wv", [P, P])
        identb, negb = st.sb("identb", [P, P], BF16), st.sb("negb", [P, P], BF16)
        xhat, xT = st.sb("xhat", [P, 2, P]), st.sb("xT", [P, T])
        q_h, k_f = st.sb("q_h", [P, 4, T]), st.sb("k_f", [P, T])
        v_pad = st.sb("v_pad", [P, 2, NH * (P + HS)])
        probs = st.sb("probs", [P, 2, 1024])
        probsT = st.sb("probsT", [P, 2, 1024])
        mx, rs = st.sb("mx", [P, 6, 8]), st.sb("rs", [P, 2, NH])
        yT, y = st.sb("yT", [P, T]), st.sb("y", [P, 2, NH, HS])
        S = st.ps("scores", 2048)
        PT = st.ps("probsT_ps", 1024)
        FR = st.ps("front_ps", 512)
        O = st.ps("out_ps", 512)

        ch = st.chain()
        prep = st.semaphore("prep", 1)
        prep_sb = st.semaphore("prep_sb", 1)
        zeroed = st.semaphore("zeroed", 1)
        xhat_ready = st.semaphore("xhat_ready", 1)
        xT_ps, xT_sb = st.semaphore("xT_ps", 1), st.semaphore("xT_sb", 1)
        qk_ps, v_ps = st.semaphore("qk_ps", 1), st.semaphore("v_ps", 1)
        q_ready, k_ready, v_ready = (st.semaphore(n, 1) for n in ("q_ready", "k_ready", "v_ready"))
        scored = st.semaphore("scored", 6)
        shifted = st.semaphore("shifted", 6, True)
        expd = st.semaphore("expd", 6)
        added = st.semaphore("added", 6, True)
        turned = st.semaphore("turned", 6, True)
        turned_sb = st.semaphore("turned_sb", 6, True)
        summed = st.semaphore("summed", 6, True)
        yT_sb, y_turned = st.semaphore("yT_sb", 1), st.semaphore("y_turned", 1)
        out_read = st.semaphore("out_read", 1, True)

        def unit(u):
            g, jp = u // 2, u % 2
            if g == 0:
                return 0, [(j, r, [(0, j * 512 + r * 128)]) for j in (2 * jp, 2 * jp + 1) for r in range(4)]
            return 1, [(j, 2 * (g - 1) + r, [(0, j * 512 + r * 256), (1, j * 512 + r * 256 + 128)])
                       for j in (2 * jp, 2 * jp + 1) for r in range(2)]

        def by_head(u, ap):
            g, jp = u // 2, u % 2
            rows = (0, 4) if g == 0 else (2 * g - 2, 2 * g)
            return ap.rearrange("p (j r) -> p j r", r=4)[:, 2 * jp:2 * jp + 2, rows[0]:rows[1]]

        with nc.Block() as block:

            @block.gpsimd
            def _(pool):
                st.give_credits(pool)
                pool.memset(v_pad[:], 0.0).then_inc(zeroed.sem, 1)

            @block.tensor
            def _(pe):
                def mm(out, lhsT, rhs):
                    return pe.matmul(out, lhsT, rhs, start=True, stop=True)

                mm(FR[:, 0:128], w["A_wdq"], w["A_wuqT"])
                mm(FR[:, 128:256], w["A_wuqT"], w["A_wdq"])
                mm(FR[0:L, 256:384], w["A_wuv"], w["A_woT"]).then_inc(prep.sem, 1)
                pe.wait_ge(prep_sb.sem, 1)
                mm(O[0:L, 0:128], w["A_wuk"], wqT[:])
                mm(O[:, 128:256], w["A_wdkv"], veff[:]).then_inc(prep.sem, 1)
                pe.wait_ge(prep_sb.sem, 2)
                mm(O[:, 256:384], w["A_wdkv"], keffT[:]).then_inc(prep.sem, 1)
                pe.wait_ge(prep_sb.sem, 3)

                def turn_x():
                    for k in range(2):
                        ins = pe.transpose(FR[:, 128 * k:128 * k + 128], xhat[:, k, :], sh.c("ident"))
                    ins.then_inc(xT_ps.sem, 1)

                def project_qk():
                    mm(FR[:, 0:T], wq[:], xT[:])
                    mm(FR[:, T:2 * T], wk[:], xT[:]).then_inc(qk_ps.sem, 1)

                def project_v():
                    for k in range(2):
                        ins = mm(FR[:, 128 * k:128 * k + 128], xT[:, 128 * k:128 * k + 128], wv[:])
                    ins.then_inc(v_ps.sem, 1)

                pe.wait_ge(xhat_ready.sem, 1)
                turn_x()
                pe.wait_ge(xT_sb.sem, 1)
                project_qk()

                with pe.Fori(0, NS) as i:

                    def scores(u):
                        tq, heads = unit(u)
                        if u < 2:
                            pe.wait_ge(shifted.sem, shifted.last(i, u + 5))
                        else:
                            pe.wait_ge(shifted.sem, shifted.now(i, u - 1))
                        for j, r, cols in heads:
                            c0, n = cols[0][1], 128 * len(cols)
                            pe.matmul(S[:, c0:c0 + n], q_h[32 * j:32 * j + 32, r, 128 * tq:128 * tq + 128],
                                      k_f[32 * j:32 * j + 32, 0:n], start=True, stop=True)
                            ins = pe.matmul(S[:, c0 + n - 128:c0 + n], identb[:], negb[:], start=False, stop=True, skip_group_check=True)
                        ins.then_inc(scored.sem, 1)

                    def turn(u):
                        pe.wait_ge(expd.sem, expd.now(i, u + 1))
                        if u:
                            pe.wait_ge(turned_sb.sem, turned_sb.now(i, u))
                        else:
                            pe.wait_ge(turned_sb.sem, turned_sb.last(i))
                        for b in range(8):
                            ins = pe.transpose(PT[:, 128 * b:128 * b + 128], probs[:, u % 2, 128 * b:128 * b + 128], sh.c("ident"))
                        ins.then_inc(turned.sem, 1)

                    def values(u):
                        pe.wait_ge(turned_sb.sem, turned_sb.now(i, u + 1))
                        tq, heads = unit(u)
                        b = 0
                        for j, r, cols in heads:
                            h = 4 * j + r
                            for tk, _ in cols:
                                ins = pe.matmul(O[:, 128 * tq:128 * tq + 128], v_pad[:, tk, P * h:P * h + P], probsT[:, u % 2, 128 * b:128 * b + 128],
                                                start=(b == 0 and u in (0, 2)), stop=(b == 7 and u in (1, 5)), skip_group_check=True)
                                b += 1
                        ins.then_inc(summed.sem, 1)

                    pe.wait_ge(q_ready.sem, q_ready.now(i))
                    pe.wait_ge(k_ready.sem, k_ready.now(i))
                    scores(0)
                    scores(1)
                    project_v()
                    for u in range(6):
                        turn(u)
                        if u + 2 < 6:
                            scores(u + 2)
                        if u == 1:
                            pe.wait_ge(v_ready.sem, v_ready.now(i))
                            pe.wait_ge(out_read.sem, out_read.last(i))
                        if u:
                            values(u - 1)
                        if u == 2:
                            pe.wait_ge(xhat_ready.sem, i + 2)
                            turn_x()
                        if u == 3:
                            pe.wait_ge(xT_sb.sem, i + 2)
                            project_qk()
                    values(5)
                    pe.wait_ge(yT_sb.sem, yT_sb.now(i))
                    for k in range(2):
                        ins = pe.transpose(O[:, 128 * k:128 * k + 128], yT[:, 128 * k:128 * k + 128], sh.c("ident"))
                    ins.then_inc(y_turned.sem, 1)

            @block.scalar
            def _(act):
                act.wait_ge(prep.sem, 1)
                act.copy(wq[:], FR[:, 0:128])
                act.copy(wqT[:], FR[:, 128:256])
                act.copy(veff[:], FR[0:L, 256:384]).then_inc(prep_sb.sem, 1)
                act.wait_ge(prep.sem, 2)
                act.copy(keffT[:], O[0:L, 0:128])
                act.copy(wv[:], O[:, 128:256]).then_inc(prep_sb.sem, 1)
                act.wait_ge(prep.sem, 3)
                act.copy(identb[:], sh.c("ident"))
                act.copy(wk[:], O[:, 256:384])
                act.copy(negb[:], sh.c("neg_after")).then_inc(prep_sb.sem, 1)

                def take_x():
                    act.copy(xT[:], FR[:, 0:T]).then_inc(xT_sb.sem, 1)

                def take_k():
                    act.copy(k_f[:], FR[:, T:2 * T]).then_inc(k_ready.sem, 1)

                def take_v():
                    act.copy(v_pad[:].rearrange("p a (h s) -> p a h s", h=NH)[:, :, :, 0:HS],
                             FR[:, 0:T].rearrange("p (a h d) -> p a h d", a=2, h=NH)).then_inc(v_ready.sem, 1)

                act.wait_ge(zeroed.sem, 1)
                act.wait_ge(xT_ps.sem, 1)
                take_x()
                act.wait_ge(q_ready.sem, 1)
                take_k()
                with act.Fori(0, NS) as i:

                    def expo(u):
                        act.wait_ge(shifted.sem, shifted.now(i, u + 1))
                        act.activation(probs[:, u % 2, :], probs[:, u % 2, :], ACT.Exp, scale=SCALE).then_inc(expd.sem, 1)

                    def evac(u):
                        act.wait_ge(turned.sem, turned.now(i, u + 1))
                        if u >= 2:
                            act.wait_ge(summed.sem, summed.now(i, u - 1))
                        else:
                            act.wait_ge(summed.sem, summed.last(i, u + 5))
                        act.copy(probsT[:, u % 2, :], PT[:]).then_inc(turned_sb.sem, 1)

                    expo(0)
                    act.wait_ge(v_ps.sem, v_ps.now(i))
                    act.wait_ge(summed.sem, summed.last(i))
                    take_v()
                    for u in range(6):
                        if u + 1 < 6:
                            expo(u + 1)
                        evac(u)
                        if u == 3:
                            act.wait_ge(xT_ps.sem, i + 2)
                            act.wait_ge(v_ps.sem, v_ps.now(i))
                            take_x()
                    act.wait_ge(q_ready.sem, i + 2)
                    act.wait_ge(scored.sem, scored.now(i, 6))
                    take_k()
                    act.wait_ge(summed.sem, summed.now(i, 6))
                    act.copy(yT[:], O[:, 0:T]).then_inc(yT_sb.sem, 1)

            @block.vector
            def _(vec):
                c = Chain(vec, ch)

                def take_q():
                    for r in range(4):
                        ins = vec.tensor_scalar(q_h[:, r, :], FR[:, 0:T], sh.c("head_rows")[:, r:r + 1], None, ALU.mult)
                    ins.then_inc(q_ready.sem, 1)

                front_vector(sh, st, vec, c, 0, xhat).then_inc(xhat_ready.sem, 1)
                vec.wait_ge(qk_ps.sem, 1)
                take_q()
                with vec.Fori(0, NS) as i:
                    c.restart()
                    vec.wait_ge(out_read.sem, out_read.last(i))

                    def add(u):
                        h = 4 if u < 2 else 2
                        vec.wait_ge(expd.sem, expd.now(i, u + 1))
                        vec.tensor_reduce(by_head(u, rs[:, unit(u)[0], :]), probs[:, u % 2, :].rearrange("p (j r s) -> p j r s", j=2, r=h),
                                          AX.X, ALU.add).then_inc(added.sem, 1)

                    for u in range(6):
                        tq, heads = unit(u)
                        n = len(heads)
                        s = S[:, 1024 * (u % 2):1024 * (u % 2) + 1024].rearrange("p (h s) -> p h s", h=n)
                        vec.wait_ge(scored.sem, scored.now(i, u + 1))
                        c.link(vec.tensor_reduce(mx[:, u, 0:n], s, AX.X, ALU.max))
                        if u >= 2:
                            vec.wait_ge(turned.sem, turned.now(i, u - 1))
                            vec.wait_ge(added.sem, added.now(i, u - 1))
                        else:
                            vec.wait_ge(turned.sem, turned.last(i, u + 5))
                            vec.wait_ge(added.sem, added.last(i, u + 5))
                        vec.tensor_tensor(probs[:, u % 2, :].rearrange("p (h s) -> p h s", h=n), s,
                                          mx[:, u, 0:n].unsqueeze(2).broadcast_to([P, n, 1024 // n]),
                                          ALU.subtract).then_inc(shifted.sem, 1)
                        if u:
                            add(u - 1)
                        if u == 1:
                            vec.wait_ge(xT_ps.sem, xT_ps.now(i))
                            front_vector(sh, st, vec, c, i + 1, xhat).then_inc(xhat_ready.sem, 1)
                    vec.wait_ge(qk_ps.sem, i + 2)
                    vec.wait_ge(scored.sem, scored.now(i, 6))
                    take_q()
                    add(5)
                    vec.wait_ge(added.sem, added.now(i, 6))
                    c.link(vec.reciprocal(rs[:], rs[:]))
                    vec.wait_ge(y_turned.sem, y_turned.now(i))
                    o = O[:, 0:T].rearrange("p (a h d) -> p a h d", a=2, h=NH)
                    for k in range(2):
                        m = c.mark(vec.tensor_tensor(y[:, k], o[:, k], rs[:, k].unsqueeze(2).broadcast_to([P, NH, HS]), ALU.mult))
                    c.need(m)
                    residual(sh, vec, c, i, y[:].rearrange("p a h d -> p a (h d)"), out_read)


def gate(sh, name, gate_w, logits, xT_all):
    nc, turns, K = sh.nc, sh.seqs // 4, 4
    with Stage(nc, name) as st:
        xhat, xT = st.sb("xhat", [P, 2, K, P]), st.sb("xT", [P, 2, K * P])
        XT = [st.ps(f"xT_ps{j}", 512) for j in range(2)]
        LG = [st.ps(f"logits_ps{j}", 512) for j in range(2)]
        xhat_ready = st.semaphore("xhat_ready", 2)
        turned, xT_sb = st.semaphore("turned", 2, True), st.semaphore("xT_sb", 2, True)
        scored, scored_sb = st.semaphore("scored", 2, True), st.semaphore("scored_sb", 2, True)
        kept = st.semaphore("kept", 2, True)
        with nc.Block() as block:

            @block.gpsimd
            def _(pool):
                st.give_credits(pool)
                with pool.Fori(0, turns) as i:
                    for j in range(2):
                        pool.wait_ge(xT_sb.sem, xT_sb.now(i, j + 1))
                        if xT_all is not None:
                            pool.tensor_copy(xT_all[:, bass.ds(i * 1024 + 512 * j, 512)], xT[:, j, :]).then_inc(kept.sem, 1)
                        else:
                            pool.sem_inc(kept.sem, 1)

            @block.vector
            def _(vec):
                with vec.Fori(0, turns) as i:
                    for j in range(2):
                        vec.wait_ge(turned.sem, turned.last(i, j + 1))
                        for k in range(K):
                            t = 2 * K * i + K * j + k
                            ins = vec.tensor_scalar(xhat[:, j, k, :], sh.x[:, bass.ds(t, 1), :], sh.mean[:, bass.ds(t, 1)],
                                                    sh.rstd[:, bass.ds(t, 1)], ALU.subtract, ALU.mult)
                        ins.then_inc(xhat_ready.sem, 1)

            @block.tensor
            def _(pe):
                with pe.Fori(0, turns) as i:
                    for j in range(2):
                        pe.wait_ge(xhat_ready.sem, xhat_ready.now(i, j + 1))
                        pe.wait_ge(xT_sb.sem, xT_sb.last(i, j + 1))
                        for k in range(K):
                            ins = pe.transpose(XT[j][:, 128 * k:128 * k + 128], xhat[:, j, k, :], sh.c("ident"))
                        ins.then_inc(turned.sem, 1)
                    for j in range(2):
                        pe.wait_ge(xT_sb.sem, xT_sb.now(i, j + 1))
                        pe.wait_ge(scored_sb.sem, scored_sb.last(i, j + 1))
                        for k in range(K):
                            ins = pe.matmul(LG[j][:, 8 * k:8 * k + 8], xT[:, j, 128 * k:128 * k + 128], gate_w, start=True, stop=True)
                        ins.then_inc(scored.sem, 1)

            @block.scalar
            def _(act):
                with act.Fori(0, turns) as i:
                    for j in range(2):
                        act.wait_ge(turned.sem, turned.now(i, j + 1))
                        act.wait_ge(scored.sem, scored.last(i, j + 1))
                        act.wait_ge(kept.sem, kept.last(i, j + 1))
                        act.copy(xT[:, j, :], XT[j][:]).then_inc(xT_sb.sem, 1)
                    for j in range(2):
                        act.wait_ge(scored.sem, scored.now(i, j + 1))
                        act.copy(logits[:, bass.ds(2 * K * i + K * j, K), :], LG[j][:, 0:8 * K].rearrange("p (k e) -> p k e", k=K)).then_inc(scored_sb.sem, 1)


def softmax8(sh, name, logits, after=None):
    nc, n = sh.nc, sh.tiles
    with Stage(nc, name) as st:
        ch, shifted, expd = st.chain(), st.semaphore("shifted", 1), st.semaphore("expd", 1)
        m = st.sb("m", [P, n])
        extra = after and after(st)
        with nc.Block() as block:
            @block.vector
            def _(vec):
                c = Chain(vec, ch)
                c.link(vec.tensor_reduce(m[:], logits[:], AX.X, ALU.max))
                vec.tensor_tensor(logits[:], logits[:], m[:].unsqueeze(2).broadcast_to([P, n, 8]),
                                  ALU.subtract).then_inc(shifted.sem, 1)
                vec.wait_ge(expd.sem, 1)
                c.link(vec.tensor_reduce(m[:], logits[:], AX.X, ALU.add))
                c.link(vec.reciprocal(m[:], m[:]))
                c.link(vec.tensor_tensor(logits[:], logits[:], m[:].unsqueeze(2).broadcast_to([P, n, 8]), ALU.mult))
                if extra:
                    extra(vec, c)

            @block.scalar
            def _(act):
                act.wait_ge(shifted.sem, 1)
                act.activation(logits[:], logits[:], ACT.Exp).then_inc(expd.sem, 1)


def top2_ffn(sh, w, name):
    nc, NE, NS = sh.nc, 8, sh.seqs
    with ExitStack() as ctx:
        def keep(n, shape, dt=F32):
            return ctx.enter_context(nc.sbuf_tensor(f"{name}_{n}", shape, dt))
        g_all, xT_all = keep("g_all", [P, sh.tiles, NE]), keep("xT_all", [P, sh.tiles * P])
        picked_all = keep("picked_all", [P, sh.tiles, NE])
        gate(sh, name + "_gate", w["B_gateT"], g_all, xT_all)

        def top2(st):
            half = sh.tiles // 2
            better, equal = st.sb("better", [P, half, NE, NE]), st.sb("equal", [P, half, NE, NE])
            rank = st.sb("rank", [P, half, NE])

            def run(vec, c):
                for b in range(2):
                    g = g_all[:, b * half:(b + 1) * half, :]
                    other = g.unsqueeze(2).broadcast_to([P, half, NE, NE])
                    own = g.unsqueeze(3).broadcast_to([P, half, NE, NE])
                    vec.tensor_tensor(better[:], other, own, ALU.is_gt)
                    c.link(vec.tensor_tensor(equal[:], other, own, ALU.is_equal))
                    tie = sh.c("earlier8").rearrange("p (a b) -> p a b", a=NE).unsqueeze(1).broadcast_to([P, half, NE, NE])
                    c.link(vec.tensor_tensor(equal[:], equal[:], tie, ALU.mult))
                    c.link(vec.tensor_tensor(better[:], better[:], equal[:], ALU.add))
                    c.link(vec.tensor_reduce(rank[:], better[:], AX.X, ALU.add))
                    picked = picked_all[:, b * half:(b + 1) * half, :]
                    c.link(vec.tensor_scalar(picked, rank[:], 1.5, None, ALU.is_lt))
                    c.link(vec.tensor_tensor(g, g, picked, ALU.mult))
            return run

        softmax8(sh, name + "_top2", g_all, top2)

        N2 = 2 * T
        with Stage(nc, name) as st:
            g, picked = st.sb("g", [P, 4, NE]), st.sb("picked", [P, 4, NE], BF16)
            identb, touch = st.sb("identb", [P, P], BF16), st.sb("touch", [P, 1])
            xs, picked_f = st.sb("xs", [P, 4, N2]), st.sb("picked_f", [P, 2, N2])
            h, hz = st.sb("h", [P, 2, N2]), st.sb("hz", [P, 2, N2])
            t1, y, ysum = st.sb("t1", [P, 2, N2]), st.sb("y", [P, 2, N2]), st.sb("ysum", [P, N2])
            GB, MB, Y = (st.ps(n, 512) for n in ("g_ps", "picked_ps", "y_ps"))
            H = [st.ps("h0_ps", 512), st.ps("h1_ps", 512)]
            X = [st.ps("x0_ps", 512), st.ps("x1_ps", 512)]
            ch = st.chain()
            ready = st.semaphore("ready", 1)
            staged = st.semaphore("staged", 1)
            STEPS, SH = NE + 2, 2
            spread = st.semaphore("spread", NE, True)
            picked_sb, scaled = st.semaphore("picked_sb", NE, True), st.semaphore("scaled", NE, True)
            x_ps, h_ps = st.semaphore("x_ps", STEPS), st.semaphore("h_ps", STEPS)
            act_done = st.semaphore("act_done", STEPS, True)
            down, d_taken = st.semaphore("down", NE, True), st.semaphore("d_taken", NE, True)
            x_taken = st.semaphore("x_taken", STEPS, True)
            total = st.semaphore("total", 1)
            out_ps, out_read = st.semaphore("out_ps", 1, True), st.semaphore("out_read", 1, True)

            with nc.Block() as block:

                @block.gpsimd
                def _(pool):
                    pool.memset(touch[:], 0.0)
                    pool.tensor_copy(identb[:], sh.c("ident")).then_inc(ready.sem, 1)
                    st.give_credits(pool)
                    with pool.Fori(0, NS // 2) as i:
                        pool.wait_ge(spread.sem, spread.last(i))
                        pool.tensor_copy(g[:], g_all[:, bass.ds(4 * i, 4), :])
                        pool.tensor_copy(picked[:], picked_all[:, bass.ds(4 * i, 4), :]).then_inc(staged.sem, 1)

                @block.tensor
                def _(pe):
                    pe.wait_ge(ready.sem, 1)
                    with pe.Fori(0, NS // 2) as i:
                        xT = xT_all[:, bass.ds(i * N2, N2)]

                        def prev(sig, m, n):
                            if m > 0:
                                pe.wait_ge(sig.sem, sig.now(i, m))
                            else:
                                pe.wait_ge(sig.sem, sig.last(i, m + n))

                        def spread_expert(e):
                            prev(scaled, e, NE)
                            prev(picked_sb, e, NE)
                            for k in range(4):
                                c = slice(128 * k, 128 * k + 128)
                                pe.transpose(GB[:, c], g[:, k, e:e + 1].broadcast_to([P, P]), sh.c("ident"))
                                ins = pe.matmul(MB[:, c], picked[:, k, e:e + 1].broadcast_to([P, P]), identb[:],
                                                start=True, stop=True)
                            ins.then_inc(spread.sem, 1)

                        def source(n):
                            return xs[:, n % 4, :] if n >= SH else xT

                        def expand_x(n):
                            if n >= SH:
                                pe.wait_ge(scaled.sem, scaled.now(i, n - SH + 1))
                            prev(x_taken, n - 1, STEPS)
                            a = w["B_w3T"][:, 128 * (n - SH):128 * (n - SH) + 128] if n >= SH else w["B_sw2T"][:, 128 * n:128 * n + 128]
                            pe.matmul(X[n % 2][:], a, source(n), start=True, stop=True).then_inc(x_ps.sem, 1)

                        def expand_h(n):
                            if n in (2, 3):
                                pe.wait_ge(act_done.sem, act_done.now(i, n - 1))
                            else:
                                prev(d_taken, n - 3, STEPS)
                            a = w["B_w1T"][:, 128 * (n - SH):128 * (n - SH) + 128] if n >= SH else w["B_sw1T"][:, 128 * n:128 * n + 128]
                            pe.matmul(H[n % 2][:], a, source(n), start=True, stop=True).then_inc(h_ps.sem, 1)

                        def contract(n):
                            e = n - SH
                            pe.wait_ge(act_done.sem, act_done.now(i, n + 1))
                            pe.matmul(H[n % 2][:], w["B_w2T"][:, 128 * e:128 * e + 128], h[:, n % 2, :],
                                      start=True, stop=True).then_inc(down.sem, 1)

                        for n in range(SH):
                            expand_x(n)
                            expand_h(n)
                            if n == 0:
                                pe.wait_ge(staged.sem, staged.now(i))
                                spread_expert(0)
                        for n in range(STEPS):
                            if n >= SH:
                                contract(n)
                            if n + 2 < STEPS:
                                expand_x(n + 2)
                                if n + 1 < NE:
                                    spread_expert(n + 1)
                                expand_h(n + 2)
                        pe.wait_ge(out_read.sem, out_read.last(i))
                        pe.wait_ge(x_taken.sem, x_taken.now(i, SH))
                        for k in range(4):
                            t = slice(128 * k, 128 * k + 128)
                            for s in range(2):
                                pe.matmul(Y[:, t], hz[:, s, t], w["B_sw3T"][:, 128 * s:128 * s + 128], start=(k == 0 and s == 0), stop=False,
                                          skip_group_check=True)
                        pe.wait_ge(total.sem, total.now(i))
                        for k in range(4):
                            t = slice(128 * k, 128 * k + 128)
                            ins = pe.matmul(Y[:, t], ysum[:, t], sh.c("ident"), start=False, stop=True, skip_group_check=True)
                        ins.then_inc(out_ps.sem, 1)

                @block.scalar
                def _(act):
                    act.wait_ge(ready.sem, 1)
                    with act.Fori(0, NS // 2) as i:
                        def masks(e):
                            act.wait_ge(spread.sem, spread.now(i, e + 1))
                            if e < 2:
                                act.wait_ge(x_taken.sem, x_taken.last(i))
                            else:
                                act.wait_ge(x_taken.sem, x_taken.now(i, SH + e - 1))
                            act.copy(picked_f[:, e % 2, :], MB[:]).then_inc(picked_sb.sem, 1)

                        act.activation(touch[:], touch[:], ACT.Silu)
                        for n in range(STEPS):
                            e = n - SH
                            act.wait_ge(h_ps.sem, h_ps.now(i, n + 1))
                            if n < 2:
                                act.wait_ge(down.sem, down.last(i, NE - 1 + n))
                            elif n < 4:
                                act.wait_ge(x_taken.sem, x_taken.now(i, n - 1))
                            else:
                                act.wait_ge(down.sem, down.now(i, n - 3))
                            bias = w["B_b1T"][:, e:e + 1] if e >= 0 else 0.0
                            act.activation(h[:, n % 2, :], H[n % 2][:], ACT.Silu, bias=bias).then_inc(act_done.sem, 1)
                            if n + 0 < NE:
                                masks(n)

                @block.vector
                def _(vec):
                    c = Chain(vec, ch)
                    with vec.Fori(0, NS // 2) as i:
                        c.restart()
                        vec.wait_ge(out_read.sem, out_read.last(i))
                        xT = xT_all[:, bass.ds(i * N2, N2)]

                        def scale(e):
                            vec.wait_ge(spread.sem, spread.now(i, e + 1))
                            vec.tensor_tensor(xs[:, (e + SH) % 4, :], xT, GB[:], ALU.mult).then_inc(scaled.sem, 1)

                        def third(e):
                            n = e + SH
                            vec.wait_ge(x_ps.sem, x_ps.now(i, n + 1))
                            vec.wait_ge(picked_sb.sem, picked_sb.now(i, e + 1))
                            vec.scalar_tensor_tensor(t1[:, e % 2, :], X[n % 2][:], w["B_b3T"][:, e:e + 1], picked_f[:, e % 2, :],
                                                     ALU.add, ALU.mult).then_inc(x_taken.sem, 1)

                        def second(e):
                            n = e + SH
                            vec.wait_ge(down.sem, down.now(i, e + 1))
                            vec.wait_ge(x_taken.sem, x_taken.now(i, n + 1))
                            dst = y[:, e % 2, :] if e else ysum[:]
                            vec.scalar_tensor_tensor(dst, H[n % 2][:], w["B_b2T"][:, e:e + 1], t1[:, e % 2, :],
                                                     ALU.add, ALU.mult).then_inc(d_taken.sem, 1)

                        scale(0)
                        vec.wait_ge(out_ps.sem, out_ps.last(i))
                        for s in range(SH):
                            vec.wait_ge(act_done.sem, act_done.now(i, s + 1))
                            vec.wait_ge(x_ps.sem, x_ps.now(i, s + 1))
                            vec.tensor_tensor(hz[:, s, :], h[:, s, :], X[s][:], ALU.mult).then_inc(x_taken.sem, 1)
                            scale(s + 1)
                        third(0)
                        for e in range(NE):
                            second(e)
                            if e + 3 < NE:
                                scale(e + 3)
                            if e + 1 < NE:
                                third(e + 1)
                            if e:
                                vec.wait_ge(d_taken.sem, d_taken.now(i, e + 1))
                                if e > 1:
                                    c.need(m)
                                ins = vec.tensor_tensor(ysum[:], ysum[:], y[:, e % 2, :], ALU.add)
                                if e < NE - 1:
                                    m = c.mark(ins)
                                else:
                                    ins.then_inc(total.sem, 1)
                        vec.wait_ge(out_ps.sem, out_ps.now(i))
                        for s in range(2):
                            residual(sh, vec, c, 2 * i + s, Y[:, T * s:T * s + T].rearrange("p (a b) -> p a b", a=2), out_read if s else None)




def top2_ffn_first(sh, w):
    top2_ffn(sh, w, "ffn_b")


def top2_ffn_second(sh, w):
    top2_ffn(sh, w, "ffn_d")


def linear_attention_small(sh, w):
    nc, NH, HS, NS = sh.nc, 16, 8, sh.seqs
    EPS = 1e-8
    with Stage(nc, "small") as st:
        xhat, xT = st.sb("xhat", [P, 2, P]), st.sb("xT", [P, T])
        e, f = st.sb("e", [P, 2 * T]), st.sb("f", [P, 2 * T])
        neg = st.sb("neg", [P, 2 * T])
        q_h, k_t = st.sb("q_h", [P, 4, T]), st.sb("k_t", [P, T])
        v_pad, state = st.sb("v_pad", [P, 2, NH * (P + HS)]), st.sb("state", [P, P])
        v_cols = v_pad[:].rearrange("p a (h s) -> p a h s", h=NH)[:, :, :, 0:HS]
        A = st.sb("A", [P, 2, 1024])
        upto_all, qk, den, y = st.sb("upto_all", [P, T]), st.sb("qk", [P, T]), st.sb("den", [P, T]), st.sb("y", [P, T])
        S = st.ps("scores", 2048)
        FR, QK, O, Y = (st.ps(n, 512) for n in ("front_ps", "qk_ps", "o_ps", "y_ps"))

        ch = st.chain()
        ready, mask_ready = st.semaphore("ready", 1), st.semaphore("mask_ready", 1)
        xhat_ready = st.semaphore("xhat_ready", 1)
        xT_ps, xT_sb = st.semaphore("xT_ps", 1), st.semaphore("xT_sb", 1)
        qk_ps, v_ps, v_sb = st.semaphore("qk_ps", 1), st.semaphore("v_ps", 1), st.semaphore("v_sb", 1)
        neg_ready, elu_in, f_ready, q_ready = (st.semaphore(n, 1) for n in ("neg_ready", "elu_in", "f_ready", "q_ready"))
        kt_ps, kt_sb = st.semaphore("kt_ps", 1), st.semaphore("kt_sb", 1)
        state_ps, state_sb = st.semaphore("state_ps", 1), st.semaphore("state_sb", 1)
        den_ps, den_read = st.semaphore("den_ps", 1), st.semaphore("den_read", 1)
        scored, masked, summed = st.semaphore("scored", 4), st.semaphore("masked", 4, True), st.semaphore("summed", 4, True)
        y_ready, out_ps, out_read = st.semaphore("y_ready", 1, True), st.semaphore("out_ps", 1), st.semaphore("out_read", 1, True)

        with nc.Block() as block:

            @block.gpsimd
            def _(pool):
                st.give_credits(pool)
                pool.tensor_copy(upto_all[:, 0:P], sh.c("upto_f"))
                pool.memset(upto_all[:, P:T], 1.0).then_inc(mask_ready.sem, 1)
                pool.memset(v_pad[:], 0.0).then_inc(ready.sem, 1)

            @block.tensor
            def _(pe):
                def mm(out, lhsT, rhs, start=True, stop=True, **k):
                    return pe.matmul(out, lhsT, rhs, start=start, stop=stop, **k)

                def turn_x():
                    for k in range(2):
                        ins = pe.transpose(FR[:, 128 * k:128 * k + 128], xhat[:, k, :], sh.c("ident"))
                    ins.then_inc(xT_ps.sem, 1)

                def project_qk():
                    mm(QK[:, 0:T], w["C_wqT"], xT[:])
                    mm(QK[:, T:2 * T], w["C_wkT"], xT[:]).then_inc(qk_ps.sem, 1)

                def project_v():
                    for k in range(2):
                        ins = mm(FR[:, T + 128 * k:T + 128 * k + 128], xT[:, 128 * k:128 * k + 128], w["C_wvT"])
                    ins.then_inc(v_ps.sem, 1)

                pe.wait_ge(xhat_ready.sem, 1)
                turn_x()
                pe.wait_ge(xT_sb.sem, 1)
                project_qk()
                project_v()
                pe.wait_ge(mask_ready.sem, 1)
                with pe.Fori(0, NS) as i:

                    def scores(u):
                        k, jp = u // 2, u % 2
                        if u < 2:
                            pe.wait_ge(masked.sem, masked.last(i, u + 3))
                        else:
                            pe.wait_ge(masked.sem, masked.now(i, u - 1))
                        t = slice(128 * k, 128 * k + 128)
                        for j in (2 * jp, 2 * jp + 1):
                            for r in range(4):
                                c0 = 512 * j + 128 * r
                                ins = mm(S[:, c0:c0 + 128], f[32 * j:32 * j + 32, T + 128 * k:T + 128 * k + 128], q_h[32 * j:32 * j + 32, r, t])
                        ins.then_inc(scored.sem, 1)

                    def values(u):
                        pe.wait_ge(masked.sem, masked.now(i, u + 1))
                        k, jp = u // 2, u % 2
                        if u == 0:
                            pe.wait_ge(y_ready.sem, y_ready.last(i))
                        if u == 2:
                            mm(O[:, 128:256], state[:], f[:, 128:256], stop=False, skip_group_check=True)
                        for b in range(8):
                            h = 8 * jp + b
                            ins = mm(O[:, 128 * k:128 * k + 128], v_pad[:, k, P * h:P * h + P], A[:, u % 2, 128 * b:128 * b + 128],
                                     start=(h == 0 and k == 0), stop=(h == NH - 1), skip_group_check=True)
                        ins.then_inc(summed.sem, 1)

                    pe.wait_ge(f_ready.sem, f_ready.now(i))
                    for k in range(2):
                        ins = pe.transpose(QK[:, 128 * k:128 * k + 128], f[:, T + 128 * k:T + 128 * k + 128], sh.c("ident"))
                    ins.then_inc(kt_ps.sem, 1)
                    pe.wait_ge(q_ready.sem, q_ready.now(i))
                    scores(0)
                    scores(1)
                    pe.wait_ge(kt_sb.sem, kt_sb.now(i))
                    pe.wait_ge(v_sb.sem, v_sb.now(i))
                    mm(QK[:, 0:128], k_t[:, 0:128], v_cols[:, 0])
                    mm(QK[:, T:T + 128], k_t[:, 0:128], upto_all[:, 0:128])
                    mm(QK[:, T + 128:2 * T], k_t[:, 0:128], upto_all[:, 128:256], stop=False)
                    mm(QK[:, T + 128:2 * T], k_t[:, 128:256], upto_all[:, 0:128], start=False).then_inc(state_ps.sem, 1)
                    values(0)
                    scores(2)
                    values(1)
                    scores(3)
                    pe.wait_ge(state_sb.sem, state_sb.now(i))
                    pe.wait_ge(out_read.sem, out_read.last(i))
                    mm(Y[:, 0:T], sh.c("same_head8"), qk[:]).then_inc(den_ps.sem, 1)
                    pe.wait_ge(xhat_ready.sem, i + 2)
                    turn_x()
                    values(2)
                    pe.wait_ge(xT_sb.sem, i + 2)
                    project_qk()
                    values(3)
                    project_v()
                    pe.wait_ge(y_ready.sem, y_ready.now(i))
                    for k in range(2):
                        ins = mm(Y[:, 128 * k:128 * k + 128], y[:, 128 * k:128 * k + 128], w["C_woT"])
                    ins.then_inc(out_ps.sem, 1)

            @block.scalar
            def _(act):
                def take_x():
                    act.copy(xT[:], FR[:, 0:T]).then_inc(xT_sb.sem, 1)

                def elu_inputs(n):
                    act.wait_ge(qk_ps.sem, n)
                    act.activation(neg[:], QK[:], ACT.Relu, scale=-1.0).then_inc(neg_ready.sem, 1)
                    act.wait_ge(neg_ready.sem, n)
                    act.activation(e[:], neg[:], ACT.Exp, scale=-1.0).then_inc(elu_in.sem, 1)

                act.wait_ge(xT_ps.sem, 1)
                take_x()
                elu_inputs(1)
                act.wait_ge(ready.sem, 1)
                with act.Fori(0, NS) as i:
                    act.wait_ge(v_ps.sem, v_ps.now(i))
                    act.wait_ge(summed.sem, summed.last(i))
                    act.copy(v_cols, FR[:, T:2 * T].rearrange("p (a h d) -> p a h d", a=2, h=NH)).then_inc(v_sb.sem, 1)
                    act.wait_ge(kt_ps.sem, kt_ps.now(i))
                    act.copy(k_t[:], QK[:, 0:T]).then_inc(kt_sb.sem, 1)
                    act.wait_ge(xT_ps.sem, i + 2)
                    take_x()
                    act.wait_ge(f_ready.sem, f_ready.now(i))
                    elu_inputs(i + 2)

            @block.vector
            def _(vec):
                c = Chain(vec, ch)

                def features(n):
                    vec.wait_ge(elu_in.sem, n)
                    vec.scalar_tensor_tensor(f[:], QK[:], 0.0, e[:], ALU.max, ALU.add).then_inc(f_ready.sem, 1)
                    vec.wait_ge(f_ready.sem, n)
                    for r in range(4):
                        ins = vec.tensor_scalar(q_h[:, r, :], f[:, 0:T], sh.c("head_rows")[:, r:r + 1], None, ALU.mult)
                    ins.then_inc(q_ready.sem, 1)

                front_vector(sh, st, vec, c, 0, xhat).then_inc(xhat_ready.sem, 1)
                features(1)
                with vec.Fori(0, NS) as i:
                    c.restart()
                    vec.wait_ge(out_read.sem, out_read.last(i))
                    for u in range(4):
                        vec.wait_ge(scored.sem, scored.now(i, u + 1))
                        if u < 2:
                            vec.wait_ge(summed.sem, summed.last(i, u + 3))
                        else:
                            vec.wait_ge(summed.sem, summed.now(i, u - 1))
                        vec.tensor_tensor(A[:, u % 2, :].rearrange("p (b t) -> p b t", b=8),
                                          S[:, 1024 * (u % 2):1024 * (u % 2) + 1024].rearrange("p (b t) -> p b t", b=8),
                                          sh.c("upto_f").unsqueeze(1).broadcast_to([P, 8, P]), ALU.mult).then_inc(masked.sem, 1)
                        if u == 1:
                            vec.wait_ge(state_ps.sem, state_ps.now(i))
                            vec.tensor_tensor(state[:], QK[:, 0:P], sh.c("same_head8"), ALU.mult)
                            vec.tensor_tensor(qk[:], QK[:, T:2 * T], f[:, 0:T], ALU.mult).then_inc(state_sb.sem, 1)
                            vec.wait_ge(xT_ps.sem, xT_ps.now(i))
                            front_vector(sh, st, vec, c, i + 1, xhat).then_inc(xhat_ready.sem, 1)
                    vec.wait_ge(den_ps.sem, den_ps.now(i))
                    c.link(vec.tensor_scalar(den[:], Y[:, 0:T], EPS, None, ALU.add))
                    vec.reciprocal(den[:], den[:]).then_inc(den_read.sem, 1)
                    vec.wait_ge(summed.sem, summed.now(i, 3))
                    features(i + 2)
                    vec.wait_ge(den_read.sem, den_read.now(i))
                    vec.wait_ge(summed.sem, summed.now(i))
                    vec.tensor_tensor(y[:], O[:, 0:T], den[:], ALU.mult).then_inc(y_ready.sem, 1)
                    vec.wait_ge(out_ps.sem, out_ps.now(i))
                    residual(sh, vec, c, i, Y[:, 0:T].rearrange("p (a b) -> p a b", a=2), out_read)


def linear_attention_large(sh, w):
    nc, NH, HS, NS = sh.nc, 16, 64, sh.seqs
    NU = NH // 2
    EPS = 1e-6
    V1 = HS + 1
    with Stage(nc, "large") as st:
        wqp, wkp = st.sb("wqp", [P, NH * HS]), st.sb("wkp", [P, NH * HS])
        xhat, xT = st.sb("xhat", [P, 2, P]), st.sb("xT", [P, T])
        e, neg, f = st.sb("e", [P, 2, 2 * T]), st.sb("neg", [P, 2, 2 * T]), st.sb("f", [P, 2, 2 * T])
        v1 = st.sb("v1", [P, 2, NH, V1])
        A, mask3 = st.sb("A", [P, 2, 2, 3 * P]), st.sb("mask3", [P, 3, P])
        den, y, yT = st.sb("den", [P, 2, 4]), st.sb("y", [P, 2, 2, 2, HS]), st.sb("yT", [P, 2, T])
        S = st.ps("scores", 2048)
        QK, O, YT, Y = (st.ps(n, 512) for n in ("qk_ps", "o_ps", "yT_ps", "y_ps"))

        ch = st.chain()
        ready = st.semaphore("ready", 1)
        prep, prep_sb = st.semaphore("prep", 1), st.semaphore("prep_sb", 1)
        xhat_ready = st.semaphore("xhat_ready", 1)
        xT_ps, xT_sb = st.semaphore("xT_ps", 1), st.semaphore("xT_sb", 1)
        v_ps, v_sb = st.semaphore("v_ps", 4), st.semaphore("v_sb", 4, True)
        qk_ps = st.semaphore("qk_ps", NU)
        neg_ready = st.semaphore("neg_ready", NU)
        elu_in, f_ready = st.semaphore("elu_in", NU), st.semaphore("f_ready", NU, True)
        scored, masked, summed = st.semaphore("scored", NU, True), st.semaphore("masked", NU, True), st.semaphore("summed", NU, True)
        y_ready, turned, turned_sb = st.semaphore("y_ready", NU, True), st.semaphore("turned", NU, True), st.semaphore("turned_sb", NU, True)
        projected = st.semaphore("projected", NU, True)
        out_read = st.semaphore("out_read", 1, True)

        with nc.Block() as block:
            def prev(eng, sig, i, m):
                if m > 0:
                    eng.wait_ge(sig.sem, sig.now(i, m))
                else:
                    eng.wait_ge(sig.sem, sig.last(i, m + sig.per))

            @block.gpsimd
            def _(pool):
                st.give_credits(pool)
                pool.memset(v1[:, :, :, HS:V1], 1.0)
                pool.memset(mask3[:, 1, :], 1.0)
                pool.tensor_copy(mask3[:, 0, :], sh.c("upto_f"))
                pool.tensor_copy(mask3[:, 2, :], sh.c("upto_f")).then_inc(ready.sem, 1)

            @block.tensor
            def _(pe):
                def mm(out, lhsT, rhs, start=True, stop=True, **k):
                    return pe.matmul(out, lhsT, rhs, start=start, stop=stop, **k)

                for n, wt in enumerate((w["E_wqT"], w["E_wkT"])):
                    for h in range(NH):
                        ins = mm(S[:, 1024 * n + HS * h:1024 * n + HS * h + HS], wt[:, P * h:P * h + P], w["E_proj"])
                ins.then_inc(prep.sem, 1)
                pe.wait_ge(prep_sb.sem, 1)
                pe.wait_ge(ready.sem, 1)

                def turn_x():
                    for k in range(2):
                        ins = pe.transpose(QK[:, 128 * k:128 * k + 128], xhat[:, k, :], sh.c("ident"))
                    ins.then_inc(xT_ps.sem, 1)

                def project(i, p):
                    prev(pe, f_ready, i, p)
                    c = slice(P * (p % NU), P * (p % NU) + P)
                    mm(QK[:, 0:T], wqp[:, c], xT[:])
                    mm(QK[:, T:2 * T], wkp[:, c], xT[:]).then_inc(qk_ps.sem, 1)

                pe.wait_ge(xhat_ready.sem, 1)
                turn_x()
                pe.wait_ge(xT_sb.sem, 1)
                project(0, 0)
                with pe.Fori(0, NS) as i:
                    def values_of(n):
                        if n >= 2:
                            pe.wait_ge(v_sb.sem, v_sb.now(i, n - 1))
                        else:
                            prev(pe, (y_ready, turned_sb)[n], i, 0)
                        mm((O, YT)[n % 2][:], xT[:, 128 * (n // 2):128 * (n // 2) + 128], w["E_wv"][:, 512 * (n % 2):512 * (n % 2) + 512]).then_inc(v_ps.sem, 1)

                    def scores(p):
                        pe.wait_ge(f_ready.sem, f_ready.now(i, p + 1))
                        prev(pe, masked, i, p - 1)
                        for a in range(2):
                            b, r = 1024 * (p % 2) + 512 * a, slice(64 * a, 64 * a + 64)
                            mm(S[:, b:b + 256], f[r, p % 2, T:T + 128], f[r, p % 2, 0:T])
                            ins = mm(S[:, b + 256:b + 384], f[r, p % 2, T + 128:2 * T], f[r, p % 2, 128:T])
                        ins.then_inc(scored.sem, 1)

                    def values(p):
                        pe.wait_ge(masked.sem, masked.now(i, p + 1))
                        if p == 0:
                            pe.wait_ge(v_sb.sem, v_sb.now(i))
                        prev(pe, y_ready, i, p)
                        for a in range(2):
                            h = 2 * p + a
                            mm(O[:, V1 * a:V1 * a + V1], A[:, p % 2, a, 0:128], v1[:, 0, h, :])
                            o = O[:, V1 * (2 + a):V1 * (2 + a) + V1]
                            mm(o, A[:, p % 2, a, 128:256], v1[:, 0, h, :], stop=False)
                            ins = mm(o, A[:, p % 2, a, 256:384], v1[:, 1, h, :], start=False)
                        ins.then_inc(summed.sem, 1)

                    def turn(p):
                        pe.wait_ge(y_ready.sem, y_ready.now(i, p + 1))
                        if p == 0:
                            pe.wait_ge(v_sb.sem, v_sb.now(i))
                        prev(pe, turned_sb, i, p)
                        for k in range(2):
                            ins = pe.transpose(YT[:, 128 * k:128 * k + 128], y[:, p % 2, k].rearrange("p a d -> p (a d)"), sh.c("ident"))
                        ins.then_inc(turned.sem, 1)

                    def out_of(p):
                        pe.wait_ge(turned_sb.sem, turned_sb.now(i, p + 1))
                        if p == 0:
                            pe.wait_ge(out_read.sem, out_read.last(i))
                        for k in range(2):
                            ins = mm(Y[:, 128 * k:128 * k + 128], yT[:, p % 2, 128 * k:128 * k + 128], w["E_wo"][:, P * p:P * p + P],
                                     start=(p == 0 and k == 0), stop=(p == NU - 1), skip_group_check=True)
                        ins.then_inc(projected.sem, 1)

                    for n in range(2):
                        values_of(n)
                    for p in range(NU + 3):
                        if p + 1 < NU:
                            project(i, p + 1)
                        if p < NU:
                            scores(p)
                        if p == 0:
                            for n in range(2, 4):
                                values_of(n)
                        if p == NU:
                            pe.wait_ge(f_ready.sem, f_ready.now(i))
                            pe.wait_ge(xhat_ready.sem, i + 2)
                            turn_x()
                        if 1 <= p <= NU:
                            values(p - 1)
                        if 2 <= p <= NU + 1:
                            turn(p - 2)
                        if p == NU + 1:
                            pe.wait_ge(xT_sb.sem, i + 2)
                            project(i, NU)
                        if 3 <= p <= NU + 2:
                            out_of(p - 3)

            @block.scalar
            def _(act):
                act.wait_ge(prep.sem, 1)
                act.copy(wqp[:], S[:, 0:1024])
                act.copy(wkp[:], S[:, 1024:2048]).then_inc(prep_sb.sem, 1)

                def take_x():
                    act.copy(xT[:], QK[:, 0:T]).then_inc(xT_sb.sem, 1)

                def elu_inputs(i, p):
                    act.wait_ge(qk_ps.sem, qk_ps.now(i, p + 1))
                    prev(act, f_ready, i, p - 1)
                    act.activation(neg[:, p % 2, :], QK[:], ACT.Relu, scale=-1.0).then_inc(neg_ready.sem, 1)
                    act.wait_ge(neg_ready.sem, neg_ready.now(i, p + 1))
                    act.activation(e[:, p % 2, :], neg[:, p % 2, :], ACT.Exp, scale=-1.0).then_inc(elu_in.sem, 1)

                act.wait_ge(xT_ps.sem, 1)
                take_x()
                elu_inputs(0, 0)
                with act.Fori(0, NS) as i:
                    def turned_copy(p):
                        act.wait_ge(turned.sem, turned.now(i, p + 1))
                        prev(act, projected, i, p - 1)
                        act.copy(yT[:, p % 2, :], YT[:, 0:T]).then_inc(turned_sb.sem, 1)

                    def take_v(n):
                        act.wait_ge(v_ps.sem, v_ps.now(i, n + 1))
                        act.copy(v1[:, n // 2, 8 * (n % 2):8 * (n % 2) + 8, 0:HS], (O, YT)[n % 2][:].rearrange("p (h d) -> p h d", h=8)).then_inc(v_sb.sem, 1)

                    act.wait_ge(summed.sem, summed.last(i))
                    for n in range(2):
                        take_v(n)
                    for p in range(NU + 2):
                        if p + 1 < NU:
                            elu_inputs(i, p + 1)
                        if p == 0:
                            for n in range(2, 4):
                                take_v(n)
                        if p == NU:
                            act.wait_ge(xT_ps.sem, i + 2)
                            act.wait_ge(qk_ps.sem, qk_ps.now(i))
                            take_x()
                        if p >= 2:
                            turned_copy(p - 2)
                        if p == NU + 1:
                            elu_inputs(i, NU)

            @block.vector
            def _(vec):
                c = Chain(vec, ch)

                def features(i, p):
                    vec.wait_ge(elu_in.sem, elu_in.now(i, p + 1))
                    prev(vec, scored, i, p - 1)
                    vec.scalar_tensor_tensor(f[:, p % 2, :], QK[:], 0.0, e[:, p % 2, :], ALU.max, ALU.add).then_inc(f_ready.sem, 1)

                front_vector(sh, st, vec, c, 0, xhat).then_inc(xhat_ready.sem, 1)
                features(0, 0)
                with vec.Fori(0, NS) as i:
                    c.restart()
                    vec.wait_ge(out_read.sem, out_read.last(i))

                    def mask(p):
                        vec.wait_ge(scored.sem, scored.now(i, p + 1))
                        prev(vec, summed, i, p - 1)
                        vec.tensor_tensor(A[:, p % 2].rearrange("p a (b t) -> p a b t", b=3),
                                          S[:, 1024 * (p % 2):1024 * (p % 2) + 1024].rearrange("p (a b t) -> p a b t", a=2, b=4)[:, :, 0:3, :],
                                          mask3[:].unsqueeze(1).broadcast_to([P, 2, 3, P]), ALU.mult).then_inc(masked.sem, 1)

                    def normalise(p):
                        vec.wait_ge(summed.sem, summed.now(i, p + 1))
                        o = O[:, 0:4 * V1].rearrange("p (b d) -> p b d", b=4)
                        c.link(vec.tensor_scalar(den[:, p % 2, :], o[:, :, HS], EPS, None, ALU.add))
                        c.link(vec.reciprocal(den[:, p % 2, :], den[:, p % 2, :]))
                        prev(vec, turned, i, p - 1)
                        vec.tensor_tensor(y[:, p % 2].rearrange("p k a d -> p (k a) d"), o[:, :, 0:HS],
                                          den[:, p % 2, :].unsqueeze(2).broadcast_to([P, 4, HS]), ALU.mult).then_inc(y_ready.sem, 1)

                    for p in range(NU + 1):
                        if p + 1 < NU:
                            features(i, p + 1)
                        if p < NU:
                            mask(p)
                        if p >= 1:
                            normalise(p - 1)
                        if p == 1:
                            vec.wait_ge(xT_ps.sem, xT_ps.now(i))
                            front_vector(sh, st, vec, c, i + 1, xhat).then_inc(xhat_ready.sem, 1)
                    features(i, NU)
                    vec.wait_ge(projected.sem, projected.now(i))
                    residual(sh, vec, c, i, Y[:, 0:T].rearrange("p (a b) -> p a b", a=2), out_read)


def expert_choice_ffn(sh, w, name):
    nc, NE, NS = sh.nc, 8, sh.seqs
    KEEP = 2 * T // NE
    HC = 4
    turns = NS // 2
    rows = min(16, NS) * NE
    groups = NS * NE // rows
    per_group = rows // NE
    with ExitStack() as ctx:
        p_pad = ctx.enter_context(nc.sbuf_tensor(f"{name}_p_all", [P, sh.tiles + PAD, NE], F32))
        slot_pad = ctx.enter_context(nc.sbuf_tensor(f"{name}_slot_all", [P, sh.tiles + PAD, NE], F32))
        p_all, slot_all = p_pad[:, 0:sh.tiles, :], slot_pad[:, 0:sh.tiles, :]
        gate(sh, name + "_gate", w["F_gate"], p_all, None)
        softmax8(sh, name + "_probs", p_all)

        with Stage(nc, name + "_pick") as st:
            pT = st.sb("pT", [rows, groups, T])
            best = st.sb("best", [rows, groups, KEEP])
            slots, one = st.sb("slots", [rows, groups, T]), st.sb("one", [rows, T])
            PT, ST = st.ps("pT_ps", groups * T), st.ps("slots_ps", 1024)
            pk = st.sb("pk", [P, 2, NS * NE])
            ch, split = st.chain(), st.semaphore("split", 1)
            turned, turned_sb = st.semaphore("turned", 1), st.semaphore("turned_sb", 1)
            placed, back = st.semaphore("placed", 1), st.semaphore("back", 1)

            def by_tile(a, g, k):
                v = a[:].rearrange("p (s k) e -> p s k e", k=2)
                return v[:, g * per_group:(g + 1) * per_group, k, :]

            with nc.Block() as block:
                @block.tensor
                def _(pe):
                    pe.wait_ge(split.sem, 1)
                    for g in range(groups):
                        for k in range(2):
                            c0 = g * T + 128 * k
                            ins = pe.transpose(PT[0:rows, c0:c0 + 128], pk[:, k, g * rows:(g + 1) * rows], sh.c("ident"))
                    ins.then_inc(turned.sem, 1)
                    pe.wait_ge(placed.sem, 1)
                    for g in range(groups):
                        for k in range(2):
                            c0 = (2 * g + k) * rows
                            ins = pe.transpose(ST[:, c0:c0 + rows], slots[:, g, 128 * k:128 * k + 128], sh.c("ident")[0:rows, 0:rows])
                    ins.then_inc(back.sem, 1)

                @block.scalar
                def _(act):
                    act.wait_ge(turned.sem, 1)
                    act.copy(pT[:].rearrange("p g t -> p (g t)"), PT[0:rows, :]).then_inc(turned_sb.sem, 1)

                @block.vector
                def _(vec):
                    c = Chain(vec, ch)
                    vec.memset(one[:], 1.0)
                    vec.memset(p_pad[:, sh.tiles:, :], 0.0)
                    vec.memset(slot_pad[:, sh.tiles:, :], 0.0)
                    vec.tensor_copy(pk[:].rearrange("p k (s e) -> p s k e", e=NE), p_all[:].rearrange("p (s k) e -> p s k e", k=2)).then_inc(split.sem, 1)
                    vec.wait_ge(turned_sb.sem, 1)
                    for r in range(KEEP // 8):
                        for g in range(groups):
                            m = c.mark(vec.max(best[:, g, 8 * r:8 * r + 8], pT[:, g, :]))
                        for g in range(groups):
                            c.need(m - groups + 1 + g)
                            m2 = c.mark(vec.match_replace(pT[:, g, :], best[:, g, 8 * r:8 * r + 8], pT[:, g, :], -1.0))
                        c.need(m2)
                    c.link(vec.tensor_scalar(pT[:], pT[:], 0.0, None, ALU.is_lt))
                    for g in range(groups):
                        m = c.mark(vec.tensor_tensor_scan(slots[:, g, :], one[:], pT[:, g, :], 0.0, ALU.mult, ALU.add))
                    c.need(m)
                    vec.tensor_tensor(slots[:], slots[:], pT[:], ALU.mult).then_inc(placed.sem, 1)
                    vec.wait_ge(back.sem, 1)
                    for g in range(groups):
                        for k in range(2):
                            c0 = (2 * g + k) * rows
                            vec.tensor_copy(by_tile(slot_all, g, k), ST[:, c0:c0 + rows].rearrange("p (s e) -> p s e", e=NE))

        with Stage(nc, name) as st:
            xhat = st.sb("xhat", [P, 4, P])
            sel, selp = st.sb("sel", [P, 4, NE, KEEP]), st.sb("selp", [P, 2, NE, 2, KEEP])
            xin = st.sb("xin", [P, 2, NE, KEEP])
            selT, h = st.sb("selT", [P, 3, T]), st.sb("h", [P, 2, HC * P])
            yd = st.sb("yd", [P, 3, D])
            ob = st.sb("ob", [P, 4, D], BF16)
            G, TR = st.ps("gather_ps", 512), st.ps("selT_ps", 512)
            H = [st.ps("h0_ps", 512), st.ps("h1_ps", 512)]
            Y = [st.ps("y0_ps", 512), st.ps("y1_ps", 512)]
            O = [st.ps("o0_ps", 512), st.ps("o1_ps", 512)]
            ch = st.chain()
            sel_ready, selp_ready = st.semaphore("sel_ready", 1), st.semaphore("selp_ready", 1)
            gathered, gathered_sb = st.semaphore("gathered", 2), st.semaphore("gathered_sb", 2)
            up, gelu_done = st.semaphore("up", NE, True), st.semaphore("gelu_done", NE, True)
            down, down_sb = st.semaphore("down", NE, True), st.semaphore("down_sb", NE, True)
            turned, turned_sb = st.semaphore("turned", NE, True), st.semaphore("turned_sb", NE, True)
            scattered = st.semaphore("scattered", NE, True)
            rounded, out_read = st.semaphore("rounded", 1, True), st.semaphore("out_read", 1, True)

            def prev(eng, sig, i, m):
                if m > 0:
                    eng.wait_ge(sig.sem, sig.now(i, m))
                else:
                    eng.wait_ge(sig.sem, sig.last(i, m + sig.per))

            with nc.Block() as block:

                @block.gpsimd
                def _(pool):
                    st.give_credits(pool)

                @block.tensor
                def _(pe):
                    def gather(s):
                        for k in range(2):
                            ins = pe.matmul(G[:], xhat[:, 2 * s + k, :], sel[:, 2 * s + k].rearrange("p e c -> p (e c)"),
                                            start=(k == 0), stop=(k == 1))
                        ins.then_inc(gathered.sem, 1)

                    pe.wait_ge(sel_ready.sem, 1)
                    gather(0)
                    pe.wait_ge(gathered_sb.sem, 1)
                    gather(1)
                    with pe.Fori(0, turns) as i:
                        pe.wait_ge(gathered_sb.sem, gathered_sb.now(i))
                        pe.wait_ge(selp_ready.sem, selp_ready.now(i))

                        def expand(e):
                            prev(pe, gelu_done, i, e - 1)
                            for m in range(HC):
                                w0 = (e * HC + m) * P
                                ins = pe.matmul(H[e % 2][:, P * m:P * m + P], w["F_w1"][:, w0:w0 + P], xin[:, :, e, :], start=True, stop=True)
                            ins.then_inc(up.sem, 1)

                        def turn(e):
                            prev(pe, turned_sb, i, e)
                            for k in range(2):
                                ins = pe.transpose(TR[:, P * k:P * k + P], selp[:, k, e].rearrange("p s c -> p (s c)"), sh.c("ident"))
                            ins.then_inc(turned.sem, 1)

                        def contract(e):
                            pe.wait_ge(gelu_done.sem, gelu_done.now(i, e + 1))
                            prev(pe, down_sb, i, e - 1)
                            for m in range(HC):
                                w0 = (e * HC + m) * P
                                ins = pe.matmul(Y[e % 2][:, 0:D], h[:, e % 2, P * m:P * m + P], w["F_w2"][:, w0:w0 + P], start=(m == 0), stop=(m == HC - 1))
                            ins.then_inc(down.sem, 1)

                        def scatter(e):
                            pe.wait_ge(down_sb.sem, down_sb.now(i, e + 1))
                            pe.wait_ge(turned_sb.sem, turned_sb.now(i, e + 1))
                            if e == 0:
                                pe.wait_ge(rounded.sem, rounded.last(i))
                            for k in range(2):
                                for s in range(2):
                                    r = slice(64 * s, 64 * s + 64)
                                    ins = pe.matmul(O[s][:, P * k:P * k + P], selT[r, e % 3, P * k:P * k + P], yd[r, e % 3, :],
                                                    start=(e == 0 and k == 0), stop=(e == NE - 1), skip_group_check=True)
                            ins.then_inc(scattered.sem, 1)

                        for e in range(NE + 2):
                            if e < NE:
                                expand(e)
                                turn(e)
                            if e == NE - 1:
                                pe.wait_ge(sel_ready.sem, i + 2)
                                gather(0)
                            if e == NE:
                                pe.wait_ge(gathered_sb.sem, 2 * i + 3)
                                gather(1)
                            if 1 <= e <= NE:
                                contract(e - 1)
                            if e >= 2:
                                scatter(e - 2)

                @block.scalar
                def _(act):
                    def take(s):
                        act.copy(xin[:, s].rearrange("p e c -> p (e c)"), G[:]).then_inc(gathered_sb.sem, 1)

                    for s in range(2):
                        act.wait_ge(gathered.sem, s + 1)
                        take(s)
                    with act.Fori(0, turns) as i:
                        for e in range(NE):
                            act.wait_ge(up.sem, up.now(i, e + 1))
                            prev(act, down, i, e - 1)
                            act.activation(h[:, e % 2, :], H[e % 2][:], ACT.Gelu_apprx_tanh).then_inc(gelu_done.sem, 1)
                        for s in range(2):
                            act.wait_ge(gathered.sem, 2 * i + 3 + s)
                            take(s)
                        act.wait_ge(scattered.sem, scattered.now(i))
                        act.wait_ge(out_read.sem, out_read.last(i))
                        act.copy(ob[:, 0:2, :].rearrange("p k d -> p (k d)"), O[0][:, 0:T])
                        act.copy(ob[:, 2:4, :].rearrange("p k d -> p (k d)"), O[1][:, 0:T]).then_inc(rounded.sem, 1)

                @block.vector
                def _(vec):
                    c = Chain(vec, ch)
                    def normalise(i):
                        for k in range(4):
                            t = 4 * i + k
                            vec.tensor_scalar(xhat[:, k, :], sh.x[:, bass.ds(t, 1), :], sh.mean[:, bass.ds(t, 1)],
                                              sh.rstd[:, bass.ds(t, 1)], ALU.subtract, ALU.mult)

                    def spread(a, t):
                        return a[:, bass.ds(t, 1), :].rearrange("p a e -> p (a e)").unsqueeze(2).broadcast_to([P, NE, KEEP])

                    def select(i, k):
                        return vec.tensor_tensor(sel[:, k], sh.c("iota").unsqueeze(1).broadcast_to([P, NE, KEEP]), spread(slot_pad, 4 * i + k), ALU.is_equal)

                    def weigh(i):
                        for k in range(4):
                            ins = vec.tensor_tensor(selp[:, k % 2, :, k // 2, :], sel[:, k], spread(p_pad, 4 * i + k), ALU.mult)
                        ins.then_inc(selp_ready.sem, 1)

                    normalise(0)
                    for k in range(4):
                        ins = select(0, k)
                    ins.then_inc(sel_ready.sem, 1)
                    vec.wait_ge(sel_ready.sem, 1)
                    weigh(0)
                    with vec.Fori(0, turns) as i:
                        c.restart()
                        vec.wait_ge(out_read.sem, out_read.last(i))
                        for e in range(NE + 1):
                            if e < NE:
                                vec.wait_ge(turned.sem, turned.now(i, e + 1))
                                prev(vec, scattered, i, e - 2)
                                vec.tensor_copy(selT[:, e % 3, :], TR[:, 0:T]).then_inc(turned_sb.sem, 1)
                            if e == 1:
                                vec.wait_ge(gathered.sem, gathered.now(i))
                                vec.wait_ge(selp_ready.sem, selp_ready.now(i))
                                normalise(i + 1)
                            if 2 <= e < 6:
                                ins = select(i + 1, e - 2)
                                if e == 5:
                                    ins.then_inc(sel_ready.sem, 1)
                            if e:
                                vec.wait_ge(down.sem, down.now(i, e))
                                prev(vec, scattered, i, e - 3)
                                vec.tensor_copy(yd[:, (e - 1) % 3, :], Y[(e - 1) % 2][:, 0:D]).then_inc(down_sb.sem, 1)
                        vec.wait_ge(sel_ready.sem, i + 2)
                        weigh(i + 1)
                        vec.wait_ge(rounded.sem, rounded.now(i))
                        for s in range(2):
                            residual(sh, vec, c, 2 * i + s, ob[:, 2 * s:2 * s + 2, :], out_read if s else None)


def expert_choice_ffn_first(sh, w):
    expert_choice_ffn(sh, w, "ffn_f")


def expert_choice_ffn_second(sh, w):
    expert_choice_ffn(sh, w, "ffn_h")


def delta_rule_mixer(sh, w):
    nc, NH, HS, NS = sh.nc, 4, 32, sh.seqs
    TAPS, LOCAL, MID = 4, 7, 25
    NF, RH = 14 * NH, 2 * (D + 14 * NH)
    NFW = 80
    FLOOR, EPS = 0.01, 1e-5
    RC = [(0, 128), (128, 256), (256, RH)]
    LEVELS = (2, 4, 8, 16, 32, 64)
    with Stage(nc, "delta") as st:
        wtap = st.sb("wtap", [P, 3, TAPS, P])
        diag = st.sb("diag", [P, MID, P])
        half = st.sb("half", [P, 16])
        ch = st.chain()
        prep, prep_sb, ready = (st.semaphore(n, 1) for n in ("prep", "prep_sb", "ready"))

        class Lane:

            def __init__(self, q):
                def sb(name, shape):
                    return st.sb(f"{name}{q}", shape)

                def sem(name, per=1, credit=False):
                    return st.semaphore(f"{name}{q}", per, credit)

                self.q = q
                self.xhat, self.xT = sb("xhat", [P, 2, P]), sb("xT", [P, TAPS - 1 + T])
                self.qk_f, self.v_f = sb("qk_f", [P, 2 * T]), sb("v_f", [P, MID - 1 + T])
                self.beta = sb("beta", [P, 2, NH])
                self.loc_f, self.mid_f = sb("loc_f", [P, T]), sb("mid_f", [P, T])
                self.qk_t = sb("qk_t", [P, 2, 2, P])
                self.ss, self.rn = sb("ss", [P, 16]), sb("rn", [P, 16])
                self.nkb, self.vb = sb("nkb", [P, 2, P]), sb("vb", [P, 2, P])
                self.qkn_T = sb("qkn_T", [P, 3, T])
                self.A, self.At = sb("A", [P, 8 * P]), sb("At", [P, 8 * P])
                TUQ = sb("TUQ", [P, 3, 8 * P])
                self.Tm, self.Um, self.Q = TUQ[:, 0], TUQ[:, 1], TUQ[:, 2]
                self.u, self.S = sb("u", [P, 2, P]), sb("S", [P, P])
                self.outs = sb("outs", [P, 2, 4, P])
                self.sq = self.Q[:, 0:512]
                self.prod = self.A[:, 0:6 * P].rearrange("p (n d) -> p n d", n=6)
                self.prod2 = self.Q[:, 0:6 * P].rearrange("p (n d) -> p n d", n=6)
                self.sqo = self.Um.rearrange("p (k n d) -> p k n d", k=2, n=4)
                self.h1 = self.At[:, 0:3 * T].rearrange("p (n t) -> p n t", n=3)
                self.feats, self.mm2 = sb("feats", [P, 2, NFW]), sb("mm2", [P, 2, 16])
                self.featsT = sb("featsT", [NF, T])
                self.lg, self.lm = sb("lg", [P, 2, NH, 4]), sb("lm", [P, 2, NH])
                self.mixed, self.sqm = sb("mixed", [P, 2, P]), sb("sqm", [P, 2, P])
                self.rm, self.rr = sb("rm", [P, 8]), sb("rr", [P, 8])
                self.oT, self.xR = sb("oT", [P, T]), sb("xR", [P, T])
                self.ps = st.ps(f"banks{q}", 2048)
                self.B = [self.ps[:, 512 * b:512 * b + 512] for b in range(4)]
                self.out_read = sem("out_read", 1, True)
                (self.xhat_ready, self.xT_ps, self.xT_sb, self.qk_ps, self.v_ps, self.qk_sb, self.v_sb, self.beta_sb,
                 self.mid_ps, self.mid_sb, self.loc_sb, self.qk_turned, self.v_turned, self.mid_turned, self.qkt_sb,
                 self.v_t_sb, self.conv_sb, self.ss_ready, self.rn_ready, self.normed, self.normed_ps, self.normed_sb,
                 self.first_u, self.s_ps, self.s_sb, self.ks_ps, self.o_ps, self.o_sb, self.squared, self.feats_ready,
                 self.featsT_ps, self.featsT_sb, self.h1_ps, self.h1_sb, self.lg_ps, self.lg_shifted, self.lg_exp,
                 self.on_ready, self.oT_ps, self.oT_sb, self.out_ps, self.xR_sb) = (sem(n) for n in (
                     "xhat_ready xT_ps xT_sb qk_ps v_ps qk_sb v_sb beta_sb mid_ps mid_sb loc_sb qk_turned v_turned "
                     "mid_turned qkt_sb v_t_sb conv_sb ss_ready rn_ready normed normed_ps normed_sb first_u s_ps s_sb "
                     "ks_ps o_ps o_sb squared feats_ready featsT_ps featsT_sb h1_ps h1_sb lg_ps lg_shifted lg_exp "
                     "on_ready oT_ps oT_sb out_ps xR_sb").split())
                self.gram, self.gram_read, self.r_ready = sem("gram", 2), sem("gram_read", 2), sem("r_ready", 2)
                self.q_ps, self.q_sb = sem("q_ps", 6), sem("q_sb", 6)
                self.u_ps, self.u_sb = sem("u_ps", 6), sem("u_sb", 6)
                self.t_ps, self.t_sb = sem("t_ps", 6), sem("t_sb", 6)
                self.z_ps, self.z_sb = sem("z_ps", 2), sem("z_sb", 2)
                self.ms_ready, self.mr_ready = sem("ms_ready", 2), sem("mr_ready", 2)

        lanes = [Lane(0), Lane(1)]

        def heads(ap):
            return ap.rearrange("p k (h d) -> p (k h) d", h=NH)

        def spread(ap, n, m):
            return ap.unsqueeze(2).broadcast_to([P, n, m])

        def tiles2(ap):
            return ap.rearrange("p (k d) -> p k d", k=2)

        def col(n):
            return slice(P * n, P * n + P)

        def own(h):
            return slice(HS * h, HS * h + HS)

        with nc.Block() as block:

            @block.gpsimd
            def _(pool):
                st.give_credits(pool)
                pool.memset(half[:], -0.5)
                for L in lanes:
                    pool.memset(L.feats[:], 0.0)
                    pool.memset(L.xT[:, 0:TAPS - 1], 0.0)
                    ins = pool.memset(L.v_f[:, 0:MID - 1], 0.0)
                ins.then_inc(ready.sem, 1)
                pool.wait_ge(ready.sem, 1)

                def norm_powers(n):
                    for L in lanes:
                        pool.wait_ge(L.ss_ready.sem, n)
                        pool.tensor_tensor(L.rn[:], L.ss[:], half[:], ALU.pow).then_inc(L.rn_ready.sem, 1)

                norm_powers(1)
                with pool.Fori(0, NS // 2) as i:
                    for n in range(2):
                        for L in lanes:
                            pool.wait_ge(L.ms_ready.sem, L.ms_ready.now(i, n + 1))
                            pool.tensor_tensor(L.rr[:], L.rm[:], half[:, 0:8], ALU.pow).then_inc(L.mr_ready.sem, 1)
                        if n == 0:
                            norm_powers(i + 2)

            @block.tensor
            def _(pe):
                def mm(out, lhsT, rhs, start=True, stop=True, **k):
                    return pe.matmul(out, lhsT, rhs, start=start, stop=stop, **k)

                ident = sh.c("ident")
                for n in range(3):
                    for tau in range(TAPS):
                        ins = pe.transpose(lanes[0].B[n][:, col(tau)], w["G_conv"][:, TAPS * n + tau:TAPS * n + tau + 1].broadcast_to([P, P]), ident)
                ins.then_inc(prep.sem, 1)
                pe.wait_ge(prep_sb.sem, 1)
                pe.wait_ge(ready.sem, 1)

                def turn_x(L):
                    for k in range(2):
                        ins = pe.transpose(L.B[2][:, col(k)], L.xhat[:, k, :], ident)
                    ins.then_inc(L.xT_ps.sem, 1)

                def project(L):
                    for n, (b, c0) in ((2, (2, 0)), (0, (3, 0)), (1, (3, T))):
                        for tau in range(TAPS):
                            ins = mm(L.B[b][:, c0:c0 + T], wtap[:, n, tau, :], L.xT[:, tau:tau + T], start=(tau == 0), stop=(tau == TAPS - 1))
                        if n == 2:
                            for k in range(2):
                                t0 = TAPS - 1 + P * k
                                ins = mm(L.B[2][:, T + NH * k:T + NH * k + NH], L.xT[:, t0:t0 + P], w["G_wb"])
                            ins.then_inc(L.v_ps.sem, 1)
                    ins.then_inc(L.qk_ps.sem, 1)

                def project_lanes(n):
                    for L in lanes:
                        pe.wait_ge(L.xhat_ready.sem, n)
                        turn_x(L)
                    for L in lanes:
                        pe.wait_ge(L.xT_sb.sem, n)
                        project(L)

                def convolve_lanes(n):
                    for L in lanes:
                        pe.wait_ge(L.qk_sb.sem, n)
                        pe.wait_ge(L.beta_sb.sem, n)
                        for m in range(4):
                            ins = pe.transpose(L.B[2][:, col(m)], L.qk_f[:, col(m)], ident)
                        ins.then_inc(L.qk_turned.sem, 1)
                    for L in lanes:
                        pe.wait_ge(L.v_sb.sem, n)
                        for tau in range(MID):
                            ins = mm(L.B[3][:, 0:T], diag[:, tau, :], L.v_f[:, tau:tau + T], start=(tau == 0), stop=(tau == MID - 1))
                        ins.then_inc(L.mid_ps.sem, 1)

                project_lanes(1)
                convolve_lanes(1)
                with pe.Fori(0, NS // 2) as i:
                    for L in lanes:
                        pe.wait_ge(L.loc_sb.sem, L.loc_sb.now(i))
                        for k in range(2):
                            pe.transpose(L.B[1][:, col(k)], L.v_f[:, MID - 1 + P * k:MID - 1 + P * k + P], ident)
                            ins = pe.transpose(L.B[1][:, col(2 + k)], L.loc_f[:, col(k)], ident)
                        ins.then_inc(L.v_turned.sem, 1)
                    for L in lanes:
                        pe.wait_ge(L.mid_sb.sem, L.mid_sb.now(i))
                        pe.wait_ge(L.out_read.sem, L.out_read.last(i))
                        for k in range(2):
                            ins = pe.transpose(L.B[0][:, col(k)], L.mid_f[:, col(k)], ident)
                        ins.then_inc(L.mid_turned.sem, 1)
                        pe.wait_ge(L.normed.sem, L.normed.now(i))
                        for n in range(2):
                            for k in range(2):
                                pe.transpose(L.B[2][:, col(2 * n + k)], L.qk_t[:, n, k, :], ident)
                        for k in range(2):
                            ins = pe.transpose(L.B[3][:, col(k)], L.nkb[:, k, :], ident)
                        ins.then_inc(L.normed_ps.sem, 1)
                    for k in range(2):
                        for L in lanes:
                            if k:
                                pe.wait_ge(L.gram_read.sem, L.gram_read.now(i, 1))
                            else:
                                pe.wait_ge(L.normed_sb.sem, L.normed_sb.now(i))
                                pe.wait_ge(L.conv_sb.sem, L.conv_sb.now(i))
                            for h in range(NH):
                                q, kk, nk = (L.qkn_T[own(h), n, col(k)] for n in range(3))
                                mm(L.B[h][:, 0:P], nk, kk)
                                mm(L.B[h][:, P:2 * P], kk, nk)
                                ins = mm(L.B[h][:, 2 * P:3 * P], kk, q)
                            ins.then_inc(L.gram.sem, 1)
                    for lv in range(len(LEVELS)):
                        for L in lanes:
                            if lv:
                                pe.wait_ge(L.u_sb.sem, L.u_sb.now(i, lv))
                            else:
                                pe.wait_ge(L.gram_read.sem, L.gram_read.now(i))
                                pe.wait_ge(L.first_u.sem, L.first_u.now(i))
                            for n in range(8):
                                ins = mm(L.ps[:, col(n)], L.A[:, col(n)], L.Um[:, col(n)])
                            ins.then_inc(L.q_ps.sem, 1)
                            for n in range(8):
                                ins = pe.transpose(L.ps[:, col(8 + n)], L.Um[:, col(n)], ident)
                            ins.then_inc(L.t_ps.sem, 1)
                        for L in lanes:
                            pe.wait_ge(L.q_sb.sem, L.q_sb.now(i, lv + 1))
                            pe.wait_ge(L.t_sb.sem, L.t_sb.now(i, lv + 1))
                            for n in range(8):
                                ins = mm(L.ps[:, col(8 + n)], L.Tm[:, col(n)], L.Q[:, col(n)])
                            ins.then_inc(L.u_ps.sem, 1)
                    for k in range(2):
                        for L in lanes:
                            pe.wait_ge(L.u_sb.sem, L.u_sb.now(i))
                            pe.wait_ge(L.r_ready.sem, L.r_ready.now(i, k + 1))
                            for h in range(NH):
                                ins = mm(L.B[2][:, own(h)], L.Um[:, col(4 * k + h)], L.vb[:, k, own(h)])
                            ins.then_inc(L.z_ps.sem, 1)
                        if k == 0:
                            for L in lanes:
                                pe.wait_ge(L.z_sb.sem, L.z_sb.now(i, 1))
                                mm(L.B[2][:, 0:P], L.qk_t[:, 1, 0, :], L.u[:, 0, :]).then_inc(L.s_ps.sem, 1)
                            for L in lanes:
                                pe.wait_ge(L.s_sb.sem, L.s_sb.now(i))
                                mm(L.B[3][:, 0:P], L.qkn_T[:, 2, P:2 * P], L.S[:]).then_inc(L.ks_ps.sem, 1)
                        for L in lanes:
                            if k:
                                pe.wait_ge(L.z_sb.sem, L.z_sb.now(i))
                            for h in range(NH):
                                ins = mm(L.B[1][:, P * k + HS * h:P * k + HS * h + HS], L.At[:, col(4 * k + h)], L.u[:, k, own(h)],
                                         start=(h == 0), stop=(k == 0), skip_group_check=True)
                            if k:
                                mm(L.B[1][:, P:2 * P], L.qkn_T[:, 0, P:2 * P], L.S[:], start=False, skip_group_check=True).then_inc(L.o_ps.sem, 1)
                    project_lanes(i + 2)
                    for L in lanes:
                        pe.wait_ge(L.feats_ready.sem, L.feats_ready.now(i))
                        for k in range(2):
                            ins = pe.transpose(L.B[0][0:NFW, col(k)], L.feats[:, k, :], ident)
                        ins.then_inc(L.featsT_ps.sem, 1)
                    for L in lanes:
                        pe.wait_ge(L.featsT_sb.sem, L.featsT_sb.now(i))
                        pe.wait_ge(L.xR_sb.sem, L.xR_sb.now(i))
                        pe.wait_ge(L.qk_sb.sem, i + 2)
                        pe.wait_ge(L.beta_sb.sem, i + 2)
                        for n, (a, b) in enumerate(RC):
                            o = L.B[2 + n // 2][0:b - a, T * (n % 2):T * (n % 2) + T]
                            mm(o, w["G_rw1x"][:, a:b], L.xR[:], stop=False)
                            ins = mm(o, w["G_rw1f"][:, a:b], L.featsT[:], start=False)
                        ins.then_inc(L.h1_ps.sem, 1)
                    for L in lanes:
                        pe.wait_ge(L.h1_sb.sem, L.h1_sb.now(i))
                        for k in range(2):
                            o = L.B[1][:, 16 * k:16 * k + 16]
                            for n, (a, b) in enumerate(RC):
                                mm(o, L.h1[0:b - a, n, col(k)], w["G_rw2"][0:b - a, 16 * n:16 * n + 16], start=(n == 0), stop=False)
                            ins = mm(o, sh.c("ones128")[0:1, :], w["G_rb2"], start=False)
                        ins.then_inc(L.lg_ps.sem, 1)
                    convolve_lanes(i + 2)
                    for L in lanes:
                        pe.wait_ge(L.on_ready.sem, L.on_ready.now(i))
                        for k in range(2):
                            ins = pe.transpose(L.B[0][:, col(k)], L.mixed[:, k, :], ident)
                        ins.then_inc(L.oT_ps.sem, 1)
                    for L in lanes:
                        pe.wait_ge(L.oT_sb.sem, L.oT_sb.now(i))
                        for k in range(2):
                            ins = mm(L.B[0][:, col(2 + k)], L.oT[:, col(k)], w["G_wo"])
                        ins.then_inc(L.out_ps.sem, 1)

            @block.scalar
            def _(act):
                def take_x(L):
                    act.copy(L.xT[:, TAPS - 1:TAPS - 1 + T], L.B[2][:, 0:T]).then_inc(L.xT_sb.sem, 1)

                def take_projections(n):
                    for L in lanes:
                        act.wait_ge(L.v_ps.sem, n)
                        act.activation(L.v_f[:, MID - 1:MID - 1 + T], L.B[2][:, 0:T], ACT.Silu).then_inc(L.v_sb.sem, 1)
                        act.wait_ge(L.qk_ps.sem, n)
                        act.activation(L.qk_f[:], L.B[3][:], ACT.Silu).then_inc(L.qk_sb.sem, 1)
                    for L in lanes:
                        act.activation(L.beta[:].rearrange("p k h -> p (k h)"), L.B[2][:, T:T + 2 * NH], ACT.Sigmoid).then_inc(L.beta_sb.sem, 1)

                def take_qk(n):
                    for L in lanes:
                        act.wait_ge(L.qk_turned.sem, n)
                        act.copy(L.qk_t[:].rearrange("p n k d -> p (n k d)"), L.B[2][:]).then_inc(L.qkt_sb.sem, 1)

                def take_mid(n):
                    for L in lanes:
                        act.wait_ge(L.mid_ps.sem, n)
                        act.copy(L.mid_f[:], L.B[3][:, 0:T]).then_inc(L.mid_sb.sem, 1)

                for L in lanes:
                    act.wait_ge(L.xT_ps.sem, 1)
                    take_x(L)
                take_projections(1)
                take_qk(1)
                take_mid(1)
                with act.Fori(0, NS // 2) as i:
                    for L in lanes:
                        act.copy(L.xR[:], L.xT[:, TAPS - 1:TAPS - 1 + T]).then_inc(L.xR_sb.sem, 1)
                    for L in lanes:
                        act.wait_ge(L.v_turned.sem, L.v_turned.now(i))
                        act.copy(L.outs[:, :, 3, :], tiles2(L.B[1][:, 0:T]))
                        act.copy(L.outs[:, :, 0, :], tiles2(L.B[1][:, T:2 * T])).then_inc(L.v_t_sb.sem, 1)
                    for L in lanes:
                        act.wait_ge(L.mid_turned.sem, L.mid_turned.now(i))
                        act.copy(L.outs[:, :, 1, :], tiles2(L.B[0][:, 0:T])).then_inc(L.conv_sb.sem, 1)
                        act.wait_ge(L.normed_ps.sem, L.normed_ps.now(i))
                        act.copy(L.qkn_T[:, 0:2, :].rearrange("p n t -> p (n t)"), L.B[2][:])
                        act.copy(L.qkn_T[:, 2, :], L.B[3][:, 0:T]).then_inc(L.normed_sb.sem, 1)
                    for lv in range(len(LEVELS)):
                        for L in lanes:
                            act.wait_ge(L.t_ps.sem, L.t_ps.now(i, lv + 1))
                            act.copy(L.Tm, L.ps[:, 1024:2048]).then_inc(L.t_sb.sem, 1)
                    for L in lanes:
                        act.wait_ge(L.o_ps.sem, L.o_ps.now(i))
                        act.copy(L.outs[:, :, 2, :], tiles2(L.B[1][:, 0:T])).then_inc(L.o_sb.sem, 1)
                    for L in lanes:
                        act.wait_ge(L.o_sb.sem, L.o_sb.now(i))
                        act.activation(L.sqo.rearrange("p k n d -> p (k n d)"), L.outs[:].rearrange("p k n d -> p (k n d)"), ACT.Square).then_inc(L.squared.sem, 1)
                    for L in lanes:
                        act.wait_ge(L.xR_sb.sem, L.xR_sb.now(i))
                        act.wait_ge(L.xT_ps.sem, i + 2)
                        take_x(L)
                    take_projections(i + 2)
                    for L in lanes:
                        act.wait_ge(L.featsT_ps.sem, L.featsT_ps.now(i))
                        act.copy(L.featsT[:], L.B[0][0:NF, 0:T]).then_inc(L.featsT_sb.sem, 1)
                    for L in lanes:
                        act.wait_ge(L.h1_ps.sem, L.h1_ps.now(i))
                        for n, (a, b) in enumerate(RC):
                            ins = act.activation(L.h1[0:b - a, n, :], L.B[2 + n // 2][0:b - a, T * (n % 2):T * (n % 2) + T], ACT.Silu, bias=w["G_rb1"][0:b - a, n:n + 1])
                        ins.then_inc(L.h1_sb.sem, 1)
                    for L in lanes:
                        act.wait_ge(L.lg_shifted.sem, L.lg_shifted.now(i))
                        act.activation(L.lg[:], L.lg[:], ACT.Exp).then_inc(L.lg_exp.sem, 1)
                    take_qk(i + 2)
                    take_mid(i + 2)
                    for L in lanes:
                        act.wait_ge(L.oT_ps.sem, L.oT_ps.now(i))
                        act.copy(L.oT[:], L.B[0][:, 0:T]).then_inc(L.oT_sb.sem, 1)

            @block.vector
            def _(vec):
                c = Chain(vec, ch)

                def both(step):
                    for L in lanes:
                        m = c.mark(step(L))
                    c.need(m)

                def over(name, n):
                    return sh.c(name).unsqueeze(1).broadcast_to([P, n, P])

                def mats(ap):
                    return ap.rearrange("p (m t) -> p m t", t=P)

                vec.wait_ge(prep.sem, 1)
                for n, name in enumerate(("G_wq", "G_wk", "G_wv")):
                    vec.tensor_tensor(wtap[:, n], lanes[0].B[n].rearrange("p (a c) -> p a c", a=TAPS),
                                      w[name].unsqueeze(1).broadcast_to([P, TAPS, P]), ALU.mult)
                for tau in range(MID):
                    ins = vec.tensor_scalar(diag[:, tau, :], sh.c("ident"), w["G_mid"][:, tau:tau + 1], None, ALU.mult)
                ins.then_inc(prep_sb.sem, 1)
                def convolve(n):
                    s0 = MID - LOCAL
                    for L in lanes:
                        vec.wait_ge(L.v_sb.sem, n)
                    both(lambda L: vec.tensor_scalar(L.loc_f[:], L.v_f[:, s0:s0 + T], w["G_local"][:, 0:1], None, ALU.mult))
                    for tau in range(1, LOCAL - 1):
                        both(lambda L: vec.scalar_tensor_tensor(L.loc_f[:], L.v_f[:, s0 + tau:s0 + tau + T], w["G_local"][:, tau:tau + 1], L.loc_f[:], ALU.mult, ALU.add))
                    for L in lanes:
                        vec.scalar_tensor_tensor(L.loc_f[:], L.v_f[:, s0 + LOCAL - 1:s0 + LOCAL - 1 + T], w["G_local"][:, LOCAL - 1:LOCAL], L.loc_f[:],
                                                 ALU.mult, ALU.add).then_inc(L.loc_sb.sem, 1)

                def norms(n):
                    for L in lanes:
                        vec.wait_ge(L.qkt_sb.sem, n)
                    both(lambda L: vec.tensor_tensor(L.sq, L.qk_t[:].rearrange("p n k d -> p (n k d)"), L.qk_t[:].rearrange("p n k d -> p (n k d)"), ALU.mult))
                    both(lambda L: vec.tensor_reduce(L.ss[:], L.sq.rearrange("p (m d) -> p m d", d=HS), AX.X, ALU.add))
                    for L in lanes:
                        vec.tensor_scalar(L.ss[:], L.ss[:], 1e-12, None, ALU.add).then_inc(L.ss_ready.sem, 1)

                def normalise(n):
                    for L in lanes:
                        vec.wait_ge(L.rn_ready.sem, n)
                        vec.wait_ge(L.beta_sb.sem, n)
                    both(lambda L: vec.tensor_tensor(L.qk_t[:].rearrange("p n k (h d) -> p (n k h) d", h=NH), L.qk_t[:].rearrange("p n k (h d) -> p (n k h) d", h=NH), spread(L.rn[:], 16, HS), ALU.mult))
                    for L in lanes:
                        vec.scalar_tensor_tensor(heads(L.nkb[:]), heads(L.qk_t[:, 1]), -1.0, spread(L.beta[:].rearrange("p k h -> p (k h)"), 8, HS), ALU.mult, ALU.mult).then_inc(L.normed.sem, 1)

                for L in lanes:
                    front_vector(sh, st, vec, c, L.q, L.xhat).then_inc(L.xhat_ready.sem, 1)
                convolve(1)
                norms(1)
                normalise(1)
                with vec.Fori(0, NS // 2) as i:
                    c.restart()
                    for L in lanes:
                        vec.wait_ge(L.out_read.sem, L.out_read.last(i))
                    for L in lanes:
                        vec.wait_ge(L.v_t_sb.sem, L.v_t_sb.now(i))
                        for k in range(2):
                            ins = vec.tensor_tensor(L.vb[:, k].rearrange("p (h d) -> p h d", h=NH), L.outs[:, k, 3, :].rearrange("p (h d) -> p h d", h=NH), spread(L.beta[:, k], NH, HS), ALU.mult)
                        ins.then_inc(L.r_ready.sem, 1)
                    for k in range(2):
                        for L in lanes:
                            vec.wait_ge(L.gram.sem, L.gram.now(i, k + 1))
                            f = slice(512 * k, 512 * k + 512)
                            four = L.ps[:].rearrange("p (h c) -> p h c", h=NH)
                            vec.tensor_tensor(mats(L.A[:, f]), four[:, :, 0:P], over("before", NH), ALU.mult)
                            vec.tensor_tensor(mats(L.Um[:, f]), four[:, :, P:2 * P], over("mT1", NH), ALU.mult)
                            vec.tensor_tensor(mats(L.At[:, f]), four[:, :, 2 * P:3 * P], over("upto_f", NH), ALU.mult).then_inc(L.gram_read.sem, 1)
                    for L in lanes:
                        vec.wait_ge(L.gram_read.sem, L.gram_read.now(i))
                        vec.tensor_tensor(mats(L.Um), mats(L.Um), over("ident", 8), ALU.add).then_inc(L.first_u.sem, 1)
                    for lv, s in enumerate(LEVELS):
                        for L in lanes:
                            vec.wait_ge(L.q_ps.sem, L.q_ps.now(i, lv + 1))
                            vec.tensor_tensor(mats(L.Q), mats(L.ps[:, 0:1024]), over(f"mT{s}", 8), ALU.mult).then_inc(L.q_sb.sem, 1)
                        for L in lanes:
                            vec.wait_ge(L.u_ps.sem, L.u_ps.now(i, lv + 1))
                            if lv == 0:
                                vec.wait_ge(L.first_u.sem, L.first_u.now(i))
                            else:
                                vec.wait_ge(L.u_sb.sem, L.u_sb.now(i, lv))
                            vec.tensor_tensor(L.Um, L.ps[:, 1024:2048], L.Um, ALU.add).then_inc(L.u_sb.sem, 1)
                    for k in range(2):
                        for L in lanes:
                            vec.wait_ge(L.z_ps.sem, L.z_ps.now(i, k + 1))
                            vec.tensor_copy(L.u[:, k, :], L.B[2][:, 0:P]).then_inc(L.z_sb.sem, 1)
                        if k == 0:
                            for L in lanes:
                                vec.wait_ge(L.s_ps.sem, L.s_ps.now(i))
                                vec.tensor_tensor(L.S[:], L.B[2][:, 0:P], sh.c("same_head"), ALU.mult).then_inc(L.s_sb.sem, 1)
                            for L in lanes:
                                vec.wait_ge(L.ks_ps.sem, L.ks_ps.now(i))
                                vec.tensor_tensor(L.vb[:, 1, :], L.B[3][:, 0:P], L.vb[:, 1, :], ALU.add).then_inc(L.r_ready.sem, 1)
                    for L in lanes:
                        vec.wait_ge(L.xT_ps.sem, L.xT_ps.now(i))
                        front_vector(sh, st, vec, c, 2 * i + 2 + L.q, L.xhat).then_inc(L.xhat_ready.sem, 1)
                    for L in lanes:
                        vec.wait_ge(L.o_sb.sem, L.o_sb.now(i))
                        for k, prod in enumerate((L.prod, L.prod2)):
                            c0 = 0
                            for a in range(3):
                                n = 3 - a
                                vec.tensor_tensor(prod[:, c0:c0 + n, :], L.outs[:, k, a + 1:4, :], L.outs[:, k, a:a + 1, :].broadcast_to([P, n, P]), ALU.mult)
                                c0 += n
                            m = c.mark(vec.tensor_reduce(L.feats[:, k, 0:16], L.outs[:, k].rearrange("p n (h d) -> p (n h) d", h=NH), AX.X, ALU.add))
                    c.need(m)
                    for L in lanes:
                        vec.wait_ge(L.squared.sem, L.squared.now(i))
                        for k, prod in enumerate((L.prod, L.prod2)):
                            vec.tensor_reduce(L.feats[:, k, 16:32], L.sqo[:, k].rearrange("p n (h d) -> p (n h) d", h=NH), AX.X, ALU.add)
                            vec.tensor_reduce(L.feats[:, k, 32:56], prod.rearrange("p n (h d) -> p (n h) d", h=NH), AX.X, ALU.add)
                            m = c.mark(vec.scalar_tensor_tensor(L.mm2[:, k, :], L.feats[:, k, 0:16], 1.0 / HS, L.feats[:, k, 0:16], ALU.mult, ALU.mult))
                    c.need(m)
                    for L in lanes:
                        vec.tensor_scalar(L.feats[:, :, 0:16], L.feats[:, :, 0:16], 1.0 / HS, None, ALU.mult)
                        vec.tensor_scalar(L.feats[:, :, 32:56], L.feats[:, :, 32:56], 1.0 / HS, None, ALU.mult)
                    both(lambda L: vec.tensor_tensor(L.feats[:, :, 16:32], L.feats[:, :, 16:32], L.mm2[:], ALU.subtract))
                    for L in lanes:
                        vec.tensor_scalar(L.feats[:, :, 16:32], L.feats[:, :, 16:32], 1.0 / (HS - 1), None, ALU.mult).then_inc(L.feats_ready.sem, 1)

                    convolve(i + 2)

                    def lps(L):
                        return L.B[1][:, 0:32].rearrange("p (n j) -> p n j", j=4)

                    def lgv(L):
                        return L.lg[:].rearrange("p k h j -> p (k h) j")

                    def lmv(L):
                        return L.lm[:].rearrange("p k h -> p (k h)")

                    for L in lanes:
                        vec.wait_ge(L.lg_ps.sem, L.lg_ps.now(i))
                    both(lambda L: vec.tensor_reduce(lmv(L), lps(L), AX.X, ALU.max))
                    for L in lanes:
                        vec.tensor_tensor(lgv(L), lps(L), spread(lmv(L), 8, 4), ALU.subtract).then_inc(L.lg_shifted.sem, 1)
                    for L in lanes:
                        vec.wait_ge(L.lg_exp.sem, L.lg_exp.now(i))
                    both(lambda L: vec.tensor_reduce(lmv(L), lgv(L), AX.X, ALU.add))
                    both(lambda L: vec.reciprocal(lmv(L), lmv(L)))
                    both(lambda L: vec.tensor_tensor(lgv(L), lgv(L), spread(lmv(L), 8, 4), ALU.mult))
                    both(lambda L: vec.tensor_scalar(lgv(L), lgv(L), 1.0 - 4.0 * FLOOR, FLOOR, ALU.mult, ALU.add))
                    for k in range(2):
                        both(lambda L: vec.tensor_tensor(L.sqo[:, k].rearrange("p n (h d) -> p n h d", h=NH), L.outs[:, k].rearrange("p n (h d) -> p n h d", h=NH),
                                                         L.lg[:, k].rearrange("p h j -> p j h").unsqueeze(3).broadcast_to([P, 4, NH, HS]), ALU.mult))
                    both(lambda L: vec.tensor_reduce(L.mixed[:], L.sqo.rearrange("p k n d -> p k d n"), AX.X, ALU.add))
                    for n, weight in enumerate(("G_mix", "G_onorm")):
                        both(lambda L: vec.tensor_tensor(L.sqm[:], L.mixed[:], L.mixed[:], ALU.mult))
                        both(lambda L: vec.tensor_reduce(L.rm[:], heads(L.sqm[:]), AX.X, ALU.add))
                        for L in lanes:
                            vec.tensor_scalar(L.rm[:], L.rm[:], 1.0 / HS, EPS, ALU.mult, ALU.add).then_inc(L.ms_ready.sem, 1)
                        (norms, normalise)[n](i + 2)
                        for L in lanes:
                            vec.wait_ge(L.mr_ready.sem, L.mr_ready.now(i, n + 1))
                        both(lambda L: vec.tensor_tensor(heads(L.mixed[:]), heads(L.mixed[:]), spread(L.rr[:], 8, HS), ALU.mult))
                        for L in lanes:
                            ins = vec.tensor_tensor(L.mixed[:], L.mixed[:], w[weight].unsqueeze(1).broadcast_to([P, 2, P]), ALU.mult)
                            if n:
                                ins.then_inc(L.on_ready.sem, 1)
                            else:
                                m = c.mark(ins)
                        if n == 0:
                            c.need(m)
                    for L in lanes:
                        vec.wait_ge(L.out_ps.sem, L.out_ps.now(i))
                        residual(sh, vec, c, 2 * i + L.q, tiles2(L.B[0][:, T:2 * T]), L.out_read)


LAYERS = [latent_attention, top2_ffn_first, linear_attention_small, top2_ffn_second,
          linear_attention_large, expert_choice_ffn_first, delta_rule_mixer, expert_choice_ffn_second]



WEIGHTS = {
    "A_wdq": ("L0_attn_a_W_dq", lambda a: a),
    "A_wuqT": ("L0_attn_a_W_uq", lambda a: a.T),
    "A_wdkv": ("L0_attn_a_W_dkv", lambda a: a),
    "A_wuk": ("L0_attn_a_W_uk", lambda a: a),
    "A_wuv": ("L0_attn_a_W_uv", lambda a: a),
    "A_woT": ("L0_attn_a_W_o", lambda a: a.T),
    "B_gateT": ("L0_ffn_gate_w", lambda a: a.T),
    "B_w1T": ("L0_ffn_w1", lambda a: a.transpose(2, 0, 1).reshape(D, -1)),
    "B_w3T": ("L0_ffn_w3", lambda a: a.transpose(2, 0, 1).reshape(D, -1)),
    "B_w2T": ("L0_ffn_w2", lambda a: a.transpose(2, 0, 1).reshape(D, -1)),
    "B_b1T": ("L0_ffn_b1", lambda a: a.T),
    "B_b2T": ("L0_ffn_b2", lambda a: a.T),
    "B_b3T": ("L0_ffn_b3", lambda a: a.T),
    "B_sw1T": ("L0_ffn_sw1", lambda a: a.T),
    "B_sw2T": ("L0_ffn_sw2", lambda a: a.T),
    "B_sw3T": ("L0_ffn_sw3", lambda a: a.T.reshape(2, P, D).transpose(1, 0, 2).reshape(P, -1)),
    "C_wqT": ("L0_attn_b_Wq", lambda a: a.T),
    "C_wkT": ("L0_attn_b_Wk", lambda a: a.T),
    "C_wvT": ("L0_attn_b_Wv", lambda a: a.T),
    "C_woT": ("L0_attn_b_Wo", lambda a: a.T),
    "E_wqT": ("L1_attn_a_Wq", lambda a: a.T.reshape(16, 64, D).transpose(1, 0, 2).reshape(64, -1)),
    "E_wkT": ("L1_attn_a_Wk", lambda a: a.T.reshape(16, 64, D).transpose(1, 0, 2).reshape(64, -1)),
    "E_wv": ("L1_attn_a_Wv", lambda a: a),
    "E_wo": ("L1_attn_a_Wo", lambda a: a.reshape(8, P, D).transpose(1, 0, 2).reshape(P, -1)),
    "E_proj": ("L1_attn_a_proj", lambda a: a),
    "F_gate": ("L1_ffn_gate_w", lambda a: a),
    "F_w1": ("L1_ffn_w1", lambda a: a.transpose(1, 0, 2).reshape(D, -1)),
    "F_w2": ("L1_ffn_w2", lambda a: a.reshape(8, 4, P, D).transpose(2, 0, 1, 3).reshape(P, -1)),
    "G_wq": ("L1_attn_b_Wq", lambda a: a),
    "G_wk": ("L1_attn_b_Wk", lambda a: a),
    "G_wv": ("L1_attn_b_Wv", lambda a: a),
    "G_wb": ("L1_attn_b_Wb", lambda a: a),
    "G_conv": (("L1_attn_b_conv_q_w", "L1_attn_b_conv_k_w", "L1_attn_b_conv_v_w"), lambda *a: np.concatenate(a, 1)),
    "G_local": ("L1_attn_b_local_w", lambda a: a),
    "G_mid": ("L1_attn_b_mid_w", lambda a: a),
    "G_rw1x": ("L1_attn_b_r_w1", lambda a: a[:D]),
    "G_rw1f": ("L1_attn_b_r_w1", lambda a: np.concatenate(
        [a[D:D + 32].reshape(4, 2, 4, -1)[:, 0].reshape(16, -1), a[D:D + 32].reshape(4, 2, 4, -1)[:, 1].reshape(16, -1), a[D + 32:]])),
    "G_rb1": ("L1_attn_b_r_b1", lambda a: np.concatenate([a, a[:16]]).reshape(3, P).T),
    "G_rw2": ("L1_attn_b_r_w2", lambda a: np.concatenate([a, a[:16]]).reshape(3, P, 16).transpose(1, 0, 2).reshape(P, -1)),
    "G_rb2": ("L1_attn_b_r_b2", lambda a: a.reshape(1, -1)),
    "G_mix": ("L1_attn_b_mix_w", lambda a: np.tile(a.reshape(1, -1), (P, 1))),
    "G_onorm": ("L1_attn_b_onorm_w", lambda a: np.tile(a.reshape(1, -1), (P, 4))),
    "G_wo": ("L1_attn_b_Wo", lambda a: a),
}


def build(nc, x_in, const_in, weights_in, out):
    sh = Shared()
    sh.nc, sh.seqs = nc, x_in.shape[0]
    sh.tiles = x_in.shape[0] * T // P
    with ExitStack() as ctx:
        def sb(name, shape, dt=F32):
            return ctx.enter_context(nc.sbuf_tensor(name, shape, dt))

        sh.x = sb("x", [P, sh.tiles + PAD, D])
        sh.stats = sb("stats", [P, sh.tiles, 6])
        sh.mean, sh.rstd = sb("mean", [P, sh.tiles + PAD]), sb("rstd", [P, sh.tiles + PAD])
        sh.consts = sb("consts", list(const_in.shape))
        w = {k: sb(k, list(a.shape)) for k, a in weights_in.items() if k[0] in "FG"}
        until_large, until_ffn = ExitStack(), ExitStack()
        for group, letters in ((until_large, "E"), (until_ffn, "ABC")):
            for k, a in weights_in.items():
                if k[0] in letters:
                    w[k] = group.enter_context(nc.sbuf_tensor(k, list(a.shape), F32))

        parts = 4
        with Stage(nc, "load") as st:
            x_in_sb = [st.semaphore(f"x_part{n}", 16) for n in range(parts)]
            weights_sb = st.semaphore("weights", 16)
            xv = x_in.rearrange("s (k p) d -> p (s k) d", p=P)
            step = sh.tiles // parts
            with nc.Block() as block:
                @block.sync
                def _(sync):
                    for n in range(parts):
                        sync.dma_start(sh.x[:, n * step:(n + 1) * step, :], xv[:, n * step:(n + 1) * step, :]).then_inc(x_in_sb[n].sem, 16)

                @block.scalar
                def _(act):
                    act.dma_start(sh.consts[:], const_in).then_inc(weights_sb.sem, 16)
                    for k, a in weights_in.items():
                        act.dma_start(w[k][:], a).then_inc(weights_sb.sem, 16)
                    act.wait_ge(weights_sb.sem, 16 * (1 + len(w)))

                @block.vector
                def _(vec):
                    vec.memset(sh.x[:, sh.tiles:, :], 0.0)
                    vec.memset(sh.mean[:, sh.tiles:], 0.0)
                    vec.memset(sh.rstd[:, sh.tiles:], 0.0)
                    for n in range(parts):
                        vec.wait_ge(x_in_sb[n].sem, 16)
                        for t in range(n * step, (n + 1) * step):
                            vec.bn_stats(sh.stats[:, t, :], sh.x[:, t, :])

        w = {k: v[:] for k, v in w.items()}
        for n, layer in enumerate(LAYERS):
            finish_stats(sh, f"norm{n}")
            layer(sh, w)
            if n == 3:
                until_ffn.close()
            if n == 4:
                until_large.close()

        with Stage(nc, "store") as st:
            stored = st.semaphore("stored", 16)
            with nc.Block() as block:
                @block.sync
                def _(sync):
                    sync.dma_start(out.rearrange("s (k p) d -> p (s k) d", p=P), sh.x[:, 0:sh.tiles, :]).then_inc(stored.sem, 16)
                    sync.wait_ge(stored.sem, 16)
        if len(LAYERS) < 8:
            until_ffn.close()
            until_large.close()


def kernel(**inputs):
    import numpy as _np
    import concourse.bacc as _bacc
    from concourse import mybir as _mybir
    from concourse.bass_utils import run_bass_kernel_spmd as _run

    nc = _bacc.Bacc("TRN2", target_bir_lowering=False, num_devices=1)
    arrays = {"x_dram": _np.ascontiguousarray(inputs["L0_attn_a_x"]), "const_dram": CONSTS}
    for name, (source, layout) in WEIGHTS.items():
        arrays[f"{name}_dram"] = _np.ascontiguousarray(
            layout(*(_np.asarray(inputs[s]) for s in ((source,) if isinstance(source, str) else source))))
    aps = {k: nc.dram_tensor(k, a.shape, _mybir.dt.from_np(a.dtype), kind="ExternalInput").ap() for k, a in arrays.items()}
    out = nc.dram_tensor("out_dram", arrays["x_dram"].shape, F32, kind="ExternalOutput").ap()
    build(nc, aps["x_dram"], aps["const_dram"], {k: aps[f"{k}_dram"] for k in WEIGHTS}, out)
    r = _run(nc, [arrays], core_ids=[0])
    return r.results[0]["out_dram"]
```
